# Optimizing a Trainium2 kernel written in Bass

```python
import numpy as np
import jax
import jax.numpy as jnp

def _softmax(x, axis=-1):
    return jax.nn.softmax(x, axis=axis)

def _gelu(x):
    return jax.nn.gelu(x, approximate=True)

def _silu(x):
    return jax.nn.silu(x)

def _sigmoid(x):
    return jax.nn.sigmoid(x)

def _layernorm(x, axis=-1, eps=1e-05):
    m = jnp.mean(x, axis=axis, keepdims=True)
    v = jnp.var(x, axis=axis, keepdims=True)
    return (x - m) / jnp.sqrt(v + eps)

def _scatter_add(tgt, idx, src, axis=0):
    return tgt.at[idx].add(src)

def _segment_sum(src, seg, n):
    return jax.ops.segment_sum(src, seg, n)
kernel_name = 'mk_gnn_resnorm_d4_gnn_r8_10e350'

def setup_inputs(seed: int=0):
    np.random.seed(seed)
    _w = jnp.asarray

    def _rec_inputs():
        import jax
        import jax.numpy as jnp
        _gk = jax.random.key(seed)
        x = -0.0005121 + 1.001 * jax.random.normal(jax.random.fold_in(_gk, 1), (12500, 32), jnp.float32)
        src = jax.random.randint(jax.random.fold_in(_gk, 2), (200000,), 0, 12500, jnp.int32)
        dst = jax.random.randint(jax.random.fold_in(_gk, 3), (200000,), 0, 12500, jnp.int32)
        _o = jnp.argsort(dst, stable=True)
        src = src[_o]
        dst = dst[_o]
        edge_attr_32 = 0.000216709 + 1.00012 * jax.random.normal(jax.random.fold_in(_gk, 12), (200000, 32), jnp.float32)
        edge_attr_4 = 0.000714719 + 1.00021 * jax.random.normal(jax.random.fold_in(_gk, 13), (200000, 4), jnp.float32)
        return (x, src, dst, edge_attr_32, edge_attr_4)
    x, src, dst, edge_attr_32, edge_attr_4 = _rec_inputs()

    def _L0_gnn_setup():
        import jax, jax.numpy as jnp
        import numpy as np
        N_NODES = 12500
        EPS = 1e-12

        def _agnn_layer(x, src, dst, beta, n):
            xn = x / jnp.maximum(jnp.linalg.norm(x, axis=-1, keepdims=True), EPS)
            alpha = beta * jnp.sum(xn[src] * xn[dst], axis=-1)
            m = jax.ops.segment_max(alpha, dst, num_segments=n)
            e = jnp.exp(alpha - m[dst])
            s = jax.ops.segment_sum(e, dst, num_segments=n)
            a = e / s[dst]
            return jax.ops.segment_sum(x[src] * a[:, None], dst, num_segments=n)
        key = jax.random.key(seed)
        k1, k2 = jax.random.split(key)
        x = jax.random.normal(k1, (N_NODES, 32), dtype=jnp.float32)
        edge_index = jax.random.randint(k2, (2, 200000), 0, N_NODES, dtype=jnp.int64)
        return {'x': x, 'edge_index': edge_index, 'beta1': jnp.ones((1,), dtype=jnp.float32), 'beta2': jnp.ones((1,), dtype=jnp.float32), 'beta3': jnp.ones((1,), dtype=jnp.float32)}
    _L0_gnn_all = _L0_gnn_setup()
    _L0_gnn_in = {k: v for k, v in _L0_gnn_all.items() if k in ('beta1', 'beta2', 'beta3')}
    del _L0_gnn_all

    def _L1_gnn_setup():
        import jax, jax.numpy as jnp
        import numpy as np
        MUL = 8
        N_NODES = 12500
        N_EDGES = 100000
        EDGE_DIM = 32
        MLP_DIM = 64
        W_NUMEL = 4 * MUL * MUL
        ALPHA = 0.25
        C110 = 1.0 / np.sqrt(3.0)
        SI_SCALE = 1.0 / np.sqrt(MUL)
        key = jax.random.key(seed)
        ks = jax.random.split(key, 10)
        node_attr = jax.random.normal(ks[0], (N_NODES, 4 * MUL), dtype=jnp.float32)
        edge_index = jax.random.randint(ks[1], (2, N_EDGES), 0, N_NODES, dtype=jnp.int64)
        edge_sh = jax.random.normal(ks[2], (N_EDGES, 4), dtype=jnp.float32)
        edge_feat = jax.random.normal(ks[3], (N_EDGES, EDGE_DIM), dtype=jnp.float32)
        W1 = jax.random.normal(ks[4], (EDGE_DIM, MLP_DIM), dtype=jnp.float32) / np.sqrt(EDGE_DIM)
        b1 = jnp.zeros((MLP_DIM,), dtype=jnp.float32)
        W2 = jax.random.normal(ks[5], (MLP_DIM, W_NUMEL), dtype=jnp.float32) / np.sqrt(MLP_DIM)
        b2 = jnp.zeros((W_NUMEL,), dtype=jnp.float32)
        si_w0 = jax.random.normal(ks[6], (MUL, MUL), dtype=jnp.float32)
        si_w1 = jax.random.normal(ks[7], (MUL, MUL), dtype=jnp.float32)
        return {'node_attr': node_attr, 'edge_index': edge_index, 'edge_sh': edge_sh, 'edge_feat': edge_feat, 'W1': W1, 'b1': b1, 'W2': W2, 'b2': b2, 'si_w0': si_w0, 'si_w1': si_w1}
    _L1_gnn_all = _L1_gnn_setup()
    _L1_gnn_in = {k: v for k, v in _L1_gnn_all.items() if k in ('W1', 'b1', 'W2', 'b2', 'si_w0', 'si_w1')}
    del _L1_gnn_all

    def _L2_gnn_setup():
        import jax, jax.numpy as jnp
        import numpy as np
        N_NODES = 12500
        N_EDGES = 200000
        D = 32
        K = 3
        NEG_SLOPE = 0.2
        key = jax.random.key(seed)
        ks = jax.random.split(key, 10)
        s = 1.0 / np.sqrt(D)
        return {'u': jax.random.normal(ks[0], (N_NODES, D), jnp.float32), 'lambda_max': jnp.full((1,), 2.0, jnp.float32), 'edge_src': jax.random.randint(ks[1], (N_EDGES,), 0, N_NODES, jnp.int32), 'edge_dst': jax.random.randint(ks[2], (N_EDGES,), 0, N_NODES, jnp.int32), 'cheb_W': jax.random.normal(ks[3], (K * D, D), jnp.float32) * s, 'cheb_b': jnp.zeros((D,), jnp.float32), 'src_W': jax.random.normal(ks[4], (D, D), jnp.float32) * s, 'src_b': jnp.zeros((D,), jnp.float32), 'dst_W': jax.random.normal(ks[5], (D, D), jnp.float32) * s, 'dst_b': jnp.zeros((D,), jnp.float32), 'attn': jax.random.normal(ks[6], (1, D), jnp.float32) * s}
    _L2_gnn_all = _L2_gnn_setup()
    _L2_gnn_in = {k: v for k, v in _L2_gnn_all.items() if k in ('lambda_max', 'cheb_W', 'cheb_b', 'src_W', 'src_b', 'dst_W', 'dst_b', 'attn')}
    del _L2_gnn_all

    def _L3_gnn_setup():
        import jax, jax.numpy as jnp
        import numpy as np
        N_NODES = 12500
        N_EDGES = 200000
        D_IN, D_HID, D_OUT = (32, 64, 32)

        def sage_conv(x, edge_index, W_l, b_l, W_r, num_segments):
            src, dst = (edge_index[0], edge_index[1])
            agg = jax.ops.segment_sum(x[src], dst, num_segments=num_segments)
            return agg @ W_l.T + b_l + x @ W_r.T
        key = jax.random.key(seed)
        ks = jax.random.split(key, 8)
        x = jax.random.normal(ks[0], (N_NODES, D_IN), dtype=jnp.float32)
        edge_index = jax.random.randint(ks[1], (2, N_EDGES), 0, N_NODES, dtype=jnp.int64)
        s_in = 1.0 / np.sqrt(D_IN)
        s_hid = 1.0 / np.sqrt(D_HID)
        W_l_in = jax.random.normal(ks[2], (D_HID, D_IN), dtype=jnp.float32) * s_in
        b_l_in = jnp.zeros((D_HID,), dtype=jnp.float32)
        W_r_in = jax.random.normal(ks[3], (D_HID, D_IN), dtype=jnp.float32) * s_in
        W_l_out = jax.random.normal(ks[4], (D_OUT, D_HID), dtype=jnp.float32) * s_hid
        b_l_out = jnp.zeros((D_OUT,), dtype=jnp.float32)
        W_r_out = jax.random.normal(ks[5], (D_OUT, D_HID), dtype=jnp.float32) * s_hid
        return {'x': x, 'edge_index': edge_index, 'W_l_in': W_l_in, 'b_l_in': b_l_in, 'W_r_in': W_r_in, 'W_l_out': W_l_out, 'b_l_out': b_l_out, 'W_r_out': W_r_out}
    _L3_gnn_all = _L3_gnn_setup()
    _L3_gnn_in = {k: v for k, v in _L3_gnn_all.items() if k in ('W_l_in', 'b_l_in', 'W_r_in', 'W_l_out', 'b_l_out', 'W_r_out')}
    del _L3_gnn_all
    return {'x': x, 'src': src, 'dst': dst, 'edge_attr_32': edge_attr_32, 'edge_attr_4': edge_attr_4, 'L0_gnn_beta1': _L0_gnn_in['beta1'], 'L0_gnn_beta2': _L0_gnn_in['beta2'], 'L0_gnn_beta3': _L0_gnn_in['beta3'], 'L1_gnn_W1': _L1_gnn_in['W1'], 'L1_gnn_b1': _L1_gnn_in['b1'], 'L1_gnn_W2': _L1_gnn_in['W2'], 'L1_gnn_b2': _L1_gnn_in['b2'], 'L1_gnn_si_w0': _L1_gnn_in['si_w0'], 'L1_gnn_si_w1': _L1_gnn_in['si_w1'], 'L2_gnn_lambda_max': _L2_gnn_in['lambda_max'], 'L2_gnn_cheb_W': _L2_gnn_in['cheb_W'], 'L2_gnn_cheb_b': _L2_gnn_in['cheb_b'], 'L2_gnn_src_W': _L2_gnn_in['src_W'], 'L2_gnn_src_b': _L2_gnn_in['src_b'], 'L2_gnn_dst_W': _L2_gnn_in['dst_W'], 'L2_gnn_dst_b': _L2_gnn_in['dst_b'], 'L2_gnn_attn': _L2_gnn_in['attn'], 'L3_gnn_W_l_in': _L3_gnn_in['W_l_in'], 'L3_gnn_b_l_in': _L3_gnn_in['b_l_in'], 'L3_gnn_W_r_in': _L3_gnn_in['W_r_in'], 'L3_gnn_W_l_out': _L3_gnn_in['W_l_out'], 'L3_gnn_b_l_out': _L3_gnn_in['b_l_out'], 'L3_gnn_W_r_out': _L3_gnn_in['W_r_out']}

def reference(x, src, dst, edge_attr_32, edge_attr_4, L0_gnn_beta1, L0_gnn_beta2, L0_gnn_beta3, L1_gnn_W1, L1_gnn_b1, L1_gnn_W2, L1_gnn_b2, L1_gnn_si_w0, L1_gnn_si_w1, L2_gnn_lambda_max, L2_gnn_cheb_W, L2_gnn_cheb_b, L2_gnn_src_W, L2_gnn_src_b, L2_gnn_dst_W, L2_gnn_dst_b, L2_gnn_attn, L3_gnn_W_l_in, L3_gnn_b_l_in, L3_gnn_W_r_in, L3_gnn_W_l_out, L3_gnn_b_l_out, L3_gnn_W_r_out):
    import jax
    import jax.numpy as jnp

    def _L0_gnn_ref(x, edge_index, beta1, beta2, beta3):
        import jax, jax.numpy as jnp
        import numpy as np
        N_NODES = 12500
        EPS = 1e-12

        def _agnn_layer(x, src, dst, beta, n):
            xn = x / jnp.maximum(jnp.linalg.norm(x, axis=-1, keepdims=True), EPS)
            alpha = beta * jnp.sum(xn[src] * xn[dst], axis=-1)
            m = jax.ops.segment_max(alpha, dst, num_segments=n)
            e = jnp.exp(alpha - m[dst])
            s = jax.ops.segment_sum(e, dst, num_segments=n)
            a = e / s[dst]
            return jax.ops.segment_sum(x[src] * a[:, None], dst, num_segments=n)
        n = x.shape[0]
        loops = jnp.arange(n, dtype=edge_index.dtype)
        src = jnp.concatenate([edge_index[0], loops])
        dst = jnp.concatenate([edge_index[1], loops])
        x = _agnn_layer(x, src, dst, beta1[0], n)
        x = _agnn_layer(x, src, dst, beta2[0], n)
        x = _agnn_layer(x, src, dst, beta3[0], n)
        return x

    def _L1_gnn_ref(node_attr, edge_index, edge_sh, edge_feat, W1, b1, W2, b2, si_w0, si_w1):
        import jax, jax.numpy as jnp
        import numpy as np
        MUL = 8
        N_NODES = 12500
        N_EDGES = 100000
        EDGE_DIM = 32
        MLP_DIM = 64
        W_NUMEL = 4 * MUL * MUL
        ALPHA = 0.25
        C110 = 1.0 / np.sqrt(3.0)
        SI_SCALE = 1.0 / np.sqrt(MUL)
        n = node_attr.shape[0]
        e = edge_sh.shape[0]
        h = jax.nn.relu(edge_feat @ W1 + b1)
        w = (h @ W2 + b2).reshape(e, 4, MUL, MUL)
        w_000, w_011, w_101, w_110 = (w[:, 0], w[:, 1], w[:, 2], w[:, 3])
        s = node_attr[:, :MUL]
        v = node_attr[:, MUL:].reshape(n, MUL, 3)
        src, dst = (edge_index[0], edge_index[1])
        s_e = s[src]
        v_e = v[src]
        sh0 = edge_sh[:, 0]
        sh1 = edge_sh[:, 1:4]
        m0 = ALPHA * (jnp.einsum('ei,eio->eo', s_e * sh0[:, None], w_000) + C110 * jnp.einsum('eim,em,eio->eo', v_e, sh1, w_110))
        m1 = ALPHA * (jnp.einsum('ei,em,eio->eom', s_e, sh1, w_011) + jnp.einsum('eim,eio->eom', v_e * sh0[:, None, None], w_101))
        out0 = jax.ops.segment_sum(m0, dst, num_segments=n)
        out1 = jax.ops.segment_sum(m1.reshape(e, MUL * 3), dst, num_segments=n).reshape(n, MUL, 3)
        out0 = out0 + SI_SCALE * (s @ si_w0)
        out1 = out1 + SI_SCALE * jnp.einsum('nim,io->nom', v, si_w1)
        return jnp.concatenate([out0, out1.reshape(n, MUL * 3)], axis=-1)

    def _L2_gnn_ref(u, lambda_max, edge_src, edge_dst, cheb_W, cheb_b, src_W, src_b, dst_W, dst_b, attn):
        import jax, jax.numpy as jnp
        import numpy as np
        N_NODES = 12500
        N_EDGES = 200000
        D = 32
        K = 3
        NEG_SLOPE = 0.2
        N = u.shape[0]
        deg = jnp.zeros((N,), u.dtype).at[edge_dst].add(1.0)
        Dinv = jnp.clip(deg, 1.0, None) ** (-0.5)

        def unnL(x):
            m = (x * Dinv[:, None])[edge_src]
            agg = jax.ops.segment_sum(m, edge_dst, num_segments=N)
            return agg * Dinv[:, None]
        re_norm = 2.0 / lambda_max
        X0 = u
        Xt = [X0]
        X1 = X0
        if K > 1:
            h = unnL(X0)
            X1 = -re_norm * h + X0 * (re_norm - 1.0)
            Xt.append(X1)
        for _ in range(2, K):
            h = unnL(X1)
            Xi = -2.0 * re_norm * h + X1 * (2.0 * (re_norm - 1.0)) - X0
            Xt.append(Xi)
            X0, X1 = (X1, Xi)
        Xcat = jnp.concatenate(Xt, axis=1)
        hc = jax.nn.relu(Xcat @ cheb_W + cheb_b)
        H = attn.shape[0]
        fsrc = (hc @ src_W + src_b).reshape(N, H, -1)
        fdst = (hc @ dst_W + dst_b).reshape(N, H, -1)
        e = jax.nn.leaky_relu(fsrc[edge_src] + fdst[edge_dst], NEG_SLOPE)
        logits = jnp.einsum('ehd,hd->eh', e, attn)
        mx = jax.ops.segment_max(logits, edge_dst, num_segments=N)
        mx = jnp.where(jnp.isfinite(mx), mx, 0.0)
        ex = jnp.exp(logits - mx[edge_dst])
        den = jax.ops.segment_sum(ex, edge_dst, num_segments=N)
        a = ex / jnp.where(den > 0, den, 1.0)[edge_dst]
        msg = fsrc[edge_src] * a[:, :, None]
        out = jax.ops.segment_sum(msg, edge_dst, num_segments=N)
        return out.squeeze(1)

    def _L3_gnn_ref(x, edge_index, W_l_in, b_l_in, W_r_in, W_l_out, b_l_out, W_r_out):
        import jax, jax.numpy as jnp
        import numpy as np
        N_NODES = 12500
        N_EDGES = 200000
        D_IN, D_HID, D_OUT = (32, 64, 32)

        def sage_conv(x, edge_index, W_l, b_l, W_r, num_segments):
            src, dst = (edge_index[0], edge_index[1])
            agg = jax.ops.segment_sum(x[src], dst, num_segments=num_segments)
            return agg @ W_l.T + b_l + x @ W_r.T
        n = x.shape[0]
        h = sage_conv(x, edge_index, W_l_in, b_l_in, W_r_in, n)
        h = jax.nn.relu(h)
        out = sage_conv(h, edge_index, W_l_out, b_l_out, W_r_out, n)
        return out
    edge_index = jnp.stack([src, dst])
    x = _layernorm(x + _L0_gnn_ref(x, edge_index, L0_gnn_beta1, L0_gnn_beta2, L0_gnn_beta3), axis=-1)
    x = _layernorm(x + _L1_gnn_ref(x, edge_index, edge_attr_4, edge_attr_32, L1_gnn_W1, L1_gnn_b1, L1_gnn_W2, L1_gnn_b2, L1_gnn_si_w0, L1_gnn_si_w1), axis=-1)
    x = _layernorm(x + _L2_gnn_ref(x, L2_gnn_lambda_max, src, dst, L2_gnn_cheb_W, L2_gnn_cheb_b, L2_gnn_src_W, L2_gnn_src_b, L2_gnn_dst_W, L2_gnn_dst_b, L2_gnn_attn), axis=-1)
    x = _layernorm(x + _L3_gnn_ref(x, edge_index, L3_gnn_W_l_in, L3_gnn_b_l_in, L3_gnn_W_r_in, L3_gnn_W_l_out, L3_gnn_b_l_out, L3_gnn_W_r_out), axis=-1)
    return x

_drawn_inputs = setup_inputs


def setup_inputs(seed=0):
    import zlib

    import numpy as np

    out = dict(_drawn_inputs(seed))
    spreads = {'L1_gnn_b1': (0.0, 0.582),
     'L1_gnn_b2': (0.0, 0.3),
     'L2_gnn_cheb_b': (0.0, 0.1),
     'L2_gnn_src_b': (0.0, 0.1),
     'L2_gnn_dst_b': (0.0, 0.663),
     'L3_gnn_b_l_in': (0.0, 0.674),
     'L3_gnn_b_l_out': (0.0, 2.0)}
    factors = {}
    for name, (base, spread) in spreads.items():
        noise = np.random.default_rng([zlib.crc32(name.encode()), seed]).standard_normal(out[name].shape)
        drawn = base * np.exp(spread * noise) if base else spread * noise
        out[name] = jnp.asarray(drawn.astype(out[name].dtype))
    for name, factor in factors.items():
        out[name] = (out[name] * factor).astype(out[name].dtype)
    return out
```

```python
import concourse.bass as bass
from concourse import mybir
from contextlib import ExitStack, contextmanager
from itertools import count

F32 = mybir.dt.float32
BF16 = mybir.dt.bfloat16
I32 = mybir.dt.int32
ALU = mybir.AluOpType
ACT = mybir.ActivationFunctionType
AX = mybir.AxisListType

P = 128
N = 12500
E = 200000
D = 32
NT = (N + P - 1) // P
NP = NT * P
EP, EC = 125, E // 125
U = 16
W = D + 2
ONE, RN = D, D + 1
SPLIT = 64
MAXU = NT + E // U + 2
AW = 36
R_BASE, R_NV, R_TILE, R_NK, RW = 16, 17, 18, 19, 20
BIG = 1e30
G7, NG = 7, NT // 7
EPS_LN = 1e-5
EPS_NORM = 1e-12
MH = 64


def unique(nc, name):
    return f"{name}_{next(_names)}"


_names = count()


def sbuf(nc, name, shape, dt):
    return nc.sbuf_tensor(unique(nc, name), shape, dt)


def psum(nc, name, shape, dt):
    return nc.psum_tensor(unique(nc, name), shape, dt)


@contextmanager
def phase(nc, *names):
    with ExitStack() as stack:
        sems = [stack.enter_context(nc.semaphore(unique(nc, n))) for n in names]
        yield sems
        if sems:
            nums = sorted(s.num for s in sems)
            while nums:
                run = 1
                while run < len(nums) and nums[run] == nums[0] + run:
                    run += 1
                nc.gpsimd.dma_reset(range(nums[0], nums[0] + run))
                nc.gpsimd.sem_clear(range(nums[0], nums[0] + run))
                nums = nums[run:]
            nc.all_engine_barrier()


def over(ap, n, shape):
    return ap.unsqueeze(n).broadcast_to(shape)


def build(nc, A, out):
    ctx = ExitStack()
    with ctx:
        def sb(name, shape, dt=F32):
            return ctx.enter_context(sbuf(nc, name, shape, dt))

        def dram(name, shape, dt):
            return nc.dram_tensor(name, shape, dt, kind="Internal").ap()

        table = dram("table", (NP, W), F32)
        order = dram("order", (NP, 4), I32)
        srcw = dram("srcw", (E + U, 1), I32)
        attw = dram("attw", (E + U, AW), F32)
        recs = dram("recs", (MAXU, P, RW), I32)

        ident = sb("ident", [P, P])
        tri = sb("tri", [P, P])
        onesq = sb("onesq", [P, P])
        iota16 = sb("iota16", [P, U])
        nid = sb("nid", [P, NT], I32)
        degf = sb("degf", [P, NT])
        startf = sb("startf", [P, NT])
        kmax = sb("kmax", [P, NT])
        tcol = sb("tcol", [P, NT], I32)
        ulim = sb("ulim", [P, NT + 1], I32)
        ucnt = sb("ucnt", [P, 2], I32)
        x = sb("x", [P, NT, D])
        row = sb("row", [P, NT, W])
        agg = sb("agg", [P, NT, D + 1])
        aux = sb("aux", [P, NT, D])
        mx = sb("mx", [P, NT])
        small = sb("small", [P, 6, NT])
        g = sb("g", [P, 2, U, W])
        rec = sb("rec", [P, 2, RW], I32)
        big = sb("big", [P, NT * 96])
        negbeta = sb("negbeta", [P, 3])
        tally = ctx.enter_context(nc.semaphore("tally"))
        s_attr = ctx.enter_context(nc.semaphore("attributes_copied"))

        def make_constants():
            with phase(nc, "iota_done", "const_loaded") as (iota_done, const_loaded), \
                    sbuf(nc, "io", [P, P], I32) as io, sbuf(nc, "pc", [P, 1], I32) as pc, \
                    sbuf(nc, "iof", [P, P], F32) as iof, sbuf(nc, "pcf", [P, 1], F32) as pcf, \
                    sbuf(nc, "zero", [P, AW * U], F32) as zero, nc.Block() as block:
                @block.gpsimd
                def _(pool):
                    nc.gpsimd.iota(io[:], [[1, P]], base=0, channel_multiplier=0)
                    nc.gpsimd.iota(pc[:], [[0, 1]], base=0, channel_multiplier=1)
                    nc.gpsimd.iota(tcol[:], [[1, NT]], base=0, channel_multiplier=0)
                    pool.drain().then_inc(iota_done, 1)

                @block.vector
                def _(dve):
                    nc.vector.memset(onesq[:], 1.0)
                    nc.vector.memset(g[:], 0.0)
                    nc.vector.memset(row[:], 0.0)
                    nc.vector.memset(zero[:], 0.0)
                    dve.drain()
                    nc.vector.memset(row[:, :, ONE:ONE + 1], 1.0).then_inc(iota_done, 1)
                    dve.wait_ge(iota_done, 2)
                    nc.vector.tensor_copy(iof[:], io[:])
                    nc.vector.tensor_copy(pcf[:], pc[:])
                    dve.drain()
                    nc.vector.tensor_scalar(ident[:], iof[:], pcf[:, 0:1], None, ALU.is_equal)
                    nc.vector.tensor_scalar(tri[:], iof[:], pcf[:, 0:1], None, ALU.is_gt)
                    nc.vector.tensor_copy(iota16[:], iof[:, 0:U])
                    dve.wait_ge(const_loaded, 16 * 3)
                    nc.vector.tensor_scalar(negbeta[:], negbeta[:], -1.0, None, ALU.mult)

                @block.sync
                def _(sp):
                    sp.dma_start(negbeta[:], A["betas"].rearrange("(a b) -> a b", a=1).broadcast_to([P, 3])).then_inc(const_loaded, 16)
                    sp.wait_ge(iota_done, 2)
                    sp.dma_start(srcw[E:E + U, :].rearrange("a b -> b a"), zero[0:1, 0:U].bitcast(I32)).then_inc(const_loaded, 16)
                    sp.dma_start(attw[E:E + U, :].rearrange("(z a) b -> z (a b)", z=1), zero[0:1, 0:U * AW]).then_inc(const_loaded, 16)
                    sp.wait_ge(const_loaded, 16 * 3)

        def count_and_order():
            CH = 16
            pe_ctx = ExitStack()
            with pe_ctx:
                s = lambda n, sh, dt=F32: pe_ctx.enter_context(sbuf(nc, n, sh, dt))
                ps = lambda n, sh: pe_ctx.enter_context(psum(nc, n, sh, F32))
                dst_i = s("dst_i", [EP, EC], I32)
                part_i = s("part_i", [EP, EC], I32)
                hi = s("hi", [EP, EC], BF16)
                lo = s("lo", [EP, EC], BF16)
                iob = s("iob", [P, P], BF16)
                ioi = s("ioi", [P, P], I32)
                ohh = s("ohh", [EP, 2, CH, NT], BF16)
                ohl = s("ohl", [EP, 2, CH, P], BF16)
                zb = s("zb", [EP, P], BF16)
                hist = ps("hist", [NT, P])
                with phase(nc, "dst_loaded", "srcs_copied", "onehot", "used", "hist_zero", "iota_ready") as \
                        (dst_loaded, srcs_copied, onehot, used, hist_zero, iota_ready), nc.Block() as block:
                    @block.sync
                    def _(sp):
                        sp.dma_start(dst_i[:], A["dst"].rearrange("(p c) -> p c", c=EC)).then_inc(dst_loaded, 16)
                        sp.dma_start(srcw[0:E, :].rearrange("(p c) a -> p (c a)", p=EP), A["src"].rearrange("(p c) -> p c", c=EC)).then_inc(srcs_copied, 16)
                        sp.wait_ge(srcs_copied, 16)
                        sp.dma_start(attw[0:E, :].rearrange("(p c) b -> p (c b)", p=EP * 16), A["attr"].rearrange("(p c) b -> p (c b)", p=EP * 16)).then_inc(s_attr, 16)

                    @block.gpsimd
                    def _(pool):
                        nc.gpsimd.iota(ioi[:], [[1, P]], base=0, channel_multiplier=0).then_inc(iota_ready, 1)

                    @block.vector
                    def _(dve):
                        nc.vector.memset(zb[:], 0.0).then_inc(hist_zero, 1)
                        dve.wait_ge(iota_ready, 1)
                        nc.vector.tensor_copy(iob[:], ioi[:])
                        dve.wait_ge(dst_loaded, 16)
                        nc.vector.tensor_scalar(part_i[:], dst_i[:], 7, None, ALU.logical_shift_right)
                        dve.drain()
                        nc.vector.tensor_copy(hi[:], part_i[:])
                        dve.drain()
                        nc.vector.tensor_scalar(part_i[:], dst_i[:], P - 1, None, ALU.bitwise_and)
                        dve.drain()
                        nc.vector.tensor_copy(lo[:], part_i[:])
                        dve.drain()
                        with dve.Fori(0, EC // (2 * CH)) as it:
                            for h in range(2):
                                dve.wait_ge(used, 2 * it + h + 1)
                                dve.sem_inc(tally, 1)
                                c0 = (2 * it + h) * CH
                                nc.vector.tensor_tensor(ohh[:, h], over(iob[0:EP, 0:NT], 1, [EP, CH, NT]),
                                                        over(hi[:, bass.ds(c0, CH)], 2, [EP, CH, NT]), ALU.is_equal)
                                nc.vector.tensor_tensor(ohl[:, h], over(iob[0:EP, :], 1, [EP, CH, P]),
                                                        over(lo[:, bass.ds(c0, CH)], 2, [EP, CH, P]), ALU.is_equal)
                                dve.drain().then_inc(onehot, 1)

                    @block.tensor
                    def _(pe):
                        pe.wait_ge(hist_zero, 1)
                        nc.tensor.matmul(hist[:], zb[:, 0:NT], zb[:], start=True, stop=False)
                        pe.drain().then_inc(used, 2)
                        with pe.Fori(0, EC // (2 * CH)) as it:
                            for h in range(2):
                                pe.wait_ge(onehot, 2 * it + h + 1)
                                pe.sem_inc(tally, 1)
                                for c in range(CH):
                                    last = nc.tensor.matmul(hist[:], ohh[:, h, c], ohl[:, h, c], start=False, stop=False)
                                last.then_inc(used, 1)
                        nc.tensor.matmul(hist[:], zb[:, 0:NT], zb[:], start=False, stop=True)

                with ExitStack() as st:
                    s2 = lambda n, sh, dt=F32: st.enter_context(sbuf(nc, n, sh, dt))
                    deg = s2("deg", [NT, P])
                    first = s2("first", [NT, P])
                    z1 = s2("z1", [NT, 1])
                    cls = s2("cls", [NT, P])
                    oh = big[0:NT, 0:SPLIT * P].rearrange("p (b l) -> p b l", b=SPLIT)
                    cum = s2("cum", [NT, SPLIT, P])
                    cnt = s2("cnt", [NT, SPLIT + 1])
                    rowx = s2("rowx", [NT, SPLIT])
                    base = s2("base", [NT, SPLIT])
                    tot = s2("tot", [NT, SPLIT])
                    pos = s2("pos", [NT, P])
                    posi = s2("posi", [NT, P], I32)
                    ent = s2("ent", [NT, P, 4], I32)
                    iocl = s2("iocl", [NT, SPLIT])
                    pfx = st.enter_context(psum(nc, "pfx", [NT, SPLIT + 1], F32))
                    tots = st.enter_context(psum(nc, "tots", [NT, SPLIT], F32))
                    with phase(nc, "counted", "summed", "node_iota") as (counted, summed, node_iota), nc.Block() as block:
                        @block.gpsimd
                        def _(pool):
                            nc.gpsimd.memset(ent[:], 0).then_inc(node_iota, 1)
                            pool.wait_ge(node_iota, 1)
                            nc.gpsimd.iota(ent[:, :, 0], [[1, P]], base=0, channel_multiplier=P).then_inc(node_iota, 1)

                        @block.vector
                        def _(dve):
                            nc.vector.tensor_copy(deg[:], hist[:])
                            nc.vector.memset(z1[:], 0.0)
                            nc.vector.tensor_copy(iocl[:], ioi[0:NT, 0:SPLIT])
                            dve.drain()
                            nc.vector.tensor_tensor_scan(first[:], deg[:], z1[:].broadcast_to([NT, P]), 0.0, ALU.add, ALU.add)
                            nc.vector.tensor_reduce(cnt[:, SPLIT:SPLIT + 1], deg[:], axis=AX.X, op=ALU.add)
                            nc.vector.tensor_scalar(cls[:], deg[:], float(SPLIT - 1), -1.0, ALU.min, ALU.mult)
                            dve.drain()
                            nc.vector.tensor_scalar(cls[:], cls[:], float(SPLIT - 1), None, ALU.add)
                            dve.drain()
                            nc.vector.tensor_tensor(oh, over(iocl[:], 2, [NT, SPLIT, P]), over(cls[:], 1, [NT, SPLIT, P]), ALU.is_equal)
                            dve.drain()
                            nc.vector.tensor_reduce(cnt[:, 0:SPLIT], oh, axis=AX.X, op=ALU.add)
                            nc.vector.tensor_tensor_scan(cum[:].rearrange("p b l -> p (b l)"), big[0:NT, 0:SPLIT * P],
                                                         z1[:].broadcast_to([NT, SPLIT * P]), 0.0, ALU.add, ALU.add)
                            dve.drain().then_inc(counted, 1)
                            nc.vector.tensor_tensor_scan(rowx[:], cnt[:, 0:SPLIT], z1[:].broadcast_to([NT, SPLIT]), 0.0, ALU.add, ALU.add)
                            dve.drain()
                            nc.vector.tensor_tensor(rowx[:], rowx[:], cnt[:, 0:SPLIT], ALU.subtract)
                            dve.wait_ge(summed, 1)
                            nc.vector.tensor_copy(tot[:], tots[:])
                            nc.vector.tensor_tensor(first[:], first[:], deg[:], ALU.subtract)
                            dve.drain()
                            nc.vector.tensor_scalar(first[:], first[:], pfx[:, SPLIT:SPLIT + 1], None, ALU.add)
                            nc.vector.tensor_tensor_scan(base[:], tot[:], z1[:].broadcast_to([NT, SPLIT]), 0.0, ALU.add, ALU.add)
                            dve.drain()
                            nc.vector.tensor_tensor(base[:], base[:], tot[:], ALU.subtract)
                            dve.drain()
                            nc.vector.tensor_tensor(base[:], base[:], pfx[:, 0:SPLIT], ALU.add)
                            dve.drain()
                            nc.vector.tensor_tensor(base[:], base[:], rowx[:], ALU.subtract)
                            dve.drain()
                            nc.vector.tensor_tensor(cum[:], cum[:], over(base[:], 2, [NT, SPLIT, P]), ALU.add)
                            dve.drain()
                            nc.vector.tensor_tensor(cum[:], cum[:], oh, ALU.mult)
                            dve.drain()
                            nc.vector.tensor_reduce(pos[:], cum[:].rearrange("p b l -> p l b"), axis=AX.X, op=ALU.add)
                            dve.wait_ge(node_iota, 2)
                            nc.vector.tensor_copy(ent[:, :, 1], first[:])
                            nc.vector.tensor_copy(ent[:, :, 2], deg[:])
                            dve.drain()
                            nc.vector.tensor_scalar(posi[:], pos[:], -1.0, None, ALU.add)

                        @block.tensor
                        def _(pe):
                            pe.wait_ge(counted, 1)
                            nc.tensor.matmul(pfx[:], tri[0:NT, 0:NT], cnt[:], start=True, stop=True)
                            nc.tensor.matmul(tots[:], onesq[0:NT, 0:NT], cnt[:, 0:SPLIT], start=True, stop=True).then_inc(summed, 1)

                    C8 = 8
                    ix = s2("ix", [NT, 2, C8], I32)
                    en = s2("en", [NT, 2, C8 * 4], I32)
                    with phase(nc, "staged0", "staged1", "free0", "free1", "stored0", "stored1") as sem, nc.Block() as block:
                        staged, free, stored = sem[0:2], sem[2:4], sem[4:6]

                        @block.vector
                        def _(dve):
                            with dve.Fori(0, P // (2 * C8)) as it:
                                for h in range(2):
                                    dve.wait_ge(free[h], it + 1)
                                    dve.sem_inc(tally, 1)
                                    c0 = (2 * it + h) * C8
                                    nc.vector.tensor_copy(ix[:, h], posi[:, bass.ds(c0, C8)]).then_inc(staged[h], 1)
                                    nc.vector.tensor_copy(en[:, h], ent[:, bass.ds(c0, C8), :].rearrange("p a b -> p (a b)")).then_inc(staged[h], 1)

                        @block.gpsimd
                        def _(pool):
                            for h in range(2):
                                pool.sem_inc(free[h], 1)
                            with pool.Fori(0, P // (2 * C8)) as it:
                                for h in range(2):
                                    pool.wait_ge(staged[h], 2 * it + 2)
                                    pool.sem_inc(tally, 1)
                                    for c in range(C8):
                                        nc.gpsimd.indirect_dma_start(
                                            out=order, out_offset=bass.IndirectOffsetOnAxis(ap=ix[:, h, c:c + 1], axis=0),
                                            in_=en[:, h, 4 * c:4 * c + 4], in_offset=None).then_inc(stored[h], 16)
                                for h in range(2):
                                    pool.wait_ge(stored[h], 16 * C8 * (it + 1))
                                    pool.sem_inc(tally, 1)
                                    pool.sem_inc(free[h], 1)

        def load_order():
            with ExitStack() as st:
                s2 = lambda n, sh, dt=F32: st.enter_context(sbuf(nc, n, sh, dt))
                ordt = s2("ordt", [P, NT, 4], I32)
                kcol = s2("kcol", [NT, 1])
                diag = s2("diag", [NT, NT])
                ki = s2("ki", [P, NT], I32)
                nu = s2("nu", [P, NT])
                uf = s2("uf", [P, NT + 1])
                z1 = s2("z1b", [P, 1])
                tps = st.enter_context(psum(nc, "tps", [NT, P], F32))
                kps = st.enter_context(psum(nc, "kps", [P, NT], F32))
                with phase(nc, "order_loaded", "deg_ready", "transposed", "diag_ready", "spread") as \
                        (order_loaded, deg_ready, transposed, diag_ready, spread), nc.Block() as block:
                    @block.sync
                    def _(sp):
                        sp.dma_start(ordt[:], order.rearrange("(t p) c -> p t c", p=P)).then_inc(order_loaded, 16)

                    @block.vector
                    def _(dve):
                        dve.wait_ge(order_loaded, 16)
                        nc.vector.tensor_copy(nid[:], ordt[:, :, 0])
                        nc.vector.tensor_copy(startf[:], ordt[:, :, 1])
                        nc.vector.tensor_copy(degf[:], ordt[:, :, 2])
                        nc.vector.memset(z1[:], 0.0)
                        dve.drain().then_inc(deg_ready, 1)
                        dve.wait_ge(transposed, 1)
                        nc.vector.tensor_reduce(kcol[:], tps[:], axis=AX.X, op=ALU.max)
                        dve.drain()
                        nc.vector.tensor_scalar(diag[:], ident[0:NT, 0:NT], kcol[:, 0:1], None, ALU.mult).then_inc(diag_ready, 1)
                        dve.wait_ge(spread, 1)
                        nc.vector.tensor_copy(kmax[:], kps[:])
                        dve.drain()
                        nc.vector.tensor_scalar(ki[:], kmax[:], float(U - 1), None, ALU.add)
                        dve.drain()
                        nc.vector.tensor_scalar(ki[:], ki[:], 4, None, ALU.logical_shift_right)
                        dve.drain()
                        nc.vector.tensor_scalar(nu[:], ki[:], 1.0, None, ALU.max)
                        nc.vector.memset(uf[:, 0:1], 0.0)
                        dve.drain()
                        nc.vector.tensor_tensor_scan(uf[:, 1:NT + 1], nu[:], z1[:].broadcast_to([P, NT]), 0.0, ALU.add, ALU.add)
                        dve.drain()
                        nc.vector.tensor_copy(ulim[:], uf[:])
                        dve.drain()
                        nc.vector.tensor_copy(ucnt[:, 0:1], ulim[:, NT:NT + 1])
                        nc.vector.tensor_scalar(ki[:, 0:1], uf[:, NT:NT + 1], 1.0, None, ALU.add)
                        dve.drain()
                        nc.vector.tensor_scalar(ucnt[:, 1:2], ki[:, 0:1], 1, None, ALU.logical_shift_right)

                    @block.tensor
                    def _(pe):
                        pe.wait_ge(deg_ready, 1)
                        nc.tensor.transpose(tps[:], degf[:], ident[:]).then_inc(transposed, 1)
                        pe.wait_ge(diag_ready, 1)
                        nc.tensor.matmul(kps[:], onesq[0:NT, :], diag[:], start=True, stop=True).then_inc(spread, 1)

        def write_records():
            with sbuf(nc, "k0", [P, 1], F32) as k0, sbuf(nc, "bi", [P, 1], I32) as bi, \
                    sbuf(nc, "win", [P, U], I32) as win, sbuf(nc, "rb", [P, RW], I32) as rb, \
                    sbuf(nc, "nv", [P, 1], F32) as nv, sbuf(nc, "vd", [P, U], F32) as vd, \
                    phase(nc, "base_ready", "window", "rec_ready", "rec_stored") as (base_ready, window, rec_ready, rec_stored), \
                    nc.Block() as block:
                @block.vector
                def _(dve):
                    with dve.Fori(0, NT) as t:
                        u0 = dve.value_load(ulim[0:1, bass.ds(t, 1)], min_val=0, max_val=MAXU)
                        u1 = dve.value_load(ulim[0:1, bass.ds(t + 1, 1)], min_val=0, max_val=MAXU)
                        nc.vector.memset(k0[:], 0.0)
                        dve.drain()
                        with dve.Fori(u0, u1) as u:
                            nc.vector.tensor_scalar(bi[:], startf[:, bass.ds(t, 1)], k0[:, 0:1], float(E), ALU.add, ALU.min).then_inc(base_ready, 1)
                            nc.vector.tensor_tensor(nv[:], degf[:, bass.ds(t, 1)], k0[:], ALU.subtract)
                            dve.drain()
                            nc.vector.tensor_scalar(vd[:], iota16[:], nv[:, 0:1], None, ALU.is_lt)
                            dve.drain()
                            dve.wait_ge(window, 16 * (u + 1))
                            dve.wait_ge(rec_stored, u + 1)
                            nc.vector.tensor_tensor(rb[:, 0:U], win[:], vd[:], ALU.mult)
                            nc.vector.tensor_copy(rb[:, R_BASE:R_BASE + 1], bi[:])
                            nc.vector.tensor_copy(rb[:, R_NV:R_NV + 1].bitcast(F32), nv[:])
                            dve.drain()
                            nc.vector.tensor_copy(rb[:, R_TILE:R_TILE + 1], tcol[:, bass.ds(t, 1)])
                            nc.vector.tensor_scalar(nv[:], kmax[:, bass.ds(t, 1)], k0[:, 0:1], float(U), ALU.subtract, ALU.min)
                            dve.drain()
                            nc.vector.tensor_copy(rb[:, R_NK:R_NK + 1], nv[:])
                            nc.vector.tensor_scalar(k0[:], k0[:], float(U), None, ALU.add)
                            dve.drain().then_inc(rec_ready, 1)
                    n = dve.value_load(ucnt[0:1, 0:1], min_val=1, max_val=MAXU - 1)
                    dve.wait_ge(rec_stored, n + 1)
                    dve.sem_inc(tally, 1)
                    nc.vector.memset(rb[:], 0)
                    dve.drain().then_inc(rec_ready, 1)

                @block.gpsimd
                def _(pool):
                    n = pool.value_load(ucnt[0:1, 0:1], min_val=1, max_val=MAXU - 1)
                    with pool.Fori(0, n) as u:
                        pool.wait_ge(base_ready, u + 1)
                        pool.sem_inc(tally, 1)
                        nc.gpsimd.indirect_dma_start(out=win[:], out_offset=None, in_=srcw,
                                                     in_offset=bass.IndirectOffsetOnAxis(ap=bi[:, 0:1], axis=0)).then_inc(window, 16)

                @block.sync
                def _(sp):
                    n = sp.value_load(ucnt[0:1, 0:1], min_val=1, max_val=MAXU - 1)
                    sp.sem_inc(rec_stored, 1)
                    with phase_sem("rec_dma") as rec_dma:
                        with sp.Fori(0, n + 1) as u:
                            sp.wait_ge(rec_ready, u + 1)
                            sp.dma_start(recs[bass.ds(u, 1), :, :].rearrange("a p w -> p (a w)"), rb[:]).then_inc(rec_dma, 16)
                            sp.wait_ge(rec_dma, 16 * (u + 1))
                            sp.sem_inc(tally, 1)
                            sp.sem_inc(rec_stored, 1)

        @contextmanager
        def phase_sem(name):
            yield extra[name]

        extra = {"rec_dma": ctx.enter_context(nc.semaphore("rec_dma"))}

        def load_nodes():
            with sbuf(nc, "ixs", [P, 2, G7], I32) as ixs, sbuf(nc, "xs", [P, 2, G7, D], F32) as xs, \
                    phase(nc, "staged0", "staged1", "free0", "free1", "got0", "got1") as sem, nc.Block() as block:
                staged, free, got = sem[0:2], sem[2:4], sem[4:6]

                @block.vector
                def _(dve):
                    nc.vector.memset(xs[:], 0.0)
                    dve.drain()
                    with dve.Fori(0, NG // 2) as it:
                        for h in range(2):
                            nc.vector.tensor_copy(ixs[:, h], nid[:, bass.ds((2 * it + h) * G7, G7)])
                            dve.drain().then_inc(staged[h], 1)
                        for h in range(2):
                            dve.wait_ge(got[h], 16 * G7 * (it + 1))
                            dve.sem_inc(tally, 1)
                            nc.vector.tensor_copy(x[:, bass.ds((2 * it + h) * G7, G7), :], xs[:, h])
                            dve.drain()
                            nc.vector.memset(xs[:, h], 0.0)
                            dve.drain()

                @block.gpsimd
                def _(pool):
                    with pool.Fori(0, NG // 2) as it:
                        for h in range(2):
                            pool.wait_ge(staged[h], it + 1)
                            pool.sem_inc(tally, 1)
                            for c in range(G7):
                                nc.gpsimd.indirect_dma_start(
                                    out=xs[:, h, c], out_offset=None, in_=A["x"],
                                    in_offset=bass.IndirectOffsetOnAxis(ap=ixs[:, h, c:c + 1], axis=0),
                                    bounds_check=N - 1, oob_is_err=False).then_inc(got[h], 16)

        def scatter_rows(dest, source, width, bound=None):
            with sbuf(nc, "ixs", [P, 2, G7], I32) as ixs, sbuf(nc, "rs", [P, 2, G7, width], F32) as rs, \
                    phase(nc, "staged0", "staged1", "free0", "free1", "stored0", "stored1") as sem, nc.Block() as block:
                staged, free, stored = sem[0:2], sem[2:4], sem[4:6]

                @block.scalar
                def _(act):
                    with act.Fori(0, NG // 2) as it:
                        for h in range(2):
                            act.wait_ge(free[h], it + 1)
                            act.sem_inc(tally, 1)
                            t0 = (2 * it + h) * G7
                            nc.scalar.copy(ixs[:, h], nid[:, bass.ds(t0, G7)]).then_inc(staged[h], 1)
                            nc.scalar.copy(rs[:, h], source[:, bass.ds(t0, G7), 0:width]).then_inc(staged[h], 1)

                @block.gpsimd
                def _(pool):
                    for h in range(2):
                        pool.sem_inc(free[h], 1)
                    more = {} if bound is None else {"bounds_check": bound, "oob_is_err": False}
                    with pool.Fori(0, NG // 2) as it:
                        for h in range(2):
                            pool.wait_ge(staged[h], 2 * it + 2)
                            pool.sem_inc(tally, 1)
                            for c in range(G7):
                                nc.gpsimd.indirect_dma_start(
                                    out=dest, out_offset=bass.IndirectOffsetOnAxis(ap=ixs[:, h, c:c + 1], axis=0),
                                    in_=rs[:, h, c], in_offset=None, **more).then_inc(stored[h], 16)
                        for h in range(2):
                            pool.wait_ge(stored[h], 16 * G7 * (it + 1))
                            pool.sem_inc(tally, 1)
                            pool.sem_inc(free[h], 1)

        def load_record(sp, it, h, full, used):
            sp.wait_ge(used, it + 1)
            sp.dma_start(rec[:, h], recs[bass.ds(2 * it + h, 1), :, :].rearrange("a p w -> p (a w)")).then_inc(full, 16)

        def gather_unit(pool, it, h, full, got):
            pool.wait_ge(full, 16 * (it + 1))
            pool.sem_inc(tally, 1)
            nk = pool.value_load(rec[0:1, h, R_NK:R_NK + 1], min_val=0, max_val=U)
            for c in range(U):
                with pool.If(nk > c):
                    nc.gpsimd.indirect_dma_start(out=g[:, h, c], out_offset=None, in_=table,
                                                 in_offset=bass.IndirectOffsetOnAxis(ap=rec[:, h, c:c + 1], axis=0)).then_inc(got, 16)

        def wait_rows(eng, h, it, full, got, total):
            eng.wait_ge(full, 16 * (it + 1))
            eng.sem_inc(tally, 1)
            t = eng.value_load(rec[0:1, h, R_TILE:R_TILE + 1], min_val=0, max_val=NT - 1)
            nk = eng.value_load(rec[0:1, h, R_NK:R_NK + 1], min_val=0, max_val=U)
            eng.reg_add(total[h], total[h], nk)
            eng.wait_ge(got, eng.snap(total[h]) * 16)
            eng.sem_inc(tally, 1)
            return t

        def pairs(eng):
            return eng.value_load(ucnt[0:1, 1:2], min_val=1, max_val=MAXU // 2)

        def sum_rows(dve, values, keep, t, h, valid, wp, red, cols):
            nc.vector.tensor_tensor(wp[:, h, :, 0:cols], values[:, :, 0:cols], over(keep, 2, [P, U, cols]), ALU.mult)
            dve.drain()
            nc.vector.tensor_reduce(red[:, h, 0:cols], wp[:, h, :, 0:cols].rearrange("p c f -> p f c"), axis=AX.X, op=ALU.add)
            dve.drain()

        def gather_sum():
            with sbuf(nc, "valid", [P, 2, U], F32) as valid, sbuf(nc, "wp", [P, 2, U, D + 1], F32) as wp, \
                    sbuf(nc, "red", [P, 2, D + 1], F32) as red, \
                    phase(nc, "full0", "full1", "used0", "used1", "got0", "got1") as sem, nc.Block() as block:
                full, used, got = sem[0:2], sem[2:4], sem[4:6]

                @block.sync
                def _(sp):
                    with sp.Fori(0, pairs(sp)) as it:
                        for h in range(2):
                            load_record(sp, it, h, full[h], used[h])

                @block.gpsimd
                def _(pool):
                    with pool.Fori(0, pairs(pool)) as it:
                        for h in range(2):
                            gather_unit(pool, it, h, full[h], got[h])

                @block.vector
                def _(dve):
                    nc.vector.memset(agg[:], 0.0)
                    dve.drain()
                    total = [dve.alloc_register(unique(nc, f"rows{h}")) for h in range(2)]
                    for h in range(2):
                        dve.reg_mov(total[h], 0)
                        dve.sem_inc(used[h], 1)
                    with dve.Fori(0, pairs(dve)) as it:
                        for h in range(2):
                            t = wait_rows(dve, h, it, full[h], got[h], total)
                            nc.vector.tensor_scalar(valid[:, h], iota16[:], rec[:, h, R_NV:R_NV + 1].bitcast(F32), None, ALU.is_lt)
                            dve.drain()
                            sum_rows(dve, g[:, h], valid[:, h], t, h, valid, wp, red, D)
                            own = agg[:, bass.ds(t, 1), 0:D].rearrange("p a f -> p (a f)")
                            nc.vector.tensor_tensor(own, own, red[:, h, 0:D], ALU.add)
                            dve.drain().then_inc(used[h], 1)
                    for h in range(2):
                        dve.free_register(total[h])

        def gather_attend(logits):
            with sbuf(nc, "valid", [P, 2, U], F32) as valid, sbuf(nc, "wp", [P, 2, U, D + 1], F32) as wp, \
                    sbuf(nc, "red", [P, 2, D + 1], F32) as red, sbuf(nc, "lg", [P, 2, U], F32) as lg, \
                    sbuf(nc, "pr", [P, 2, U], F32) as pr, sbuf(nc, "st", [P, 2, 4], F32) as st, \
                    phase(nc, "full0", "full1", "used0", "used1", "got0", "got1", "logits", "exps") as sem, nc.Block() as block:
                full, used, got, logits_ready, exps_ready = sem[0:2], sem[2:4], sem[4:6], sem[6], sem[7]

                @block.sync
                def _(sp):
                    with sp.Fori(0, pairs(sp)) as it:
                        for h in range(2):
                            load_record(sp, it, h, full[h], used[h])

                @block.gpsimd
                def _(pool):
                    with pool.Fori(0, pairs(pool)) as it:
                        for h in range(2):
                            gather_unit(pool, it, h, full[h], got[h])

                @block.scalar
                def _(act):
                    with act.Fori(0, pairs(act)) as it:
                        for h in range(2):
                            act.wait_ge(logits_ready, 2 * it + h + 1)
                            act.sem_inc(tally, 1)
                            nc.scalar.activation(pr[:, h], lg[:, h], ACT.Exp, bias=st[:, h, 1:2], scale=-1.0)
                            nc.scalar.activation(st[:, h, 2:3], st[:, h, 0:1], ACT.Exp, bias=st[:, h, 1:2], scale=-1.0)
                            act.drain().then_inc(exps_ready, 1)

                @block.vector
                def _(dve):
                    total = [dve.alloc_register(unique(nc, f"rows{h}")) for h in range(2)]
                    for h in range(2):
                        dve.reg_mov(total[h], 0)
                        dve.sem_inc(used[h], 1)
                    with dve.Fori(0, pairs(dve)) as it:
                        for h in range(2):
                            t = wait_rows(dve, h, it, full[h], got[h], total)
                            nc.vector.tensor_scalar(valid[:, h], iota16[:], rec[:, h, R_NV:R_NV + 1].bitcast(F32), None, ALU.is_lt)
                            mine = aux[:, bass.ds(t, 1), :].rearrange("p a f -> p (a f)")
                            logits(dve, h, over(mine, 1, [P, U, D]), wp[:, h], lg[:, h], valid[:, h])
                            dve.drain()
                            m_t = mx[:, bass.ds(t, 1)]
                            nc.vector.tensor_reduce(st[:, h, 3:4], lg[:, h], axis=AX.X, op=ALU.min)
                            nc.vector.tensor_copy(st[:, h, 0:1], m_t)
                            dve.drain()
                            nc.vector.tensor_tensor(st[:, h, 1:2], st[:, h, 3:4], st[:, h, 0:1], ALU.min)
                            dve.drain().then_inc(logits_ready, 1)
                            dve.wait_ge(exps_ready, 2 * it + h + 1)
                            dve.sem_inc(tally, 1)
                            nc.vector.tensor_copy(m_t, st[:, h, 1:2])
                            sum_rows(dve, g[:, h], pr[:, h], t, h, valid, wp, red, D + 1)
                            own = agg[:, bass.ds(t, 1), :].rearrange("p a f -> p (a f)")
                            nc.vector.scalar_tensor_tensor(own, own, st[:, h, 2:3], red[:, h, :], ALU.mult, ALU.add)
                            dve.drain().then_inc(used[h], 1)
                    for h in range(2):
                        dve.free_register(total[h])

        def masked(dve, lg, valid, scale):
            nc.vector.tensor_scalar(valid, valid, -BIG, BIG, ALU.mult, ALU.add)
            dve.drain()
            nc.vector.scalar_tensor_tensor(lg, lg, scale, valid, ALU.mult, ALU.add)

        def node_product(source, kin, weight, m, finish):
            with sbuf(nc, "stage", [P, G7, kin], F32) as stage, sbuf(nc, "xt", [kin, G7 * P], F32) as xt, \
                    psum(nc, "tp", [kin, 2, 4 * P], F32) as tp, psum(nc, "po", [P, 512], F32) as po, \
                    phase(nc, "staged", "transposed", "copied", "product", "finished") as \
                    (staged, transposed, copied, product, finished), nc.Block() as block:
                tpf = tp[:].rearrange("k a b -> k (a b)")

                @block.scalar
                def _(act):
                    with act.Fori(0, NG) as i:
                        act.wait_ge(finished, i + 1)
                        act.sem_inc(tally, 1)
                        nc.scalar.copy(stage[:], source[:, bass.ds(i * G7, G7), :]).then_inc(staged, 1)
                        act.wait_ge(transposed, i + 1)
                        act.sem_inc(tally, 1)
                        nc.scalar.copy(xt[:, 0:4 * P], tpf[:, 0:4 * P])
                        nc.scalar.copy(xt[:, 4 * P:G7 * P], tpf[:, 4 * P:G7 * P])
                        act.drain().then_inc(copied, 1)

                @block.tensor
                def _(pe):
                    with pe.Fori(0, NG) as i:
                        pe.wait_ge(staged, i + 1)
                        pe.sem_inc(tally, 1)
                        for c in range(G7):
                            last = nc.tensor.transpose(tpf[:, c * P:(c + 1) * P], stage[:, c], ident[:])
                        last.then_inc(transposed, 1)
                        pe.wait_ge(copied, i + 1)
                        pe.sem_inc(tally, 1)
                        for c in range(G7):
                            last = nc.tensor.matmul(po[:, c * m:(c + 1) * m], xt[:, c * P:(c + 1) * P], weight, start=True, stop=True)
                        last.then_inc(product, 1)

                @block.vector
                def _(dve):
                    dve.sem_inc(finished, 1)
                    with dve.Fori(0, NG) as i:
                        dve.wait_ge(product, i + 1)
                        dve.sem_inc(tally, 1)
                        finish(dve, bass.ds(i * G7, G7), po[:, 0:G7 * m].rearrange("p (c m) -> p c m", c=G7))
                        dve.drain().then_inc(finished, 1)

        def with_sqrt(before, after, name="root"):
            with phase(nc, "squares", "roots") as (squares, roots), nc.Block() as block:
                @block.vector
                def _(dve):
                    before(dve)
                    dve.drain().then_inc(squares, 1)
                    dve.wait_ge(roots, 1)
                    after(dve)

                @block.scalar
                def _(act):
                    act.wait_ge(squares, 1)
                    nc.scalar.activation(small[:, 1], small[:, 0], ACT.Sqrt).then_inc(roots, 1)

        scratch = big[:, 0:NT * D].rearrange("p (t f) -> p t f", f=D)
        scratch2 = big[:, NT * D:NT * 2 * D].rearrange("p (t f) -> p t f", f=D)

        def node_norms(source):
            def before(dve):
                nc.vector.tensor_tensor(scratch, source, source, ALU.mult)
                nc.vector.tensor_copy(row[:, :, 0:D], source)
                dve.drain()
                nc.vector.tensor_reduce(small[:, 0], scratch, axis=AX.X, op=ALU.add)
                dve.drain()
                nc.vector.tensor_scalar(small[:, 0], small[:, 0], EPS_NORM ** 2 / 100, None, ALU.max)

            def after(dve):
                nc.vector.tensor_scalar(small[:, 2], small[:, 1], EPS_NORM, None, ALU.max)
                dve.drain()
                nc.vector.reciprocal(small[:, 3], small[:, 2])
                dve.drain()
                nc.vector.tensor_copy(row[:, :, RN], small[:, 3])
                nc.vector.tensor_tensor(aux[:], source, over(small[:, 3], 2, [P, NT, D]), ALU.mult)
            with_sqrt(before, after)

        def layer_norm(prepare):
            def before(dve):
                prepare(dve)
                dve.drain()
                nc.vector.tensor_reduce(small[:, 2], scratch, axis=AX.X, op=ALU.add)
                dve.drain()
                nc.vector.tensor_scalar(small[:, 2], small[:, 2], 1.0 / D, None, ALU.mult)
                dve.drain()
                nc.vector.tensor_tensor(x[:], scratch, over(small[:, 2], 2, [P, NT, D]), ALU.subtract)
                dve.drain()
                nc.vector.tensor_tensor(scratch, x[:], x[:], ALU.mult)
                dve.drain()
                nc.vector.tensor_reduce(small[:, 3], scratch, axis=AX.X, op=ALU.add)
                dve.drain()
                nc.vector.tensor_scalar(small[:, 0], small[:, 3], 1.0 / D, EPS_LN, ALU.mult, ALU.add)

            def after(dve):
                nc.vector.reciprocal(small[:, 2], small[:, 1])
                dve.drain()
                nc.vector.tensor_tensor(x[:], x[:], over(small[:, 2], 2, [P, NT, D]), ALU.mult)
            with_sqrt(before, after)

        def on_vector(work):
            with nc.Block() as block:
                @block.vector
                def _(dve):
                    work(dve)

        make_constants()
        count_and_order()
        load_order()
        write_records()
        load_nodes()

        own = row[:, :, 0:D]
        on_vector(lambda dve: nc.vector.tensor_copy(row[:, :, 0:D], x[:]))
        with nc.Fori(0, 3) as r:
            beta = sb_beta = small[:, 5, 0:1]

            def square(dve):
                nc.vector.tensor_copy(beta, negbeta[:, bass.ds(r, 1)])
                nc.vector.tensor_tensor(scratch, own, own, ALU.mult)
                dve.drain()
                nc.vector.tensor_reduce(small[:, 0], scratch, axis=AX.X, op=ALU.add)
                dve.drain()
                nc.vector.tensor_scalar(small[:, 0], small[:, 0], EPS_NORM ** 2 / 100, None, ALU.max)

            def start_with_self(dve):
                nc.vector.tensor_scalar(small[:, 2], small[:, 1], EPS_NORM, None, ALU.max)
                dve.drain()
                nc.vector.reciprocal(small[:, 3], small[:, 2])
                dve.drain()
                nc.vector.tensor_copy(row[:, :, RN], small[:, 3])
                nc.vector.tensor_tensor(aux[:], own, over(small[:, 3], 2, [P, NT, D]), ALU.mult)
                dve.drain()
                nc.vector.tensor_tensor(scratch, aux[:], aux[:], ALU.mult)
                nc.vector.tensor_copy(agg[:], row[:, :, 0:D + 1])
                dve.drain()
                nc.vector.tensor_reduce(mx[:], scratch, axis=AX.X, op=ALU.add)
                dve.drain()
                nc.vector.tensor_scalar(mx[:], mx[:], beta, None, ALU.mult)
            with_sqrt(square, start_with_self)

            def cosine(dve, h, mine, wp, lg, valid):
                nc.vector.tensor_tensor(wp[:, :, 0:D], g[:, h, :, 0:D], mine, ALU.mult)
                dve.drain()
                nc.vector.tensor_reduce(lg, wp[:, :, 0:D], axis=AX.X, op=ALU.add)
                dve.drain()
                nc.vector.tensor_tensor(lg, lg, g[:, h, :, RN], ALU.mult)
                masked(dve, lg, valid, beta)

            scatter_rows(table, row, W)
            gather_attend(cosine)

            def divide(dve):
                nc.vector.reciprocal(small[:, 2], agg[:, :, D])
                dve.drain()
                nc.vector.tensor_tensor(row[:, :, 0:D], agg[:, :, 0:D], over(small[:, 2], 2, [P, NT, D]), ALU.mult)
            on_vector(divide)
        layer_norm(lambda dve: nc.vector.tensor_tensor(scratch, x[:], row[:, :, 0:D], ALU.add))

        on_vector(lambda dve: nc.vector.tensor_copy(row[:, :, 0:D], x[:]))
        scatter_rows(table, row, W)
        lin = big[:, 2 * NT * D:3 * NT * D].rearrange("p (t f) -> p t f", f=D)
        with ExitStack() as st:
            s2 = lambda n, sh, dt=F32: st.enter_context(sbuf(nc, n, sh, dt))
            selfw = s2("selfw", [D, D])
            w1 = s2("w1", [D, MH])
            w2 = s2("w2", [MH + 1, 4, 64])
            b1 = s2("b1", [MH, 1])
            ht = s2("ht", [MH + 1, 2, 512])
            with phase(nc, "zeroed", "weights_loaded") as (zeroed, weights_loaded), nc.Block() as block:
                @block.vector
                def _(dve):
                    nc.vector.memset(selfw[:], 0.0)
                    nc.vector.memset(ht[MH:MH + 1], 1.0)
                    dve.drain().then_inc(zeroed, 1)

                @block.sync
                def _(sp):
                    sp.wait_ge(zeroed, 1)
                    sp.dma_start(selfw[0:8, 0:8], A["si_w0"]).then_inc(weights_loaded, 16)
                    for m in range(3):
                        for i in range(8):
                            sp.dma_start(selfw[8 + 3 * i + m:9 + 3 * i + m, 8 + 8 * m:16 + 8 * m], A["si_w1"][i:i + 1, :]).then_inc(weights_loaded, 16)
                    sp.dma_start(w1[:], A["W1"]).then_inc(weights_loaded, 16)
                    sp.dma_start(b1[:], A["b1"].rearrange("(a b) -> a b", b=1)).then_inc(weights_loaded, 16)
                    w2_in = A["W2"].rearrange("h (k c) -> h k c", k=4)
                    b2_in = A["b2"].rearrange("(z k c) -> z k c", z=1, k=4)
                    for k, of in enumerate((0, 3, 1, 2)):
                        sp.dma_start(w2[0:MH, k], w2_in[:, of]).then_inc(weights_loaded, 16)
                        sp.dma_start(w2[MH:MH + 1, k], b2_in[:, of]).then_inc(weights_loaded, 16)
                    sp.wait_ge(weights_loaded, 16 * (1 + 24 + 2 + 8))
                    sp.wait_ge(s_attr, 16)

            node_product(x, D, selfw[:], D, lambda dve, tiles, prod: nc.vector.tensor_copy(lin[:, tiles, :], prod))
            edge_messages(nc, locals())
        def messages_in(dve):
            a4 = agg[:, :, 0:D]
            nc.vector.tensor_scalar(scratch2, lin, 1.0 / 8 ** 0.5, None, ALU.mult)
            dve.drain()
            nc.vector.scalar_tensor_tensor(scratch2, a4, 0.25, scratch2, ALU.mult, ALU.add)
            dve.drain()
            nc.vector.tensor_tensor(scratch[:, :, 0:8], x[:, :, 0:8], scratch2[:, :, 0:8], ALU.add)
            for m in range(3):
                nc.vector.tensor_tensor(scratch[:, :, 8 + m:D:3], x[:, :, 8 + m:D:3], scratch2[:, :, 8 + 8 * m:16 + 8 * m], ALU.add)
        layer_norm(messages_in)

        dinv, lam = small[:, 4], small[:, 5, 0:4]
        cat = big[:].rearrange("p (t f) -> p t f", f=3 * D)
        with ExitStack() as st:
            s2 = lambda n, sh, dt=F32: st.enter_context(sbuf(nc, n, sh, dt))
            cw = s2("cw", [3 * D, D])
            cb = s2("cb", [P, D])
            fw = s2("fw", [D, 2 * D])
            fb = s2("fb", [P, 2 * D])
            att = s2("att", [P, D])
            hc = s2("hc", [P, NT, D])
            with phase(nc, "weights_loaded") as (weights_loaded,), nc.Block() as block:
                @block.sync
                def _(sp):
                    spread = lambda a, n: a.rearrange("(a b) -> a b", a=1).broadcast_to([P, n])
                    sp.dma_start(cw[:], A["cheb_W"]).then_inc(weights_loaded, 16)
                    sp.dma_start(cb[:], spread(A["cheb_b"], D)).then_inc(weights_loaded, 16)
                    sp.dma_start(fw[:, 0:D], A["src_W"]).then_inc(weights_loaded, 16)
                    sp.dma_start(fw[:, D:2 * D], A["dst_W"]).then_inc(weights_loaded, 16)
                    sp.dma_start(fb[:, 0:D], spread(A["src_b"], D)).then_inc(weights_loaded, 16)
                    sp.dma_start(fb[:, D:2 * D], spread(A["dst_b"], D)).then_inc(weights_loaded, 16)
                    sp.dma_start(att[:], A["attn"].broadcast_to([P, D])).then_inc(weights_loaded, 16)
                    sp.dma_start(lam[:, 0:1], spread(A["lambda_max"], 1)).then_inc(weights_loaded, 16)
                    sp.wait_ge(weights_loaded, 16 * 8)

            def degrees(dve):
                nc.vector.tensor_scalar(small[:, 0], degf[:], 1.0, None, ALU.max)
                nc.vector.reciprocal(lam[:, 1:2], lam[:, 0:1])
                dve.drain()
                nc.vector.tensor_scalar(lam[:, 1:2], lam[:, 1:2], 2.0, None, ALU.mult)
                dve.drain()
                nc.vector.tensor_scalar(lam[:, 2:3], lam[:, 1:2], -1.0, None, ALU.add)
                nc.vector.tensor_scalar(lam[:, 3:4], lam[:, 1:2], -1.0, None, ALU.mult)

            def scaled(dve):
                nc.vector.reciprocal(dinv, small[:, 1])
                dve.drain()
                nc.vector.tensor_tensor(row[:, :, 0:D], x[:], over(dinv, 2, [P, NT, D]), ALU.mult)
                nc.vector.tensor_copy(cat[:, :, 0:D], x[:])
            with_sqrt(degrees, scaled)
            scatter_rows(table, row, W)
            gather_sum()

            def first_term(dve):
                c1 = cat[:, :, D:2 * D]
                nc.vector.tensor_tensor(c1, agg[:, :, 0:D], over(dinv, 2, [P, NT, D]), ALU.mult)
                nc.vector.tensor_scalar(hc[:], x[:], lam[:, 2:3], None, ALU.mult)
                dve.drain()
                nc.vector.scalar_tensor_tensor(c1, c1, lam[:, 3:4], hc[:], ALU.mult, ALU.add)
                dve.drain()
                nc.vector.tensor_tensor(row[:, :, 0:D], c1, over(dinv, 2, [P, NT, D]), ALU.mult)
            on_vector(first_term)
            scatter_rows(table, row, W)
            gather_sum()

            def second_term(dve):
                c2 = cat[:, :, 2 * D:3 * D]
                nc.vector.tensor_tensor(c2, agg[:, :, 0:D], over(dinv, 2, [P, NT, D]), ALU.mult)
                nc.vector.tensor_scalar(hc[:], cat[:, :, D:2 * D], lam[:, 2:3], None, ALU.mult)
                dve.drain()
                nc.vector.scalar_tensor_tensor(c2, c2, lam[:, 3:4], hc[:], ALU.mult, ALU.add)
                dve.drain()
                nc.vector.scalar_tensor_tensor(c2, c2, 2.0, x[:], ALU.mult, ALU.subtract)
            on_vector(second_term)

            def relu_bias(dve, tiles, prod):
                nc.vector.tensor_tensor(hc[:, tiles, :], prod, over(cb[:], 1, [P, G7, D]), ALU.add)
                dve.drain()
                nc.vector.tensor_scalar(hc[:, tiles, :], hc[:, tiles, :], 0.0, None, ALU.max)
            node_product(cat, 3 * D, cw[:], D, relu_bias)

            def both(dve, tiles, prod):
                nc.vector.tensor_tensor(row[:, tiles, 0:D], prod[:, :, 0:D], over(fb[:, 0:D], 1, [P, G7, D]), ALU.add)
                nc.vector.tensor_tensor(aux[:, tiles, :], prod[:, :, D:2 * D], over(fb[:, D:2 * D], 1, [P, G7, D]), ALU.add)
            node_product(hc, D, fw[:], 2 * D, both)
            scatter_rows(table, row, W)

            def empty_state(dve):
                nc.vector.memset(agg[:], 0.0)
                nc.vector.memset(mx[:], BIG / 10)
            on_vector(empty_state)

            def additive(dve, h, mine, wp, lg, valid):
                e = wp[:, :, 0:D]
                nc.vector.tensor_tensor(e, g[:, h, :, 0:D], mine, ALU.add)
                dve.drain()
                nc.vector.scalar_tensor_tensor(e, e, 0.2, e, ALU.mult, ALU.max)
                dve.drain()
                nc.vector.tensor_tensor(e, e, over(att[:], 1, [P, U, D]), ALU.mult)
                dve.drain()
                nc.vector.tensor_reduce(lg, e, axis=AX.X, op=ALU.add)
                dve.drain()
                masked(dve, lg, valid, -1.0)
            gather_attend(additive)

            def attended(dve):
                nc.vector.tensor_scalar(small[:, 2], agg[:, :, D], 0.0, None, ALU.is_equal)
                dve.drain()
                nc.vector.tensor_tensor(small[:, 2], small[:, 2], agg[:, :, D], ALU.add)
                dve.drain()
                nc.vector.reciprocal(small[:, 3], small[:, 2])
                dve.drain()
                nc.vector.tensor_tensor(scratch, agg[:, :, 0:D], over(small[:, 3], 2, [P, NT, D]), ALU.mult)
                dve.drain()
                nc.vector.tensor_tensor(scratch, scratch, x[:], ALU.add)
            layer_norm(attended)

        with ExitStack() as st:
            s2 = lambda n, sh, dt=F32: st.enter_context(sbuf(nc, n, sh, dt))
            win_ = s2("w_in", [2 * D, MH])
            bin_ = s2("b_in", [P, MH])
            wout = s2("w_out", [MH, 2 * D])
            bout = s2("b_out", [P, D])
            hid = s2("hid", [P, NT, MH])
            with phase(nc, "weights_loaded") as (weights_loaded,), nc.Block() as block:
                @block.sync
                def _(sp):
                    spread = lambda a, n: a.rearrange("(a b) -> a b", a=1).broadcast_to([P, n])
                    sp.dma_start(win_[0:D, :], A["W_l_in_T"]).then_inc(weights_loaded, 16)
                    sp.dma_start(win_[D:2 * D, :], A["W_r_in_T"]).then_inc(weights_loaded, 16)
                    sp.dma_start(bin_[:], spread(A["b_l_in"], MH)).then_inc(weights_loaded, 16)
                    sp.dma_start(wout[:, 0:D], A["W_l_out_T"]).then_inc(weights_loaded, 16)
                    sp.dma_start(wout[:, D:2 * D], A["W_r_out_T"]).then_inc(weights_loaded, 16)
                    sp.dma_start(bout[:], spread(A["b_l_out"], D)).then_inc(weights_loaded, 16)
                    sp.wait_ge(weights_loaded, 16 * 6)
            on_vector(lambda dve: nc.vector.tensor_copy(row[:, :, 0:D], x[:]))
            scatter_rows(table, row, W)
            gather_sum()
            ax = big[:, 0:NT * 2 * D].rearrange("p (t f) -> p t f", f=2 * D)

            def beside(dve):
                nc.vector.tensor_copy(ax[:, :, 0:D], agg[:, :, 0:D])
                nc.vector.tensor_copy(ax[:, :, D:2 * D], x[:])
            on_vector(beside)

            def relu_in(dve, tiles, prod):
                nc.vector.tensor_tensor(hid[:, tiles, :], prod, over(bin_[:], 1, [P, G7, MH]), ALU.add)
                dve.drain()
                nc.vector.tensor_scalar(hid[:, tiles, :], hid[:, tiles, :], 0.0, None, ALU.max)
            node_product(ax, 2 * D, win_[:], MH, relu_in)

            def outs(dve, tiles, prod):
                nc.vector.tensor_copy(row[:, tiles, 0:D], prod[:, :, 0:D])
                nc.vector.tensor_tensor(aux[:, tiles, :], prod[:, :, D:2 * D], over(bout[:], 1, [P, G7, D]), ALU.add)
            node_product(hid, MH, wout[:], 2 * D, outs)
            scatter_rows(table, row, W)
            gather_sum()

            def last_sum(dve):
                nc.vector.tensor_tensor(scratch, agg[:, :, 0:D], aux[:], ALU.add)
                dve.drain()
                nc.vector.tensor_tensor(scratch, scratch, x[:], ALU.add)
            layer_norm(last_sum)
        scatter_rows(out, x, D, bound=N - 1)


def edge_messages(nc, v):
    tally = v["tally"]
    """Layer 1's edges: agg[q, o] = the sum over a node's edges of z[q, i] times w[i, o]."""
    P_ = P
    g, rec, agg, iota16, attw, ident = v["g"], v["rec"], v["agg"], v["iota16"], v["attw"], v["ident"]
    w1, w2, b1, ht = v["w1"], v["w2"], v["b1"], v["ht"]
    S4 = U // 4
    with ExitStack() as st:
        s2 = lambda n, sh, dt=F32: st.enter_context(sbuf(nc, n, sh, dt))
        ea = s2("ea", [P, 2, U, AW])
        valid = s2("valid1", [P, U])
        gz = s2("gz", [P, U, D])
        z = s2("z", [P, 2, 4, U, 2, 8])
        vs = s2("vs", [P, U, 8, 3])
        bs = s2("bs", [P, U, 8])
        et = s2("et", [D, 512])
        prod = s2("prod", [P, 4, 64, 8])
        red = s2("red1", [P, D])
        etp = st.enter_context(psum(nc, "etp", [D, 512], F32))
        hps = st.enter_context(psum(nc, "hps", [MH, 512], F32))
        wps = st.enter_context(psum(nc, "wps", [P, 2, 4, 256], F32))
        names = ("full0", "full1", "used0", "used1", "got0", "got1", "attr0", "attr1",
                 "turned", "turned_copied", "hidden", "hidden_relu", "weights", "weights_used")
        with phase(nc, *names) as sem, nc.Block() as block:
            full, used, got, attr = sem[0:2], sem[2:4], sem[4:6], sem[6:8]
            turned, turned_copied, hidden, hidden_relu, weights, weights_used = sem[8:]

            @block.sync
            def _(sp):
                with sp.Fori(0, v["pairs"](sp)) as it:
                    for h in range(2):
                        v["load_record"](sp, it, h, full[h], used[h])

            @block.gpsimd
            def _(pool):
                with pool.Fori(0, v["pairs"](pool)) as it:
                    for h in range(2):
                        pool.wait_ge(full[h], 16 * (it + 1))
                        pool.sem_inc(tally, 1)
                        nc.gpsimd.indirect_dma_start(out=ea[:, h].rearrange("p a b -> p (a b)"), out_offset=None, in_=attw,
                                                     in_offset=bass.IndirectOffsetOnAxis(ap=rec[:, h, R_BASE:R_BASE + 1], axis=0)).then_inc(attr[h], 16)
                        v["gather_unit"](pool, it, h, full[h], got[h])

            @block.tensor
            def _(pe):
                with pe.Fori(0, v["pairs"](pe)) as it:
                    for h in range(2):
                        pe.wait_ge(attr[h], 16 * (it + 1))
                        pe.sem_inc(tally, 1)
                        nk = pe.value_load(rec[0:1, h, R_NK:R_NK + 1], min_val=0, max_val=U)
                        for s in range(S4):
                            n = it * 2 * S4 + h * S4 + s
                            with pe.If(nk > 4 * s):
                                for c in range(4):
                                    last = nc.tensor.transpose(etp[:, c * P:(c + 1) * P], ea[:, h, 4 * s + c, 0:D], ident[:])
                                last.then_inc(turned, 1)
                                pe.wait_ge(turned_copied, n + 1)
                                nc.tensor.matmul(hps[:], w1[:], et[:], start=True, stop=True).then_inc(hidden, 1)
                                pe.wait_ge(hidden_relu, n + 1)
                                pe.wait_ge(weights_used, n + 1)
                                pe.sem_inc(tally, 1)
                                for c in range(4):
                                    last = nc.tensor.matmul(wps[:, s % 2, c], ht[:, s % 2, c * P:(c + 1) * P],
                                                            w2[:].rearrange("h k c -> h (k c)"), start=True, stop=True)
                                last.then_inc(weights, 1)
                            with pe.Else():
                                pe.drain().then_inc(turned, 1)
                                pe.drain().then_inc(hidden, 1)
                                pe.drain().then_inc(weights, 1)

            @block.scalar
            def _(act):
                with act.Fori(0, v["pairs"](act)) as it:
                    for h in range(2):
                        act.wait_ge(full[h], 16 * (it + 1))
                        act.sem_inc(tally, 1)
                        nk = act.value_load(rec[0:1, h, R_NK:R_NK + 1], min_val=0, max_val=U)
                        for s in range(S4):
                            n = it * 2 * S4 + h * S4 + s
                            act.wait_ge(turned, n + 1)
                            act.sem_inc(tally, 1)
                            with act.If(nk > 4 * s):
                                nc.scalar.copy(et[:], etp[:]).then_inc(turned_copied, 1)
                                act.wait_ge(hidden, n + 1)
                                nc.scalar.activation(ht[0:MH, s % 2], hps[:], ACT.Relu, bias=b1[:, 0:1]).then_inc(hidden_relu, 1)
                            with act.Else():
                                act.drain().then_inc(turned_copied, 1)
                                act.drain().then_inc(hidden_relu, 1)

            @block.vector
            def _(dve):
                nc.vector.memset(agg[:], 0.0)
                dve.drain()
                total = [dve.alloc_register(unique(nc, f"rows{h}")) for h in range(2)]
                for h in range(2):
                    dve.reg_mov(total[h], 0)
                    dve.sem_inc(used[h], 1)
                dve.sem_inc(weights_used, 2)
                with dve.Fori(0, v["pairs"](dve)) as it:
                    for h in range(2):
                        t = v["wait_rows"](dve, h, it, full[h], got[h], total)
                        nk = dve.value_load(rec[0:1, h, R_NK:R_NK + 1], min_val=0, max_val=U)
                        nc.vector.tensor_scalar(valid[:], iota16[:], rec[:, h, R_NV:R_NV + 1].bitcast(F32), None, ALU.is_lt)
                        dve.drain()
                        nc.vector.tensor_tensor(gz[:], g[:, h, :, 0:D], over(valid[:], 2, [P, U, D]), ALU.mult)
                        dve.wait_ge(attr[h], 16 * (it + 1))
                        dve.sem_inc(tally, 1)
                        dve.drain()
                        sh = lambda m: over(ea[:, h, :, D + m], 2, [P, U, 8])
                        vec = gz[:, :, 8:D].rearrange("p c (i m) -> p c i m", m=3)
                        nc.vector.tensor_tensor(z[:, h, 0, :, 0], gz[:, :, 0:8], sh(0), ALU.mult)
                        for m in range(3):
                            nc.vector.tensor_tensor(z[:, h, 1 + m, :, 0], gz[:, :, 0:8], sh(1 + m), ALU.mult)
                            nc.vector.tensor_tensor(z[:, h, 1 + m, :, 1], vec[:, :, :, m], sh(0), ALU.mult)
                            nc.vector.tensor_tensor(vs[:, :, :, m], vec[:, :, :, m], sh(1 + m), ALU.mult)
                        dve.drain()
                        nc.vector.tensor_reduce(bs[:], vs[:], axis=AX.X, op=ALU.add)
                        dve.drain()
                        nc.vector.tensor_scalar(z[:, h, 0, :, 1], bs[:], 1.0 / 3 ** 0.5, None, ALU.mult)
                        dve.drain()
                        own = agg[:, bass.ds(t, 1), 0:D].rearrange("p a f -> p (a f)")
                        for s in range(S4):
                            n = it * 2 * S4 + h * S4 + s
                            dve.wait_ge(weights, n + 1)
                            dve.sem_inc(tally, 1)
                            with dve.If(nk > 4 * s):
                                for q in range(4):
                                    zq = z[:, h, q, 4 * s:4 * s + 4].rearrange("p c j i -> p c (j i)")
                                    k0 = 0 if q == 0 else 128
                                    wq = wps[:, s % 2, :, k0:k0 + 128].rearrange("p c (j o) -> p c j o", o=8)
                                    nc.vector.tensor_tensor(prod[:, q].rearrange("p (c j) o -> p c j o", c=4), wq,
                                                            over(zq, 3, [P, 4, 16, 8]), ALU.mult)
                                dve.drain().then_inc(weights_used, 1)
                                nc.vector.tensor_reduce(red[:].rearrange("p (q o) -> p q o", q=4),
                                                        prod[:].rearrange("p q r o -> p q o r"), axis=AX.X, op=ALU.add)
                                dve.drain()
                                nc.vector.tensor_tensor(own, own, red[:], ALU.add)
                                dve.drain()
                            with dve.Else():
                                dve.drain().then_inc(weights_used, 1)
                        dve.drain().then_inc(used[h], 1)
                for h in range(2):
                    dve.free_register(total[h])


_PLAIN = {
    "x": "x", "src": "src", "dst": "dst", "W1": "L1_gnn_W1", "b1": "L1_gnn_b1", "W2": "L1_gnn_W2", "b2": "L1_gnn_b2",
    "si_w0": "L1_gnn_si_w0", "si_w1": "L1_gnn_si_w1", "lambda_max": "L2_gnn_lambda_max", "cheb_W": "L2_gnn_cheb_W",
    "cheb_b": "L2_gnn_cheb_b", "src_W": "L2_gnn_src_W", "src_b": "L2_gnn_src_b", "dst_W": "L2_gnn_dst_W",
    "dst_b": "L2_gnn_dst_b", "attn": "L2_gnn_attn", "b_l_in": "L3_gnn_b_l_in", "b_l_out": "L3_gnn_b_l_out",
}
_TURNED = {"W_l_in_T": "L3_gnn_W_l_in", "W_r_in_T": "L3_gnn_W_r_in", "W_l_out_T": "L3_gnn_W_l_out", "W_r_out_T": "L3_gnn_W_r_out"}


def kernel(**inputs):
    import numpy as np
    import concourse.bacc as bacc
    from concourse.bass_utils import run_bass_kernel_spmd

    arrays = {name: np.ascontiguousarray(inputs[of]) for name, of in _PLAIN.items()}
    arrays |= {name: np.ascontiguousarray(np.asarray(inputs[of]).T) for name, of in _TURNED.items()}
    arrays["betas"] = np.concatenate([np.asarray(inputs[f"L0_gnn_beta{i}"]) for i in (1, 2, 3)])
    arrays["attr"] = np.concatenate([np.asarray(inputs["edge_attr_32"]), np.asarray(inputs["edge_attr_4"])], axis=1)

    nc = bacc.Bacc("TRN2", target_bir_lowering=False, num_devices=1)
    aps = {n: nc.dram_tensor(f"in_{n}", a.shape, mybir.dt.from_np(a.dtype), kind="ExternalInput").ap() for n, a in arrays.items()}
    out = nc.dram_tensor("out_x", (N, D), F32, kind="ExternalOutput").ap()
    build(nc, aps, out)
    r = run_bass_kernel_spmd(nc, [{f"in_{n}": a for n, a in arrays.items()}], core_ids=[0])
    return r.results[0]["out_x"]
```

```python
import concourse.bass as bass
from concourse import mybir
from contextlib import ExitStack, contextmanager
from itertools import count

F32 = mybir.dt.float32
BF16 = mybir.dt.bfloat16
I32 = mybir.dt.int32
ALU = mybir.AluOpType
ACT = mybir.ActivationFunctionType
AX = mybir.AxisListType

P = 128
N = 12500
E = 200000
D = 32
NT = (N + P - 1) // P
NP = NT * P
EP, EC = 125, E // 125
U = 16
B = 4
W = D + 2
ONE, RN = D, D + 1
SPLIT = 64
MAXU = NT + E // U + 6
AW = 36
R_BASE, R_NV, R_TILE, R_NK, RW = 16, 17, 18, 19, 20
BIG = 1e30
G7, NG = 7, NT // 7
EPS_LN = 1e-5
EPS_NORM = 1e-12
MH = 64


def unique(nc, name):
    return f"{name}_{next(_names)}"


_names = count()


def sbuf(nc, name, shape, dt):
    return nc.sbuf_tensor(unique(nc, name), shape, dt)


def psum(nc, name, shape, dt):
    return nc.psum_tensor(unique(nc, name), shape, dt)


@contextmanager
def phase(nc, *names):
    with ExitStack() as stack:
        sems = [stack.enter_context(nc.semaphore(unique(nc, n))) for n in names]
        yield sems
        if sems:
            nums = sorted(s.num for s in sems)
            while nums:
                run = 1
                while run < len(nums) and nums[run] == nums[0] + run:
                    run += 1
                nc.gpsimd.dma_reset(range(nums[0], nums[0] + run))
                nc.gpsimd.sem_clear(range(nums[0], nums[0] + run))
                nums = nums[run:]
            nc.all_engine_barrier()


def over(ap, n, shape):
    return ap.unsqueeze(n).broadcast_to(shape)


def build(nc, A, out):
    ctx = ExitStack()
    with ctx:
        def sb(name, shape, dt=F32):
            return ctx.enter_context(sbuf(nc, name, shape, dt))

        def dram(name, shape, dt):
            return nc.dram_tensor(name, shape, dt, kind="Internal").ap()

        table = dram("table", (NP, W), F32)
        order = dram("order", (NP, 4), I32)
        srcw = dram("srcw", (E + U, 1), I32)
        attw = dram("attw", (E + U, AW), F32)
        recs = dram("recs", (MAXU, P, RW), I32)

        ident = sb("ident", [P, P])
        tri = sb("tri", [P, P])
        onesq = sb("onesq", [P, P])
        iota16 = sb("iota16", [P, U])
        nid = sb("nid", [P, NT], I32)
        degf = sb("degf", [P, NT])
        startf = sb("startf", [P, NT])
        kmax = sb("kmax", [P, NT])
        tcol = sb("tcol", [P, NT], I32)
        ulim = sb("ulim", [P, NT + 1], I32)
        ulimf = sb("ulimf", [P, NT + 1])
        ucnt = sb("ucnt", [P, 1], I32)
        x = sb("x", [P, NT, D])
        row = sb("row", [P, NT, W])
        agg = sb("agg", [P, NT, D + 1])
        aux = sb("aux", [P, NT, D])
        mx = sb("mx", [P, NT])
        small = sb("small", [P, 6, NT])
        g = sb("g", [P, B, U, W])
        rec = sb("rec", [P, B, RW], I32)
        big = sb("big", [P, NT * 96])
        negbeta = sb("negbeta", [P, 3])
        tally = ctx.enter_context(nc.semaphore("tally"))
        s_attr = ctx.enter_context(nc.semaphore("attributes_copied"))

        def make_constants():
            with phase(nc, "iota_done", "const_loaded") as (iota_done, const_loaded), \
                    sbuf(nc, "io", [P, P], I32) as io, sbuf(nc, "pc", [P, 1], I32) as pc, \
                    sbuf(nc, "iof", [P, P], F32) as iof, sbuf(nc, "pcf", [P, 1], F32) as pcf, \
                    sbuf(nc, "zero", [P, AW * U], F32) as zero, nc.Block() as block:
                @block.gpsimd
                def _(pool):
                    nc.gpsimd.iota(io[:], [[1, P]], base=0, channel_multiplier=0)
                    nc.gpsimd.iota(pc[:], [[0, 1]], base=0, channel_multiplier=1)
                    nc.gpsimd.iota(tcol[:], [[1, NT]], base=0, channel_multiplier=0)
                    pool.drain().then_inc(iota_done, 1)

                @block.vector
                def _(dve):
                    nc.vector.memset(onesq[:], 1.0)
                    nc.vector.memset(g[:], 0.0)
                    nc.vector.memset(row[:], 0.0)
                    nc.vector.memset(zero[:], 0.0)
                    dve.drain()
                    nc.vector.memset(row[:, :, ONE:ONE + 1], 1.0).then_inc(iota_done, 1)
                    dve.wait_ge(iota_done, 2)
                    nc.vector.tensor_copy(iof[:], io[:])
                    nc.vector.tensor_copy(pcf[:], pc[:])
                    dve.drain()
                    nc.vector.tensor_scalar(ident[:], iof[:], pcf[:, 0:1], None, ALU.is_equal)
                    nc.vector.tensor_scalar(tri[:], iof[:], pcf[:, 0:1], None, ALU.is_gt)
                    nc.vector.tensor_copy(iota16[:], iof[:, 0:U])
                    dve.wait_ge(const_loaded, 16 * 3)
                    nc.vector.tensor_scalar(negbeta[:], negbeta[:], -1.0, None, ALU.mult)

                @block.sync
                def _(sp):
                    sp.dma_start(negbeta[:], A["betas"].rearrange("(a b) -> a b", a=1).broadcast_to([P, 3])).then_inc(const_loaded, 16)
                    sp.wait_ge(iota_done, 2)
                    sp.dma_start(srcw[E:E + U, :].rearrange("a b -> b a"), zero[0:1, 0:U].bitcast(I32)).then_inc(const_loaded, 16)
                    sp.dma_start(attw[E:E + U, :].rearrange("(z a) b -> z (a b)", z=1), zero[0:1, 0:U * AW]).then_inc(const_loaded, 16)
                    sp.wait_ge(const_loaded, 16 * 3)

        def count_and_order():
            CH = 16
            pe_ctx = ExitStack()
            with pe_ctx:
                s = lambda n, sh, dt=F32: pe_ctx.enter_context(sbuf(nc, n, sh, dt))
                ps = lambda n, sh: pe_ctx.enter_context(psum(nc, n, sh, F32))
                dst_i = s("dst_i", [EP, EC], I32)
                part_i = s("part_i", [EP, EC], I32)
                hi = s("hi", [EP, EC], BF16)
                lo = s("lo", [EP, EC], BF16)
                iob = s("iob", [P, P], BF16)
                ioi = s("ioi", [P, P], I32)
                ohh = s("ohh", [EP, 2, CH, NT], BF16)
                ohl = s("ohl", [EP, 2, CH, P], BF16)
                zb = s("zb", [EP, P], BF16)
                hist = ps("hist", [NT, P])
                with phase(nc, "dst_loaded", "srcs_copied", "onehot", "used", "hist_zero", "iota_ready") as \
                        (dst_loaded, srcs_copied, onehot, used, hist_zero, iota_ready), nc.Block() as block:
                    @block.sync
                    def _(sp):
                        sp.dma_start(dst_i[:], A["dst"].rearrange("(p c) -> p c", c=EC)).then_inc(dst_loaded, 16)
                        sp.dma_start(srcw[0:E, :].rearrange("(p c) a -> p (c a)", p=EP), A["src"].rearrange("(p c) -> p c", c=EC)).then_inc(srcs_copied, 16)
                        sp.wait_ge(srcs_copied, 16)
                        sp.dma_start(attw[0:E, :].rearrange("(p c) b -> p (c b)", p=EP * 16), A["attr"].rearrange("(p c) b -> p (c b)", p=EP * 16)).then_inc(s_attr, 16)

                    @block.gpsimd
                    def _(pool):
                        nc.gpsimd.iota(ioi[:], [[1, P]], base=0, channel_multiplier=0).then_inc(iota_ready, 1)

                    @block.vector
                    def _(dve):
                        nc.vector.memset(zb[:], 0.0).then_inc(hist_zero, 1)
                        dve.wait_ge(iota_ready, 1)
                        nc.vector.tensor_copy(iob[:], ioi[:])
                        dve.wait_ge(dst_loaded, 16)
                        nc.vector.tensor_scalar(part_i[:], dst_i[:], 7, None, ALU.logical_shift_right)
                        dve.drain()
                        nc.vector.tensor_copy(hi[:], part_i[:])
                        dve.drain()
                        nc.vector.tensor_scalar(part_i[:], dst_i[:], P - 1, None, ALU.bitwise_and)
                        dve.drain()
                        nc.vector.tensor_copy(lo[:], part_i[:])
                        dve.drain()
                        with dve.Fori(0, EC // (2 * CH)) as it:
                            for h in range(2):
                                dve.wait_ge(used, 2 * it + h + 1)
                                dve.sem_inc(tally, 1)
                                c0 = (2 * it + h) * CH
                                nc.vector.tensor_tensor(ohh[:, h], over(iob[0:EP, 0:NT], 1, [EP, CH, NT]),
                                                        over(hi[:, bass.ds(c0, CH)], 2, [EP, CH, NT]), ALU.is_equal)
                                nc.vector.tensor_tensor(ohl[:, h], over(iob[0:EP, :], 1, [EP, CH, P]),
                                                        over(lo[:, bass.ds(c0, CH)], 2, [EP, CH, P]), ALU.is_equal)
                                dve.drain().then_inc(onehot, 1)

                    @block.tensor
                    def _(pe):
                        pe.wait_ge(hist_zero, 1)
                        nc.tensor.matmul(hist[:], zb[:, 0:NT], zb[:], start=True, stop=False)
                        pe.drain().then_inc(used, 2)
                        with pe.Fori(0, EC // (2 * CH)) as it:
                            for h in range(2):
                                pe.wait_ge(onehot, 2 * it + h + 1)
                                pe.sem_inc(tally, 1)
                                for c in range(CH):
                                    last = nc.tensor.matmul(hist[:], ohh[:, h, c], ohl[:, h, c], start=False, stop=False)
                                last.then_inc(used, 1)
                        nc.tensor.matmul(hist[:], zb[:, 0:NT], zb[:], start=False, stop=True)

                with ExitStack() as st:
                    s2 = lambda n, sh, dt=F32: st.enter_context(sbuf(nc, n, sh, dt))
                    deg = s2("deg", [NT, P])
                    first = s2("first", [NT, P])
                    z1 = s2("z1", [NT, 1])
                    cls = s2("cls", [NT, P])
                    oh = big[0:NT, 0:SPLIT * P].rearrange("p (b l) -> p b l", b=SPLIT)
                    cum = s2("cum", [NT, SPLIT, P])
                    cnt = s2("cnt", [NT, SPLIT + 1])
                    rowx = s2("rowx", [NT, SPLIT])
                    base = s2("base", [NT, SPLIT])
                    tot = s2("tot", [NT, SPLIT])
                    pos = s2("pos", [NT, P])
                    posi = s2("posi", [NT, P], I32)
                    ent = s2("ent", [NT, P, 4], I32)
                    iocl = s2("iocl", [NT, SPLIT])
                    pfx = st.enter_context(psum(nc, "pfx", [NT, SPLIT + 1], F32))
                    tots = st.enter_context(psum(nc, "tots", [NT, SPLIT], F32))
                    with phase(nc, "counted", "summed", "node_iota") as (counted, summed, node_iota), nc.Block() as block:
                        @block.gpsimd
                        def _(pool):
                            nc.gpsimd.memset(ent[:], 0).then_inc(node_iota, 1)
                            pool.wait_ge(node_iota, 1)
                            nc.gpsimd.iota(ent[:, :, 0], [[1, P]], base=0, channel_multiplier=P).then_inc(node_iota, 1)

                        @block.vector
                        def _(dve):
                            nc.vector.tensor_copy(deg[:], hist[:])
                            nc.vector.memset(z1[:], 0.0)
                            nc.vector.tensor_copy(iocl[:], ioi[0:NT, 0:SPLIT])
                            dve.drain()
                            nc.vector.tensor_tensor_scan(first[:], deg[:], z1[:].broadcast_to([NT, P]), 0.0, ALU.add, ALU.add)
                            nc.vector.tensor_reduce(cnt[:, SPLIT:SPLIT + 1], deg[:], axis=AX.X, op=ALU.add)
                            nc.vector.tensor_scalar(cls[:], deg[:], float(SPLIT - 1), -1.0, ALU.min, ALU.mult)
                            dve.drain()
                            nc.vector.tensor_scalar(cls[:], cls[:], float(SPLIT - 1), None, ALU.add)
                            dve.drain()
                            nc.vector.tensor_tensor(oh, over(iocl[:], 2, [NT, SPLIT, P]), over(cls[:], 1, [NT, SPLIT, P]), ALU.is_equal)
                            dve.drain()
                            nc.vector.tensor_reduce(cnt[:, 0:SPLIT], oh, axis=AX.X, op=ALU.add)
                            nc.vector.tensor_tensor_scan(cum[:].rearrange("p b l -> p (b l)"), big[0:NT, 0:SPLIT * P],
                                                         z1[:].broadcast_to([NT, SPLIT * P]), 0.0, ALU.add, ALU.add)
                            dve.drain().then_inc(counted, 1)
                            nc.vector.tensor_tensor_scan(rowx[:], cnt[:, 0:SPLIT], z1[:].broadcast_to([NT, SPLIT]), 0.0, ALU.add, ALU.add)
                            dve.drain()
                            nc.vector.tensor_tensor(rowx[:], rowx[:], cnt[:, 0:SPLIT], ALU.subtract)
                            dve.wait_ge(summed, 1)
                            nc.vector.tensor_copy(tot[:], tots[:])
                            nc.vector.tensor_tensor(first[:], first[:], deg[:], ALU.subtract)
                            dve.drain()
                            nc.vector.tensor_scalar(first[:], first[:], pfx[:, SPLIT:SPLIT + 1], None, ALU.add)
                            nc.vector.tensor_tensor_scan(base[:], tot[:], z1[:].broadcast_to([NT, SPLIT]), 0.0, ALU.add, ALU.add)
                            dve.drain()
                            nc.vector.tensor_tensor(base[:], base[:], tot[:], ALU.subtract)
                            dve.drain()
                            nc.vector.tensor_tensor(base[:], base[:], pfx[:, 0:SPLIT], ALU.add)
                            dve.drain()
                            nc.vector.tensor_tensor(base[:], base[:], rowx[:], ALU.subtract)
                            dve.drain()
                            nc.vector.tensor_tensor(cum[:], cum[:], over(base[:], 2, [NT, SPLIT, P]), ALU.add)
                            dve.drain()
                            nc.vector.tensor_tensor(cum[:], cum[:], oh, ALU.mult)
                            dve.drain()
                            nc.vector.tensor_reduce(pos[:], cum[:].rearrange("p b l -> p l b"), axis=AX.X, op=ALU.add)
                            dve.wait_ge(node_iota, 2)
                            nc.vector.tensor_copy(ent[:, :, 1], first[:])
                            nc.vector.tensor_copy(ent[:, :, 2], deg[:])
                            dve.drain()
                            nc.vector.tensor_scalar(posi[:], pos[:], -1.0, None, ALU.add)

                        @block.tensor
                        def _(pe):
                            pe.wait_ge(counted, 1)
                            nc.tensor.matmul(pfx[:], tri[0:NT, 0:NT], cnt[:], start=True, stop=True)
                            nc.tensor.matmul(tots[:], onesq[0:NT, 0:NT], cnt[:, 0:SPLIT], start=True, stop=True).then_inc(summed, 1)

                    C8 = 8
                    ix = s2("ix", [NT, 2, C8], I32)
                    en = s2("en", [NT, 2, C8 * 4], I32)
                    with phase(nc, "staged0", "staged1", "free0", "free1", "stored0", "stored1") as sem, nc.Block() as block:
                        staged, free, stored = sem[0:2], sem[2:4], sem[4:6]

                        @block.vector
                        def _(dve):
                            with dve.Fori(0, P // (2 * C8)) as it:
                                for h in range(2):
                                    dve.wait_ge(free[h], it + 1)
                                    dve.sem_inc(tally, 1)
                                    c0 = (2 * it + h) * C8
                                    nc.vector.tensor_copy(ix[:, h], posi[:, bass.ds(c0, C8)]).then_inc(staged[h], 1)
                                    nc.vector.tensor_copy(en[:, h], ent[:, bass.ds(c0, C8), :].rearrange("p a b -> p (a b)")).then_inc(staged[h], 1)

                        @block.gpsimd
                        def _(pool):
                            for h in range(2):
                                pool.sem_inc(free[h], 1)
                            with pool.Fori(0, P // (2 * C8)) as it:
                                for h in range(2):
                                    pool.wait_ge(staged[h], 2 * it + 2)
                                    pool.sem_inc(tally, 1)
                                    for c in range(C8):
                                        nc.gpsimd.indirect_dma_start(
                                            out=order, out_offset=bass.IndirectOffsetOnAxis(ap=ix[:, h, c:c + 1], axis=0),
                                            in_=en[:, h, 4 * c:4 * c + 4], in_offset=None).then_inc(stored[h], 16)
                                for h in range(2):
                                    pool.wait_ge(stored[h], 16 * C8 * (it + 1))
                                    pool.sem_inc(tally, 1)
                                    pool.sem_inc(free[h], 1)

        def load_order():
            with ExitStack() as st:
                s2 = lambda n, sh, dt=F32: st.enter_context(sbuf(nc, n, sh, dt))
                ordt = s2("ordt", [P, NT, 4], I32)
                kcol = s2("kcol", [NT, 1])
                diag = s2("diag", [NT, NT])
                ki = s2("ki", [P, NT], I32)
                nu = s2("nu", [P, NT])
                uf = s2("uf", [P, NT + 1])
                z1 = s2("z1b", [P, 1])
                tps = st.enter_context(psum(nc, "tps", [NT, P], F32))
                kps = st.enter_context(psum(nc, "kps", [P, NT], F32))
                with phase(nc, "order_loaded", "deg_ready", "transposed", "diag_ready", "spread") as \
                        (order_loaded, deg_ready, transposed, diag_ready, spread), nc.Block() as block:
                    @block.sync
                    def _(sp):
                        sp.dma_start(ordt[:], order.rearrange("(t p) c -> p t c", p=P)).then_inc(order_loaded, 16)

                    @block.vector
                    def _(dve):
                        dve.wait_ge(order_loaded, 16)
                        nc.vector.tensor_copy(nid[:], ordt[:, :, 0])
                        nc.vector.tensor_copy(startf[:], ordt[:, :, 1])
                        nc.vector.tensor_copy(degf[:], ordt[:, :, 2])
                        nc.vector.memset(z1[:], 0.0)
                        dve.drain().then_inc(deg_ready, 1)
                        dve.wait_ge(transposed, 1)
                        nc.vector.tensor_reduce(kcol[:], tps[:], axis=AX.X, op=ALU.max)
                        dve.drain()
                        nc.vector.tensor_scalar(diag[:], ident[0:NT, 0:NT], kcol[:, 0:1], None, ALU.mult).then_inc(diag_ready, 1)
                        dve.wait_ge(spread, 1)
                        nc.vector.tensor_copy(kmax[:], kps[:])
                        dve.drain()
                        nc.vector.tensor_scalar(ki[:], kmax[:], float(U - 1), None, ALU.add)
                        dve.drain()
                        nc.vector.tensor_scalar(ki[:], ki[:], 4, None, ALU.logical_shift_right)
                        dve.drain()
                        nc.vector.tensor_scalar(nu[:], ki[:], 1.0, None, ALU.max)
                        nc.vector.memset(uf[:, 0:1], 0.0)
                        dve.drain()
                        nc.vector.tensor_tensor_scan(uf[:, 1:NT + 1], nu[:], z1[:].broadcast_to([P, NT]), 0.0, ALU.add, ALU.add)
                        dve.drain()
                        nc.vector.tensor_copy(ulimf[:], uf[:])
                        nc.vector.tensor_scalar(ki[:, 0:1], uf[:, NT:NT + 1], float(B - 1), None, ALU.add)
                        dve.drain()
                        nc.vector.memset(uf[:, NT:NT + 1], float(1 << 20))
                        nc.vector.tensor_scalar(ucnt[:], ki[:, 0:1], B.bit_length() - 1, None, ALU.logical_shift_right)
                        dve.drain()
                        nc.vector.tensor_copy(ulim[:], uf[:])

                    @block.tensor
                    def _(pe):
                        pe.wait_ge(deg_ready, 1)
                        nc.tensor.transpose(tps[:], degf[:], ident[:]).then_inc(transposed, 1)
                        pe.wait_ge(diag_ready, 1)
                        nc.tensor.matmul(kps[:], onesq[0:NT, :], diag[:], start=True, stop=True).then_inc(spread, 1)

        def groups(eng):
            return eng.value_load(ucnt[0:1, 0:1], min_val=1, max_val=MAXU // B)

        def write_records():
            with sbuf(nc, "k0", [P, B], F32) as k0, sbuf(nc, "bi", [P, B], I32) as bi, \
                    sbuf(nc, "win", [P, B, U], I32) as win, sbuf(nc, "rb", [P, B, RW], I32) as rb, \
                    sbuf(nc, "nv", [P, B], F32) as nv, sbuf(nc, "nk", [P, B], F32) as nk, \
                    sbuf(nc, "vd", [P, B, U], F32) as vd, sbuf(nc, "uu", [P, B], F32) as uu, \
                    phase(nc, "base_ready", "rec_ready", "rec_left", "rec_stored", "win0", "win1", "win2", "win3") as sem, \
                    nc.Block() as block:
                base_ready, rec_ready, rec_left, rec_stored, window = sem[0], sem[1], sem[2], sem[3], sem[4:]

                @block.vector
                def _(dve):
                    nc.vector.tensor_copy(uu[:], iota16[:, 0:B])
                    tile = dve.alloc_register(unique(nc, "tile"))
                    dve.reg_mov(tile, 0)
                    dve.drain()
                    with dve.Fori(0, groups(dve)) as it:
                        ts = []
                        for b in range(B):
                            last = dve.value_load(ulim[0:1, bass.ds(dve.snap(tile, min_val=0, max_val=NT - 1) + 1, 1)], min_val=0, max_val=1 << 20)
                            with dve.If(last == it * B + b):
                                dve.reg_add(tile, tile, 1)
                            t = dve.snap(tile, min_val=0, max_val=NT - 1)
                            ts.append(t)
                            nc.vector.tensor_scalar(k0[:, b:b + 1], ulimf[:, bass.ds(t, 1)], uu[:, b:b + 1], -float(U), ALU.subtract, ALU.mult)
                        dve.drain()
                        nc.vector.tensor_scalar(uu[:], uu[:], float(B), None, ALU.add)
                        for b, t in enumerate(ts):
                            nc.vector.tensor_scalar(bi[:, b:b + 1], startf[:, bass.ds(t, 1)], k0[:, b:b + 1], float(E), ALU.add, ALU.min)
                            dve.drain().then_inc(base_ready, 1)
                            nc.vector.tensor_tensor(nv[:, b:b + 1], degf[:, bass.ds(t, 1)], k0[:, b:b + 1], ALU.subtract)
                            nc.vector.tensor_scalar(nk[:, b:b + 1], kmax[:, bass.ds(t, 1)], k0[:, b:b + 1], float(U), ALU.subtract, ALU.min)
                        dve.wait_ge(rec_left, it + 1)
                        dve.sem_inc(tally, 1)
                        dve.drain()
                        for b, t in enumerate(ts):
                            nc.vector.tensor_copy(rb[:, b, R_TILE:R_TILE + 1], tcol[:, bass.ds(t, 1)])
                            nc.vector.tensor_scalar(vd[:, b], iota16[:], nv[:, b:b + 1], None, ALU.is_lt)
                        nc.vector.tensor_copy(rb[:, :, R_BASE], bi[:])
                        nc.vector.tensor_copy(rb[:, :, R_NV].bitcast(F32), nv[:])
                        nc.vector.tensor_scalar(rb[:, :, R_NK], nk[:], 0.0, None, ALU.max)
                        dve.drain()
                        for b in range(B):
                            dve.wait_ge(window[b], 16 * (it + 1))
                            nc.vector.tensor_tensor(rb[:, b, 0:U], win[:, b], vd[:, b], ALU.mult)
                        dve.drain().then_inc(rec_ready, 1)
                    dve.free_register(tile)

                @block.gpsimd
                def _(pool):
                    with pool.Fori(0, groups(pool)) as it:
                        for b in range(B):
                            pool.wait_ge(base_ready, B * it + b + 1)
                            pool.sem_inc(tally, 1)
                            nc.gpsimd.indirect_dma_start(out=win[:, b], out_offset=None, in_=srcw,
                                                         in_offset=bass.IndirectOffsetOnAxis(ap=bi[:, b:b + 1], axis=0)).then_inc(window[b], 16)

                @block.sync
                def _(sp):
                    sp.sem_inc(rec_left, 1)
                    with sp.Fori(0, groups(sp)) as it:
                        sp.wait_ge(rec_ready, it + 1)
                        sp.dma_start(recs[bass.ds(it * B, B), :, :].rearrange("u p w -> p u w"), rb[:]).then_inc(rec_stored, 16)
                        sp.wait_ge(rec_stored, 16 * (it + 1))
                        sp.sem_inc(rec_left, 1)

        def load_nodes():
            with sbuf(nc, "ixs", [P, 2, G7], I32) as ixs, sbuf(nc, "xs", [P, 2, G7, D], F32) as xs, \
                    phase(nc, "staged0", "staged1", "free0", "free1", "got0", "got1") as sem, nc.Block() as block:
                staged, free, got = sem[0:2], sem[2:4], sem[4:6]

                @block.vector
                def _(dve):
                    nc.vector.memset(xs[:], 0.0)
                    dve.drain()
                    with dve.Fori(0, NG // 2) as it:
                        for h in range(2):
                            nc.vector.tensor_copy(ixs[:, h], nid[:, bass.ds((2 * it + h) * G7, G7)])
                            dve.drain().then_inc(staged[h], 1)
                        for h in range(2):
                            dve.wait_ge(got[h], 16 * G7 * (it + 1))
                            dve.sem_inc(tally, 1)
                            nc.vector.tensor_copy(x[:, bass.ds((2 * it + h) * G7, G7), :], xs[:, h])
                            dve.drain()
                            nc.vector.memset(xs[:, h], 0.0)
                            dve.drain()

                @block.gpsimd
                def _(pool):
                    with pool.Fori(0, NG // 2) as it:
                        for h in range(2):
                            pool.wait_ge(staged[h], it + 1)
                            pool.sem_inc(tally, 1)
                            for c in range(G7):
                                nc.gpsimd.indirect_dma_start(
                                    out=xs[:, h, c], out_offset=None, in_=A["x"],
                                    in_offset=bass.IndirectOffsetOnAxis(ap=ixs[:, h, c:c + 1], axis=0),
                                    bounds_check=N - 1, oob_is_err=False).then_inc(got[h], 16)

        def scatter_rows(dest, source, width, bound=None):
            with sbuf(nc, "ixs", [P, 2, G7], I32) as ixs, sbuf(nc, "rs", [P, 2, G7, width], F32) as rs, \
                    phase(nc, "staged0", "staged1", "free0", "free1", "stored0", "stored1") as sem, nc.Block() as block:
                staged, free, stored = sem[0:2], sem[2:4], sem[4:6]

                @block.scalar
                def _(act):
                    with act.Fori(0, NG // 2) as it:
                        for h in range(2):
                            act.wait_ge(free[h], it + 1)
                            act.sem_inc(tally, 1)
                            t0 = (2 * it + h) * G7
                            nc.scalar.copy(ixs[:, h], nid[:, bass.ds(t0, G7)]).then_inc(staged[h], 1)
                            nc.scalar.copy(rs[:, h], source[:, bass.ds(t0, G7), 0:width]).then_inc(staged[h], 1)

                @block.gpsimd
                def _(pool):
                    for h in range(2):
                        pool.sem_inc(free[h], 1)
                    more = {} if bound is None else {"bounds_check": bound, "oob_is_err": False}
                    with pool.Fori(0, NG // 2) as it:
                        for h in range(2):
                            pool.wait_ge(staged[h], 2 * it + 2)
                            pool.sem_inc(tally, 1)
                            for c in range(G7):
                                nc.gpsimd.indirect_dma_start(
                                    out=dest, out_offset=bass.IndirectOffsetOnAxis(ap=ixs[:, h, c:c + 1], axis=0),
                                    in_=rs[:, h, c], in_offset=None, **more).then_inc(stored[h], 16)
                        for h in range(2):
                            pool.wait_ge(stored[h], 16 * G7 * (it + 1))
                            pool.sem_inc(tally, 1)
                            pool.sem_inc(free[h], 1)

        NAMES = [f"{n}{b}" for n in ("full", "used", "got") for b in range(B)]

        def load_record(sp, it, h, full, used):
            sp.wait_ge(used, it + 1)
            sp.dma_start(rec[:, h], recs[bass.ds(B * it + h, 1), :, :].rearrange("a p w -> p (a w)")).then_inc(full, 16)

        def gather_unit(pool, it, h, full, got):
            pool.wait_ge(full, 16 * (it + 1))
            pool.sem_inc(tally, 1)
            nk = pool.value_load(rec[0:1, h, R_NK:R_NK + 1], min_val=0, max_val=U)
            for c in range(U):
                with pool.If(nk > c):
                    nc.gpsimd.indirect_dma_start(out=g[:, h, c], out_offset=None, in_=table,
                                                 in_offset=bass.IndirectOffsetOnAxis(ap=rec[:, h, c:c + 1], axis=0)).then_inc(got, 16)

        def wait_rows(eng, h, it, full, got, total):
            eng.wait_ge(full, 16 * (it + 1))
            eng.sem_inc(tally, 1)
            t = eng.value_load(rec[0:1, h, R_TILE:R_TILE + 1], min_val=0, max_val=NT - 1)
            nk = eng.value_load(rec[0:1, h, R_NK:R_NK + 1], min_val=0, max_val=U)
            eng.reg_add(total[h], total[h], nk)
            eng.wait_ge(got, eng.snap(total[h]) * 16)
            eng.sem_inc(tally, 1)
            return t

        def sum_rows(dve, values, keep, t, h, valid, wp, red, cols):
            nc.vector.tensor_tensor(wp[:, h, :, 0:cols], values[:, :, 0:cols], over(keep, 2, [P, U, cols]), ALU.mult)
            dve.drain()
            nc.vector.tensor_reduce(red[:, h, 0:cols], wp[:, h, :, 0:cols].rearrange("p c f -> p f c"), axis=AX.X, op=ALU.add)
            dve.drain()

        def gather_sum():
            with sbuf(nc, "valid", [P, B, U], F32) as valid, sbuf(nc, "wp", [P, B, U, D + 1], F32) as wp, \
                    sbuf(nc, "red", [P, B, D + 1], F32) as red, \
                    phase(nc, *NAMES) as sem, nc.Block() as block:
                full, used, got = sem[0:B], sem[B:2 * B], sem[2 * B:3 * B]

                @block.sync
                def _(sp):
                    with sp.Fori(0, groups(sp)) as it:
                        for h in range(B):
                            load_record(sp, it, h, full[h], used[h])

                @block.gpsimd
                def _(pool):
                    with pool.Fori(0, groups(pool)) as it:
                        for h in range(B):
                            gather_unit(pool, it, h, full[h], got[h])

                @block.vector
                def _(dve):
                    nc.vector.memset(agg[:], 0.0)
                    dve.drain()
                    total = [dve.alloc_register(unique(nc, f"rows{h}")) for h in range(B)]
                    for h in range(B):
                        dve.reg_mov(total[h], 0)
                        dve.sem_inc(used[h], 1)
                    with dve.Fori(0, groups(dve)) as it:
                        for h in range(B):
                            t = wait_rows(dve, h, it, full[h], got[h], total)
                            nc.vector.tensor_scalar(valid[:, h], iota16[:], rec[:, h, R_NV:R_NV + 1].bitcast(F32), None, ALU.is_lt)
                            dve.drain()
                            sum_rows(dve, g[:, h], valid[:, h], t, h, valid, wp, red, D)
                            own = agg[:, bass.ds(t, 1), 0:D].rearrange("p a f -> p (a f)")
                            nc.vector.tensor_tensor(own, own, red[:, h, 0:D], ALU.add)
                            dve.drain().then_inc(used[h], 1)
                    for h in range(B):
                        dve.free_register(total[h])

        def gather_attend(logits):
            with sbuf(nc, "valid", [P, B, U], F32) as valid, sbuf(nc, "wp", [P, B, U, D + 1], F32) as wp, \
                    sbuf(nc, "red", [P, B, D + 1], F32) as red, sbuf(nc, "lg", [P, B, U], F32) as lg, \
                    sbuf(nc, "pr", [P, B, U], F32) as pr, sbuf(nc, "st", [P, B, 4], F32) as st, \
                    phase(nc, *NAMES, "logits", "exps") as sem, nc.Block() as block:
                full, used, got, logits_ready, exps_ready = sem[0:B], sem[B:2 * B], sem[2 * B:3 * B], sem[-2], sem[-1]

                @block.sync
                def _(sp):
                    with sp.Fori(0, groups(sp)) as it:
                        for h in range(B):
                            load_record(sp, it, h, full[h], used[h])

                @block.gpsimd
                def _(pool):
                    with pool.Fori(0, groups(pool)) as it:
                        for h in range(B):
                            gather_unit(pool, it, h, full[h], got[h])

                @block.scalar
                def _(act):
                    with act.Fori(0, groups(act)) as it:
                        for h in range(B):
                            act.wait_ge(logits_ready, B * it + h + 1)
                            act.sem_inc(tally, 1)
                            nc.scalar.activation(pr[:, h], lg[:, h], ACT.Exp, bias=st[:, h, 1:2], scale=-1.0)
                            nc.scalar.activation(st[:, h, 2:3], st[:, h, 0:1], ACT.Exp, bias=st[:, h, 1:2], scale=-1.0)
                            act.drain().then_inc(exps_ready, 1)

                @block.vector
                def _(dve):
                    total = [dve.alloc_register(unique(nc, f"rows{h}")) for h in range(B)]
                    for h in range(B):
                        dve.reg_mov(total[h], 0)
                        dve.sem_inc(used[h], 1)
                    with dve.Fori(0, groups(dve)) as it:
                        for h in range(B):
                            t = wait_rows(dve, h, it, full[h], got[h], total)
                            nc.vector.tensor_scalar(valid[:, h], iota16[:], rec[:, h, R_NV:R_NV + 1].bitcast(F32), None, ALU.is_lt)
                            mine = aux[:, bass.ds(t, 1), :].rearrange("p a f -> p (a f)")
                            logits(dve, h, over(mine, 1, [P, U, D]), wp[:, h], lg[:, h], valid[:, h])
                            dve.drain()
                            m_t = mx[:, bass.ds(t, 1)]
                            nc.vector.tensor_reduce(st[:, h, 3:4], lg[:, h], axis=AX.X, op=ALU.min)
                            nc.vector.tensor_copy(st[:, h, 0:1], m_t)
                            dve.drain()
                            nc.vector.tensor_tensor(st[:, h, 1:2], st[:, h, 3:4], st[:, h, 0:1], ALU.min)
                            dve.drain().then_inc(logits_ready, 1)
                            dve.wait_ge(exps_ready, B * it + h + 1)
                            dve.sem_inc(tally, 1)
                            nc.vector.tensor_copy(m_t, st[:, h, 1:2])
                            sum_rows(dve, g[:, h], pr[:, h], t, h, valid, wp, red, D + 1)
                            own = agg[:, bass.ds(t, 1), :].rearrange("p a f -> p (a f)")
                            nc.vector.scalar_tensor_tensor(own, own, st[:, h, 2:3], red[:, h, :], ALU.mult, ALU.add)
                            dve.drain().then_inc(used[h], 1)
                    for h in range(B):
                        dve.free_register(total[h])

        def masked(dve, lg, valid, scale):
            nc.vector.tensor_scalar(valid, valid, -BIG, BIG, ALU.mult, ALU.add)
            dve.drain()
            nc.vector.scalar_tensor_tensor(lg, lg, scale, valid, ALU.mult, ALU.add)

        def node_product(source, kin, weight, m, finish):
            with sbuf(nc, "stage", [P, G7, kin], F32) as stage, sbuf(nc, "xt", [kin, G7 * P], F32) as xt, \
                    psum(nc, "tp", [kin, 2, 4 * P], F32) as tp, psum(nc, "po", [P, 512], F32) as po, \
                    phase(nc, "staged", "transposed", "copied", "product", "finished") as \
                    (staged, transposed, copied, product, finished), nc.Block() as block:
                tpf = tp[:].rearrange("k a b -> k (a b)")

                @block.scalar
                def _(act):
                    with act.Fori(0, NG) as i:
                        act.wait_ge(finished, i + 1)
                        act.sem_inc(tally, 1)
                        nc.scalar.copy(stage[:], source[:, bass.ds(i * G7, G7), :]).then_inc(staged, 1)
                        act.wait_ge(transposed, i + 1)
                        act.sem_inc(tally, 1)
                        nc.scalar.copy(xt[:, 0:4 * P], tpf[:, 0:4 * P])
                        nc.scalar.copy(xt[:, 4 * P:G7 * P], tpf[:, 4 * P:G7 * P])
                        act.drain().then_inc(copied, 1)

                @block.tensor
                def _(pe):
                    with pe.Fori(0, NG) as i:
                        pe.wait_ge(staged, i + 1)
                        pe.sem_inc(tally, 1)
                        for c in range(G7):
                            last = nc.tensor.transpose(tpf[:, c * P:(c + 1) * P], stage[:, c], ident[:])
                        last.then_inc(transposed, 1)
                        pe.wait_ge(copied, i + 1)
                        pe.sem_inc(tally, 1)
                        for c in range(G7):
                            last = nc.tensor.matmul(po[:, c * m:(c + 1) * m], xt[:, c * P:(c + 1) * P], weight, start=True, stop=True)
                        last.then_inc(product, 1)

                @block.vector
                def _(dve):
                    dve.sem_inc(finished, 1)
                    with dve.Fori(0, NG) as i:
                        dve.wait_ge(product, i + 1)
                        dve.sem_inc(tally, 1)
                        finish(dve, bass.ds(i * G7, G7), po[:, 0:G7 * m].rearrange("p (c m) -> p c m", c=G7))
                        dve.drain().then_inc(finished, 1)

        def with_sqrt(before, after, name="root"):
            with phase(nc, "squares", "roots") as (squares, roots), nc.Block() as block:
                @block.vector
                def _(dve):
                    before(dve)
                    dve.drain().then_inc(squares, 1)
                    dve.wait_ge(roots, 1)
                    after(dve)

                @block.scalar
                def _(act):
                    act.wait_ge(squares, 1)
                    nc.scalar.activation(small[:, 1], small[:, 0], ACT.Sqrt).then_inc(roots, 1)

        scratch = big[:, 0:NT * D].rearrange("p (t f) -> p t f", f=D)
        scratch2 = big[:, NT * D:NT * 2 * D].rearrange("p (t f) -> p t f", f=D)

        def node_norms(source):
            def before(dve):
                nc.vector.tensor_tensor(scratch, source, source, ALU.mult)
                nc.vector.tensor_copy(row[:, :, 0:D], source)
                dve.drain()
                nc.vector.tensor_reduce(small[:, 0], scratch, axis=AX.X, op=ALU.add)
                dve.drain()
                nc.vector.tensor_scalar(small[:, 0], small[:, 0], EPS_NORM ** 2 / 100, None, ALU.max)

            def after(dve):
                nc.vector.tensor_scalar(small[:, 2], small[:, 1], EPS_NORM, None, ALU.max)
                dve.drain()
                nc.vector.reciprocal(small[:, 3], small[:, 2])
                dve.drain()
                nc.vector.tensor_copy(row[:, :, RN], small[:, 3])
                nc.vector.tensor_tensor(aux[:], source, over(small[:, 3], 2, [P, NT, D]), ALU.mult)
            with_sqrt(before, after)

        def layer_norm(prepare):
            def before(dve):
                prepare(dve)
                dve.drain()
                nc.vector.tensor_reduce(small[:, 2], scratch, axis=AX.X, op=ALU.add)
                dve.drain()
                nc.vector.tensor_scalar(small[:, 2], small[:, 2], 1.0 / D, None, ALU.mult)
                dve.drain()
                nc.vector.tensor_tensor(x[:], scratch, over(small[:, 2], 2, [P, NT, D]), ALU.subtract)
                dve.drain()
                nc.vector.tensor_tensor(scratch, x[:], x[:], ALU.mult)
                dve.drain()
                nc.vector.tensor_reduce(small[:, 3], scratch, axis=AX.X, op=ALU.add)
                dve.drain()
                nc.vector.tensor_scalar(small[:, 0], small[:, 3], 1.0 / D, EPS_LN, ALU.mult, ALU.add)

            def after(dve):
                nc.vector.reciprocal(small[:, 2], small[:, 1])
                dve.drain()
                nc.vector.tensor_tensor(x[:], x[:], over(small[:, 2], 2, [P, NT, D]), ALU.mult)
            with_sqrt(before, after)

        def on_vector(work):
            with nc.Block() as block:
                @block.vector
                def _(dve):
                    work(dve)

        make_constants()
        count_and_order()
        load_order()
        write_records()
        load_nodes()

        own = row[:, :, 0:D]
        on_vector(lambda dve: nc.vector.tensor_copy(row[:, :, 0:D], x[:]))
        with nc.Fori(0, 3) as r:
            beta = sb_beta = small[:, 5, 0:1]

            def square(dve):
                nc.vector.tensor_copy(beta, negbeta[:, bass.ds(r, 1)])
                nc.vector.tensor_tensor(scratch, own, own, ALU.mult)
                dve.drain()
                nc.vector.tensor_reduce(small[:, 0], scratch, axis=AX.X, op=ALU.add)
                dve.drain()
                nc.vector.tensor_scalar(small[:, 0], small[:, 0], EPS_NORM ** 2 / 100, None, ALU.max)

            def start_with_self(dve):
                nc.vector.tensor_scalar(small[:, 2], small[:, 1], EPS_NORM, None, ALU.max)
                dve.drain()
                nc.vector.reciprocal(small[:, 3], small[:, 2])
                dve.drain()
                nc.vector.tensor_copy(row[:, :, RN], small[:, 3])
                nc.vector.tensor_tensor(aux[:], own, over(small[:, 3], 2, [P, NT, D]), ALU.mult)
                dve.drain()
                nc.vector.tensor_tensor(scratch, aux[:], aux[:], ALU.mult)
                nc.vector.tensor_copy(agg[:], row[:, :, 0:D + 1])
                dve.drain()
                nc.vector.tensor_reduce(mx[:], scratch, axis=AX.X, op=ALU.add)
                dve.drain()
                nc.vector.tensor_scalar(mx[:], mx[:], beta, None, ALU.mult)
            with_sqrt(square, start_with_self)

            def cosine(dve, h, mine, wp, lg, valid):
                nc.vector.tensor_tensor(wp[:, :, 0:D], g[:, h, :, 0:D], mine, ALU.mult)
                dve.drain()
                nc.vector.tensor_reduce(lg, wp[:, :, 0:D], axis=AX.X, op=ALU.add)
                dve.drain()
                nc.vector.tensor_tensor(lg, lg, g[:, h, :, RN], ALU.mult)
                masked(dve, lg, valid, beta)

            scatter_rows(table, row, W)
            gather_attend(cosine)

            def divide(dve):
                nc.vector.reciprocal(small[:, 2], agg[:, :, D])
                dve.drain()
                nc.vector.tensor_tensor(row[:, :, 0:D], agg[:, :, 0:D], over(small[:, 2], 2, [P, NT, D]), ALU.mult)
            on_vector(divide)
        layer_norm(lambda dve: nc.vector.tensor_tensor(scratch, x[:], row[:, :, 0:D], ALU.add))

        on_vector(lambda dve: nc.vector.tensor_copy(row[:, :, 0:D], x[:]))
        scatter_rows(table, row, W)
        lin = big[:, 2 * NT * D:3 * NT * D].rearrange("p (t f) -> p t f", f=D)
        with ExitStack() as st:
            s2 = lambda n, sh, dt=F32: st.enter_context(sbuf(nc, n, sh, dt))
            selfw = s2("selfw", [D, D])
            w1 = s2("w1", [D, MH])
            w2 = s2("w2", [MH + 1, 4, 64])
            b1 = s2("b1", [MH, 1])
            ht = s2("ht", [MH + 1, 4, 512])
            with phase(nc, "zeroed", "weights_loaded") as (zeroed, weights_loaded), nc.Block() as block:
                @block.vector
                def _(dve):
                    nc.vector.memset(selfw[:], 0.0)
                    nc.vector.memset(ht[MH:MH + 1], 1.0)
                    dve.drain().then_inc(zeroed, 1)
                    dve.wait_ge(weights_loaded, 16 * (1 + 24 + 2 + 8))
                    nc.vector.tensor_scalar(w2[:, 1], w2[:, 1], 1.0 / 3 ** 0.5, None, ALU.mult)

                @block.sync
                def _(sp):
                    sp.wait_ge(zeroed, 1)
                    sp.dma_start(selfw[0:8, 0:8], A["si_w0"]).then_inc(weights_loaded, 16)
                    for m in range(3):
                        for i in range(8):
                            sp.dma_start(selfw[8 + 3 * i + m:9 + 3 * i + m, 8 + 8 * m:16 + 8 * m], A["si_w1"][i:i + 1, :]).then_inc(weights_loaded, 16)
                    sp.dma_start(w1[:], A["W1"]).then_inc(weights_loaded, 16)
                    sp.dma_start(b1[:], A["b1"].rearrange("(a b) -> a b", b=1)).then_inc(weights_loaded, 16)
                    w2_in = A["W2"].rearrange("h (k c) -> h k c", k=4)
                    b2_in = A["b2"].rearrange("(z k c) -> z k c", z=1, k=4)
                    for k, of in enumerate((0, 3, 1, 2)):
                        sp.dma_start(w2[0:MH, k], w2_in[:, of]).then_inc(weights_loaded, 16)
                        sp.dma_start(w2[MH:MH + 1, k], b2_in[:, of]).then_inc(weights_loaded, 16)
                    sp.wait_ge(weights_loaded, 16 * (1 + 24 + 2 + 8))
                    sp.wait_ge(s_attr, 16)

            node_product(x, D, selfw[:], D, lambda dve, tiles, prod: nc.vector.tensor_copy(lin[:, tiles, :], prod))
            edge_messages(nc, locals())
        def messages_in(dve):
            a4 = agg[:, :, 0:D]
            nc.vector.tensor_scalar(scratch2, lin, 1.0 / 8 ** 0.5, None, ALU.mult)
            dve.drain()
            nc.vector.scalar_tensor_tensor(scratch2, a4, 0.25, scratch2, ALU.mult, ALU.add)
            dve.drain()
            nc.vector.tensor_tensor(scratch[:, :, 0:8], x[:, :, 0:8], scratch2[:, :, 0:8], ALU.add)
            for m in range(3):
                nc.vector.tensor_tensor(scratch[:, :, 8 + m:D:3], x[:, :, 8 + m:D:3], scratch2[:, :, 8 + 8 * m:16 + 8 * m], ALU.add)
        layer_norm(messages_in)

        dinv, lam = small[:, 4], small[:, 5, 0:4]
        cat = big[:].rearrange("p (t f) -> p t f", f=3 * D)
        with ExitStack() as st:
            s2 = lambda n, sh, dt=F32: st.enter_context(sbuf(nc, n, sh, dt))
            cw = s2("cw", [3 * D, D])
            cb = s2("cb", [P, D])
            fw = s2("fw", [D, 2 * D])
            fb = s2("fb", [P, 2 * D])
            att = s2("att", [P, D])
            hc = s2("hc", [P, NT, D])
            with phase(nc, "weights_loaded") as (weights_loaded,), nc.Block() as block:
                @block.sync
                def _(sp):
                    spread = lambda a, n: a.rearrange("(a b) -> a b", a=1).broadcast_to([P, n])
                    sp.dma_start(cw[:], A["cheb_W"]).then_inc(weights_loaded, 16)
                    sp.dma_start(cb[:], spread(A["cheb_b"], D)).then_inc(weights_loaded, 16)
                    sp.dma_start(fw[:, 0:D], A["src_W"]).then_inc(weights_loaded, 16)
                    sp.dma_start(fw[:, D:2 * D], A["dst_W"]).then_inc(weights_loaded, 16)
                    sp.dma_start(fb[:, 0:D], spread(A["src_b"], D)).then_inc(weights_loaded, 16)
                    sp.dma_start(fb[:, D:2 * D], spread(A["dst_b"], D)).then_inc(weights_loaded, 16)
                    sp.dma_start(att[:], A["attn"].broadcast_to([P, D])).then_inc(weights_loaded, 16)
                    sp.dma_start(lam[:, 0:1], spread(A["lambda_max"], 1)).then_inc(weights_loaded, 16)
                    sp.wait_ge(weights_loaded, 16 * 8)

            def degrees(dve):
                nc.vector.tensor_scalar(small[:, 0], degf[:], 1.0, None, ALU.max)
                nc.vector.reciprocal(lam[:, 1:2], lam[:, 0:1])
                dve.drain()
                nc.vector.tensor_scalar(lam[:, 1:2], lam[:, 1:2], 2.0, None, ALU.mult)
                dve.drain()
                nc.vector.tensor_scalar(lam[:, 2:3], lam[:, 1:2], -1.0, None, ALU.add)
                nc.vector.tensor_scalar(lam[:, 3:4], lam[:, 1:2], -1.0, None, ALU.mult)

            def scaled(dve):
                nc.vector.reciprocal(dinv, small[:, 1])
                dve.drain()
                nc.vector.tensor_tensor(row[:, :, 0:D], x[:], over(dinv, 2, [P, NT, D]), ALU.mult)
                nc.vector.tensor_copy(cat[:, :, 0:D], x[:])
            with_sqrt(degrees, scaled)
            scatter_rows(table, row, W)
            gather_sum()

            def first_term(dve):
                c1 = cat[:, :, D:2 * D]
                nc.vector.tensor_tensor(c1, agg[:, :, 0:D], over(dinv, 2, [P, NT, D]), ALU.mult)
                nc.vector.tensor_scalar(hc[:], x[:], lam[:, 2:3], None, ALU.mult)
                dve.drain()
                nc.vector.scalar_tensor_tensor(c1, c1, lam[:, 3:4], hc[:], ALU.mult, ALU.add)
                dve.drain()
                nc.vector.tensor_tensor(row[:, :, 0:D], c1, over(dinv, 2, [P, NT, D]), ALU.mult)
            on_vector(first_term)
            scatter_rows(table, row, W)
            gather_sum()

            def second_term(dve):
                c2 = cat[:, :, 2 * D:3 * D]
                nc.vector.tensor_tensor(c2, agg[:, :, 0:D], over(dinv, 2, [P, NT, D]), ALU.mult)
                nc.vector.tensor_scalar(hc[:], cat[:, :, D:2 * D], lam[:, 2:3], None, ALU.mult)
                dve.drain()
                nc.vector.scalar_tensor_tensor(c2, c2, lam[:, 3:4], hc[:], ALU.mult, ALU.add)
                dve.drain()
                nc.vector.scalar_tensor_tensor(c2, c2, 2.0, x[:], ALU.mult, ALU.subtract)
            on_vector(second_term)

            def relu_bias(dve, tiles, prod):
                nc.vector.tensor_tensor(hc[:, tiles, :], prod, over(cb[:], 1, [P, G7, D]), ALU.add)
                dve.drain()
                nc.vector.tensor_scalar(hc[:, tiles, :], hc[:, tiles, :], 0.0, None, ALU.max)
            node_product(cat, 3 * D, cw[:], D, relu_bias)

            def both(dve, tiles, prod):
                nc.vector.tensor_tensor(row[:, tiles, 0:D], prod[:, :, 0:D], over(fb[:, 0:D], 1, [P, G7, D]), ALU.add)
                nc.vector.tensor_tensor(aux[:, tiles, :], prod[:, :, D:2 * D], over(fb[:, D:2 * D], 1, [P, G7, D]), ALU.add)
            node_product(hc, D, fw[:], 2 * D, both)
            scatter_rows(table, row, W)

            def empty_state(dve):
                nc.vector.memset(agg[:], 0.0)
                nc.vector.memset(mx[:], BIG / 10)
            on_vector(empty_state)

            def additive(dve, h, mine, wp, lg, valid):
                e = wp[:, :, 0:D]
                nc.vector.tensor_tensor(e, g[:, h, :, 0:D], mine, ALU.add)
                dve.drain()
                nc.vector.scalar_tensor_tensor(e, e, 0.2, e, ALU.mult, ALU.max)
                dve.drain()
                nc.vector.tensor_tensor(e, e, over(att[:], 1, [P, U, D]), ALU.mult)
                dve.drain()
                nc.vector.tensor_reduce(lg, e, axis=AX.X, op=ALU.add)
                dve.drain()
                masked(dve, lg, valid, -1.0)
            gather_attend(additive)

            def attended(dve):
                nc.vector.tensor_scalar(small[:, 2], agg[:, :, D], 0.0, None, ALU.is_equal)
                dve.drain()
                nc.vector.tensor_tensor(small[:, 2], small[:, 2], agg[:, :, D], ALU.add)
                dve.drain()
                nc.vector.reciprocal(small[:, 3], small[:, 2])
                dve.drain()
                nc.vector.tensor_tensor(scratch, agg[:, :, 0:D], over(small[:, 3], 2, [P, NT, D]), ALU.mult)
                dve.drain()
                nc.vector.tensor_tensor(scratch, scratch, x[:], ALU.add)
            layer_norm(attended)

        with ExitStack() as st:
            s2 = lambda n, sh, dt=F32: st.enter_context(sbuf(nc, n, sh, dt))
            win_ = s2("w_in", [2 * D, MH])
            bin_ = s2("b_in", [P, MH])
            wout = s2("w_out", [MH, 2 * D])
            bout = s2("b_out", [P, D])
            hid = s2("hid", [P, NT, MH])
            with phase(nc, "weights_loaded") as (weights_loaded,), nc.Block() as block:
                @block.sync
                def _(sp):
                    spread = lambda a, n: a.rearrange("(a b) -> a b", a=1).broadcast_to([P, n])
                    sp.dma_start(win_[0:D, :], A["W_l_in_T"]).then_inc(weights_loaded, 16)
                    sp.dma_start(win_[D:2 * D, :], A["W_r_in_T"]).then_inc(weights_loaded, 16)
                    sp.dma_start(bin_[:], spread(A["b_l_in"], MH)).then_inc(weights_loaded, 16)
                    sp.dma_start(wout[:, 0:D], A["W_l_out_T"]).then_inc(weights_loaded, 16)
                    sp.dma_start(wout[:, D:2 * D], A["W_r_out_T"]).then_inc(weights_loaded, 16)
                    sp.dma_start(bout[:], spread(A["b_l_out"], D)).then_inc(weights_loaded, 16)
                    sp.wait_ge(weights_loaded, 16 * 6)
            on_vector(lambda dve: nc.vector.tensor_copy(row[:, :, 0:D], x[:]))
            scatter_rows(table, row, W)
            gather_sum()
            ax = big[:, 0:NT * 2 * D].rearrange("p (t f) -> p t f", f=2 * D)

            def beside(dve):
                nc.vector.tensor_copy(ax[:, :, 0:D], agg[:, :, 0:D])
                nc.vector.tensor_copy(ax[:, :, D:2 * D], x[:])
            on_vector(beside)

            def relu_in(dve, tiles, prod):
                nc.vector.tensor_tensor(hid[:, tiles, :], prod, over(bin_[:], 1, [P, G7, MH]), ALU.add)
                dve.drain()
                nc.vector.tensor_scalar(hid[:, tiles, :], hid[:, tiles, :], 0.0, None, ALU.max)
            node_product(ax, 2 * D, win_[:], MH, relu_in)

            def outs(dve, tiles, prod):
                nc.vector.tensor_copy(row[:, tiles, 0:D], prod[:, :, 0:D])
                nc.vector.tensor_tensor(aux[:, tiles, :], prod[:, :, D:2 * D], over(bout[:], 1, [P, G7, D]), ALU.add)
            node_product(hid, MH, wout[:], 2 * D, outs)
            scatter_rows(table, row, W)
            gather_sum()

            def last_sum(dve):
                nc.vector.tensor_tensor(scratch, agg[:, :, 0:D], aux[:], ALU.add)
                dve.drain()
                nc.vector.tensor_tensor(scratch, scratch, x[:], ALU.add)
            layer_norm(last_sum)
        scatter_rows(out, x, D, bound=N - 1)


def edge_messages(nc, v):
    tally, g, rec, agg, iota16, attw, ident = (v[k] for k in ("tally", "g", "rec", "agg", "iota16", "attw", "ident"))
    w1, w2, b1, ht = v["w1"], v["w2"], v["b1"], v["ht"]
    groups, load_record, gather_unit, wait_rows = (v[k] for k in ("groups", "load_record", "gather_unit", "wait_rows"))
    S = U // 4
    w2f = w2[:].rearrange("h k c -> h (k c)")
    with ExitStack() as st:
        s2 = lambda n, sh, dt=F32: st.enter_context(sbuf(nc, n, sh, dt))
        ea = s2("ea", [P, B, U, AW])
        valid = s2("valid", [P, U])
        sh = s2("sh", [P, U, 4])
        zz = s2("zz", [P, U, 24])
        v0 = s2("v0", [P, 3, U, 8])
        vm = s2("vm", [P, U, 8, 3])
        et = s2("et", [D, 2, 512])
        p1 = s2("p1", [P, 4, 24, 8])
        p2 = s2("p2", [P, 3, 32, 8])
        t1 = s2("t1", [P, U, 8])
        tm = s2("tm", [P, 3, U, 8])
        part = s2("part", [P, S + 1, D])
        red = s2("red", [P, D])
        etp = st.enter_context(psum(nc, "etp", [D, 2, 512], F32))
        hps = st.enter_context(psum(nc, "hps", [MH, 2, 512], F32))
        wps = st.enter_context(psum(nc, "wps", [P, 2, 4, 256], F32))
        names = v["NAMES"] + [f"attr{b}" for b in range(B)] + \
            ["turned", "turned_copied", "hidden", "hidden_relu", "weights", "weights_used"]
        with phase(nc, *names) as sem, nc.Block() as block:
            full, used, got, attr = (sem[B * k:B * (k + 1)] for k in range(4))
            turned, turned_copied, hidden, hidden_relu, weights, weights_used = sem[4 * B:]

            @block.sync
            def _(sp):
                with sp.Fori(0, groups(sp)) as it:
                    for h in range(B):
                        load_record(sp, it, h, full[h], used[h])

            @block.gpsimd
            def _(pool):
                with pool.Fori(0, groups(pool)) as it:
                    for h in range(B):
                        pool.wait_ge(full[h], 16 * (it + 1))
                        pool.sem_inc(tally, 1)
                        nc.gpsimd.indirect_dma_start(out=ea[:, h].rearrange("p a b -> p (a b)"), out_offset=None, in_=attw,
                                                     in_offset=bass.IndirectOffsetOnAxis(ap=rec[:, h, R_BASE:R_BASE + 1], axis=0)).then_inc(attr[h], 16)
                        gather_unit(pool, it, h, full[h], got[h])

            @block.tensor
            def _(pe):
                def turn(nk, h, s, n):
                    with pe.If(nk > 4 * s):
                        pe.wait_ge(turned_copied, n + 1)
                        pe.sem_inc(tally, 1)
                        for c in range(4):
                            last = nc.tensor.transpose(etp[:, s % 2, c * P:(c + 1) * P], ea[:, h, 4 * s + c, 0:D], ident[:])
                        last.then_inc(turned, 1)
                    with pe.Else():
                        pe.drain().then_inc(turned, 1)

                def hide(nk, s, n):
                    with pe.If(nk > 4 * s):
                        pe.wait_ge(turned_copied, n + 3)
                        pe.wait_ge(hidden_relu, n + 1)
                        nc.tensor.matmul(hps[:, s % 2], w1[:], et[:, s % 2], start=True, stop=True).then_inc(hidden, 1)
                    with pe.Else():
                        pe.drain().then_inc(hidden, 1)

                def weigh(nk, s, n):
                    with pe.If(nk > 4 * s):
                        pe.wait_ge(hidden_relu, n + 3)
                        pe.wait_ge(weights_used, n + 1)
                        for c in range(4):
                            last = nc.tensor.matmul(wps[:, s % 2, c], ht[:, s, c * P:(c + 1) * P], w2f, start=True, stop=True)
                        last.then_inc(weights, 1)
                    with pe.Else():
                        pe.drain().then_inc(weights, 1)

                pe.sem_inc(hidden, 2)
                pe.sem_inc(weights, 4)
                with pe.Fori(0, groups(pe)) as it:
                    for h in range(B):
                        pe.wait_ge(attr[h], 16 * (it + 1))
                        pe.sem_inc(tally, 1)
                        nk = pe.value_load(rec[0:1, h, R_NK:R_NK + 1], min_val=0, max_val=U)
                        n = S * (B * it + h)
                        turn(nk, h, 0, n)
                        for s in range(1, S):
                            turn(nk, h, s, n + s)
                            hide(nk, s - 1, n + s - 1)
                        hide(nk, S - 1, n + S - 1)
                        for s in range(S):
                            weigh(nk, s, n + s)

            @block.scalar
            def _(act):
                def copy(nk, s, n):
                    act.wait_ge(turned, n + 1)
                    act.wait_ge(hidden, n + 1)
                    act.sem_inc(tally, 1)
                    with act.If(nk > 4 * s):
                        nc.scalar.copy(et[:, s % 2], etp[:, s % 2]).then_inc(turned_copied, 1)
                    with act.Else():
                        act.drain().then_inc(turned_copied, 1)

                def relu(nk, s, n):
                    act.wait_ge(hidden, n + 3)
                    act.wait_ge(weights, n + 1)
                    act.sem_inc(tally, 1)
                    with act.If(nk > 4 * s):
                        nc.scalar.activation(ht[0:MH, s], hps[:, s % 2], ACT.Relu, bias=b1[:, 0:1]).then_inc(hidden_relu, 1)
                    with act.Else():
                        act.drain().then_inc(hidden_relu, 1)

                act.sem_inc(turned_copied, 2)
                act.sem_inc(hidden_relu, 2)
                with act.Fori(0, groups(act)) as it:
                    for h in range(B):
                        act.wait_ge(full[h], 16 * (it + 1))
                        act.sem_inc(tally, 1)
                        nk = act.value_load(rec[0:1, h, R_NK:R_NK + 1], min_val=0, max_val=U)
                        n = S * (B * it + h)
                        copy(nk, 0, n)
                        for s in range(1, S):
                            copy(nk, s, n + s)
                            relu(nk, s - 1, n + s - 1)
                        relu(nk, S - 1, n + S - 1)

            @block.vector
            def _(dve):
                nc.vector.memset(agg[:], 0.0)
                nc.vector.memset(t1[:], 0.0)
                dve.drain()
                total = [dve.alloc_register(unique(nc, f"rows{h}")) for h in range(B)]
                for h in range(B):
                    dve.reg_mov(total[h], 0)
                    dve.sem_inc(used[h], 1)
                dve.sem_inc(weights_used, 2)
                with dve.Fori(0, groups(dve)) as it:
                    for h in range(B):
                        t = wait_rows(dve, h, it, full[h], got[h], total)
                        nk = dve.value_load(rec[0:1, h, R_NK:R_NK + 1], min_val=0, max_val=U)
                        nc.vector.tensor_scalar(valid[:], iota16[:], rec[:, h, R_NV:R_NV + 1].bitcast(F32), None, ALU.is_lt)
                        dve.wait_ge(attr[h], 16 * (it + 1))
                        dve.sem_inc(tally, 1)
                        dve.drain()
                        nc.vector.tensor_tensor(sh[:], ea[:, h, :, D:D + 4], over(valid[:], 2, [P, U, 4]), ALU.mult)
                        nc.vector.tensor_copy(zz[:, :, 16:24], g[:, h, :, 0:8])
                        nc.vector.memset(part[:], 0.0)
                        dve.drain()
                        vec = g[:, h, :, 8:D].rearrange("p c (i m) -> p c i m", m=3)
                        nc.vector.tensor_tensor(vm[:], vec, over(sh[:, :, 1:4], 2, [P, U, 8, 3]), ALU.mult)
                        nc.vector.tensor_tensor(v0[:].rearrange("p m c i -> p c i m"), vec,
                                                sh[:, :, 0:1].unsqueeze(3).broadcast_to([P, U, 8, 3]), ALU.mult)
                        nc.vector.tensor_tensor(zz[:, :, 0:8], g[:, h, :, 0:8], over(sh[:, :, 0], 2, [P, U, 8]), ALU.mult)
                        dve.drain()
                        nc.vector.tensor_reduce(zz[:, :, 8:16], vm[:], axis=AX.X, op=ALU.add)
                        dve.drain()
                        for s in range(S):
                            n = S * (B * it + h) + s
                            dve.wait_ge(weights, n + 5)
                            dve.sem_inc(tally, 1)
                            with dve.If(nk > 4 * s):
                                c4 = slice(4 * s, 4 * s + 4)
                                nc.vector.tensor_tensor(p1[:], wps[:, s % 2, :, 0:192].rearrange("p c (r o) -> p c r o", o=8),
                                                        over(zz[:, c4], 3, [P, 4, 24, 8]), ALU.mult)
                                for m in range(3):
                                    nc.vector.tensor_tensor(p2[:, m].rearrange("p (c i) o -> p c i o", c=4),
                                                            wps[:, s % 2, :, 192:256].rearrange("p c (i o) -> p c i o", o=8),
                                                            over(v0[:, m, c4], 3, [P, 4, 8, 8]), ALU.mult)
                                dve.drain().then_inc(weights_used, 1)
                                nc.vector.tensor_reduce(part[:, s, 0:8], p1[:, :, 0:16].rearrange("p c r o -> p o c r"), axis=AX.XY, op=ALU.add)
                                nc.vector.tensor_reduce(t1[:, c4], p1[:, :, 16:24].rearrange("p c i o -> p c o i"), axis=AX.X, op=ALU.add)
                                nc.vector.tensor_reduce(part[:, s, 8:D].rearrange("p (m o) -> p m o", m=3),
                                                        p2[:].rearrange("p m r o -> p m o r"), axis=AX.X, op=ALU.add)
                                dve.drain()
                            with dve.Else():
                                dve.drain().then_inc(weights_used, 1)
                        dve.drain()
                        for m in range(3):
                            nc.vector.tensor_tensor(tm[:, m], t1[:], over(sh[:, :, 1 + m], 2, [P, U, 8]), ALU.mult)
                        dve.drain()
                        nc.vector.tensor_reduce(part[:, S, 8:D].rearrange("p (m o) -> p m o", m=3),
                                                tm[:].rearrange("p m c o -> p m o c"), axis=AX.X, op=ALU.add)
                        dve.drain()
                        nc.vector.tensor_reduce(red[:], part[:].rearrange("p s f -> p f s"), axis=AX.X, op=ALU.add)
                        dve.drain()
                        own = agg[:, bass.ds(t, 1), 0:D].rearrange("p a f -> p (a f)")
                        nc.vector.tensor_tensor(own, own, red[:], ALU.add)
                        dve.drain().then_inc(used[h], 1)
                for h in range(B):
                    dve.free_register(total[h])


_PLAIN = {
    "x": "x", "src": "src", "dst": "dst", "W1": "L1_gnn_W1", "b1": "L1_gnn_b1", "W2": "L1_gnn_W2", "b2": "L1_gnn_b2",
    "si_w0": "L1_gnn_si_w0", "si_w1": "L1_gnn_si_w1", "lambda_max": "L2_gnn_lambda_max", "cheb_W": "L2_gnn_cheb_W",
    "cheb_b": "L2_gnn_cheb_b", "src_W": "L2_gnn_src_W", "src_b": "L2_gnn_src_b", "dst_W": "L2_gnn_dst_W",
    "dst_b": "L2_gnn_dst_b", "attn": "L2_gnn_attn", "b_l_in": "L3_gnn_b_l_in", "b_l_out": "L3_gnn_b_l_out",
}
_TURNED = {"W_l_in_T": "L3_gnn_W_l_in", "W_r_in_T": "L3_gnn_W_r_in", "W_l_out_T": "L3_gnn_W_l_out", "W_r_out_T": "L3_gnn_W_r_out"}


def kernel(**inputs):
    import numpy as np
    import concourse.bacc as bacc
    from concourse.bass_utils import run_bass_kernel_spmd

    arrays = {name: np.ascontiguousarray(inputs[of]) for name, of in _PLAIN.items()}
    arrays |= {name: np.ascontiguousarray(np.asarray(inputs[of]).T) for name, of in _TURNED.items()}
    arrays["betas"] = np.concatenate([np.asarray(inputs[f"L0_gnn_beta{i}"]) for i in (1, 2, 3)])
    arrays["attr"] = np.concatenate([np.asarray(inputs["edge_attr_32"]), np.asarray(inputs["edge_attr_4"])], axis=1)

    nc = bacc.Bacc("TRN2", target_bir_lowering=False, num_devices=1)
    aps = {n: nc.dram_tensor(f"in_{n}", a.shape, mybir.dt.from_np(a.dtype), kind="ExternalInput").ap() for n, a in arrays.items()}
    out = nc.dram_tensor("out_x", (N, D), F32, kind="ExternalOutput").ap()
    build(nc, aps, out)
    r = run_bass_kernel_spmd(nc, [{f"in_{n}": a for n, a in arrays.items()}], core_ids=[0])
    return r.results[0]["out_x"]
```

```python
import concourse.bass as bass
from concourse import mybir
from contextlib import ExitStack, contextmanager
from itertools import count

F32 = mybir.dt.float32
BF16 = mybir.dt.bfloat16
I32 = mybir.dt.int32
ALU = mybir.AluOpType
ACT = mybir.ActivationFunctionType
AX = mybir.AxisListType

P = 128
N = 12500
E = 200000
D = 32
NT = (N + P - 1) // P
NP = NT * P
EP, EC = 125, E // 125
U = 16
B = 4
ONE, RN, PLACE, ID, W = D, D + 1, D + 2, D + 3, D + 4
SPLIT = 48
MAXU = NT + E // U + 6
AW = 36
R_BASE, R_NV, R_TILE, R_NK, RW = 16, 17, 18, 19, 20
BR = 8
BIG = 1e30
G7, NG = 7, NT // 7
EPS_LN = 1e-5
EPS_NORM = 1e-12
MH = 64


def unique(nc, name):
    return f"{name}_{next(_names)}"


_names = count()


def sbuf(nc, name, shape, dt):
    return nc.sbuf_tensor(unique(nc, name), shape, dt)


def psum(nc, name, shape, dt):
    return nc.psum_tensor(unique(nc, name), shape, dt)


@contextmanager
def phase(nc, *names):
    with ExitStack() as stack:
        sems = [stack.enter_context(nc.semaphore(unique(nc, n))) for n in names]
        yield sems
        if sems:
            nums = sorted(s.num for s in sems)
            while nums:
                run = 1
                while run < len(nums) and nums[run] == nums[0] + run:
                    run += 1
                nc.gpsimd.dma_reset(range(nums[0], nums[0] + run))
                nc.gpsimd.sem_clear(range(nums[0], nums[0] + run))
                nums = nums[run:]
            nc.all_engine_barrier()


def over(ap, n, shape):
    return ap.unsqueeze(n).broadcast_to(shape)


def build(nc, A, out):
    ctx = ExitStack()
    with ctx:
        def sb(name, shape, dt=F32):
            return ctx.enter_context(sbuf(nc, name, shape, dt))

        def dram(name, shape, dt):
            return nc.dram_tensor(name, shape, dt, kind="Internal").ap()

        table = dram("table", (NP, W), F32)
        order = dram("order", (NP, 4), I32)
        srcw = dram("srcw", (E + U, 1), I32)
        attw = dram("attw", (E + U, AW), F32)
        recs = dram("recs", (MAXU, P, RW), I32)

        ident = sb("ident", [P, P])
        tri = sb("tri", [P, P])
        onesq = sb("onesq", [P, P])
        iota16 = sb("iota16", [P, U])
        nid = sb("nid", [P, NT], I32)
        degf = sb("degf", [P, NT])
        startf = sb("startf", [P, NT])
        kmax = sb("kmax", [P, NT])
        place = sb("place", [P, NT], I32)
        tcol = sb("tcol", [P, NT], I32)
        ulim = sb("ulim", [P, NT + 1], I32)
        ulimf = sb("ulimf", [P, NT + 1])
        ucnt = sb("ucnt", [P, 2], I32)
        x = sb("x", [P, NT, D])
        row = sb("row", [P, NT, W])
        agg = sb("agg", [P, NT, D + 1])
        aux = sb("aux", [P, NT, D])
        mx = sb("mx", [P, NT])
        small = sb("small", [P, 6, NT])
        g = sb("g", [P, B, U, W])
        rec = sb("rec", [P, B, RW], I32)
        rs = sb("rs", [P, 2, G7, W])
        big = sb("big", [P, NT * 96])
        negbeta = sb("negbeta", [P, 3])
        selfw = sb("selfw", [D, D])
        w1 = sb("w1", [P, 2, P])
        w2 = sb("w2", [P, 4, 64])
        b1 = sb("b1", [P, 1])
        b2 = sb("b2", [3, 4, 64])
        b2b = sb("b2b", [3, 3, 4 * 64], BF16)
        b2s = sb("b2s", [3, 2, 4 * 64], BF16)
        b2t = sb("b2t", [3, 3, 4 * 64])
        ones3 = sb("ones3", [3, P], BF16)
        cw = sb("cw", [3 * D, D])
        cb = sb("cb", [P, D])
        fw = sb("fw", [D, 2 * D])
        fb = sb("fb", [P, 2 * D])
        att = sb("att", [P, D])
        win_ = sb("w_in", [2 * D, MH])
        bin_ = sb("b_in", [P, MH])
        wout = sb("w_out", [MH, 2 * D])
        bout = sb("b_out", [P, D])
        WEIGHT_LOADS = 1 + 24 + 4 + 2 * 5 + 4 + 8 + 6
        tally = ctx.enter_context(nc.semaphore("tally"))
        s_attr = ctx.enter_context(nc.semaphore("attributes_copied"))

        def make_constants():
            with phase(nc, "iota_done", "const_loaded") as (iota_done, const_loaded), \
                    sbuf(nc, "io", [P, P], I32) as io, sbuf(nc, "pc", [P, 1], I32) as pc, \
                    sbuf(nc, "iof", [P, P], F32) as iof, sbuf(nc, "pcf", [P, 1], F32) as pcf, \
                    sbuf(nc, "zero", [P, AW * U], F32) as zero, nc.Block() as block:
                @block.gpsimd
                def _(pool):
                    nc.gpsimd.iota(io[:], [[1, P]], base=0, channel_multiplier=0)
                    nc.gpsimd.iota(pc[:], [[0, 1]], base=0, channel_multiplier=1)
                    nc.gpsimd.iota(place[:], [[1, NT]], base=0, channel_multiplier=NT)
                    nc.gpsimd.iota(tcol[:], [[1, NT]], base=0, channel_multiplier=0)
                    pool.drain().then_inc(iota_done, 1)

                @block.vector
                def _(dve):
                    nc.vector.memset(onesq[:], 1.0)
                    nc.vector.memset(g[:], 0.0)
                    nc.vector.memset(row[:], 0.0)
                    nc.vector.memset(zero[:], 0.0)
                    nc.vector.memset(selfw[:], 0.0)
                    nc.vector.memset(w1[:], 0.0)
                    nc.vector.memset(ones3[:], 1.0)
                    dve.drain()
                    nc.vector.memset(row[:, :, ONE:ONE + 1], 1.0).then_inc(iota_done, 1)
                    dve.wait_ge(iota_done, 2)
                    nc.vector.tensor_copy(iof[:], io[:])
                    nc.vector.tensor_copy(pcf[:], pc[:])
                    dve.drain()
                    nc.vector.tensor_scalar(ident[:], iof[:], pcf[:, 0:1], None, ALU.is_equal)
                    nc.vector.tensor_scalar(tri[:], iof[:], pcf[:, 0:1], None, ALU.is_gt)
                    nc.vector.tensor_copy(iota16[:], iof[:, 0:U])
                    dve.wait_ge(const_loaded, 16 * 3)
                    nc.vector.tensor_scalar(negbeta[:], negbeta[:], -1.0, None, ALU.mult)

                @block.sync
                def _(sp):
                    sp.dma_start(negbeta[:], A["betas"].rearrange("(a b) -> a b", a=1).broadcast_to([P, 3])).then_inc(const_loaded, 16)
                    sp.wait_ge(iota_done, 2)
                    sp.dma_start(srcw[E:E + U, :].rearrange("a b -> b a"), zero[0:1, 0:U].bitcast(I32)).then_inc(const_loaded, 16)
                    sp.dma_start(attw[E:E + U, :].rearrange("(z a) b -> z (a b)", z=1), zero[0:1, 0:U * AW]).then_inc(const_loaded, 16)
                    sp.wait_ge(const_loaded, 16 * 3)

        def edges_by_target(unsorted, first, dst_i, hi, lo, iob):
            names = ("cut", "counted", "turned", "looked_up", "placed", "rows_loaded", "rows_left", "src_stored", "attr_stored", "copied")
            with ExitStack() as st:
                s2 = lambda n, sh, dt=F32: st.enter_context(sbuf(nc, n, sh, dt))
                ps = lambda n, sh, dt=F32: st.enter_context(psum(nc, n, sh, dt))
                free = s2("free", [NT, P])
                identb = s2("identb", [P, P], BF16)
                before = s2("before", [EP, EP])
                col = s2("col", [EP, 3])
                oh_hi = s2("oh_hi", [EP, NT], BF16)
                oh_lo = s2("oh_lo", [EP, P], BF16)
                diag = s2("diag", [EP, EP])
                hi_t = s2("hi_t", [NT, EP])
                sel = s2("sel", [EP, P])
                same = s2("same", [EP, EP])
                place = s2("place", [EP, 2])
                place_i = s2("place_i", [EP, 1], I32)
                src_all = s2("src_all", [EP, EC], I32)
                src_col = s2("src_col", [EP, 1], I32)
                rows = s2("rows", [EP, AW])
                ohtp = ps("ohtp", [NT, EP + 3], BF16)
                targets = ps("targets", [EP, EP])
                added = ps("added", [NT, P])
                found = ps("found", [EP, P])
                flag = lambda eng: eng.value_load(unsorted[0:1, 0:1], min_val=0, max_val=E)
                by_col = A["attr"].rearrange("(p c) f -> c p f", c=EC)
                with phase(nc, *names) as sem, nc.Block() as block:
                    cut, counted, turned, looked_up, placed, rows_loaded, rows_left, src_stored, attr_stored, copied = sem

                    @block.sync
                    def _(sp):
                        sp.dma_start(src_all[:], A["src"].rearrange("(p c) -> p c", c=EC)).then_inc(copied, 16)
                        sp.wait_ge(copied, 16)
                        with sp.If(flag(sp) > 0):
                            with sp.Fori(0, EC) as j:
                                sp.wait_ge(rows_left, j + 1)
                                sp.dma_start(rows[:], by_col[bass.ds(j, 1), :, :].rearrange("c p f -> p (c f)")).then_inc(rows_loaded, 16)
                            sp.wait_ge(rows_left, EC + 1)
                            sp.sem_inc(s_attr, 16)
                        with sp.Else():
                            sp.dma_start(srcw[0:E, :].rearrange("(p c) a -> p (c a)", p=EP), src_all[:]).then_inc(copied, 16)
                            sp.dma_start(attw[0:E, :].rearrange("(p c) b -> p (c b)", p=EP * 16),
                                         A["attr"].rearrange("(p c) b -> p (c b)", p=EP * 16)).then_inc(s_attr, 16)
                            sp.wait_ge(copied, 16 * 2)
                            sp.sem_inc(tally, 1)

                    @block.vector
                    def _(dve):
                        dve.wait_ge(copied, 16)
                        with dve.If(flag(dve) > 0):
                            nc.vector.tensor_copy(free[:], first[:])
                            nc.vector.tensor_copy(identb[:], ident[:])
                            nc.vector.tensor_tensor(before[:], tri[0:EP, 0:EP], ident[0:EP, 0:EP], ALU.add)
                            dve.drain()
                            nc.vector.tensor_scalar(before[:], before[:], -1.0, 1.0, ALU.mult, ALU.add)
                            dve.drain()
                            with dve.Fori(0, EC) as j:
                                nc.vector.tensor_copy(col[:, 0:1], hi[:, bass.ds(j, 1)])
                                nc.vector.tensor_copy(col[:, 1:2], lo[:, bass.ds(j, 1)])
                                nc.vector.tensor_copy(col[:, 2:3], dst_i[:, bass.ds(j, 1)])
                                nc.vector.tensor_copy(src_col[:], src_all[:, bass.ds(j, 1)])
                                dve.drain()
                                nc.vector.tensor_scalar(oh_hi[:], iob[0:EP, 0:NT], col[:, 0:1], None, ALU.is_equal)
                                nc.vector.tensor_scalar(oh_lo[:], iob[0:EP, :], col[:, 1:2], None, ALU.is_equal)
                                nc.vector.tensor_scalar(diag[:], ident[0:EP, 0:EP], col[:, 2:3], None, ALU.mult)
                                dve.drain().then_inc(cut, 1)
                                dve.wait_ge(counted, j + 1)
                                nc.vector.tensor_copy(hi_t[:], ohtp[:, 0:EP])
                                dve.drain().then_inc(turned, 1)
                                nc.vector.tensor_scalar(same[:], targets[:], col[:, 2:3], None, ALU.is_equal)
                                dve.drain()
                                nc.vector.tensor_tensor(same[:], same[:], before[:], ALU.mult)
                                dve.drain()
                                nc.vector.tensor_reduce(place[:, 0:1], same[:], axis=AX.X, op=ALU.add)
                                dve.wait_ge(looked_up, j + 1)
                                nc.vector.tensor_tensor(sel[:], found[:], oh_lo[:], ALU.mult)
                                dve.drain()
                                nc.vector.tensor_reduce(place[:, 1:2], sel[:], axis=AX.X, op=ALU.add)
                                nc.vector.tensor_tensor(free[:], free[:], added[:], ALU.add)
                                dve.drain()
                                nc.vector.tensor_tensor(place_i[:], place[:, 0:1], place[:, 1:2], ALU.add)
                                dve.drain().then_inc(placed, 1)
                                dve.wait_ge(rows_left, j + 2)
                                dve.sem_inc(tally, 1)
                        with dve.Else():
                            dve.drain()

                    @block.tensor
                    def _(pe):
                        with pe.If(flag(pe) > 0):
                            with pe.Fori(0, EC) as j:
                                pe.wait_ge(cut, j + 1)
                                nc.tensor.matmul(targets[:], onesq[0:EP, 0:EP], diag[:], start=True, stop=True)
                                nc.tensor.matmul(added[:], oh_hi[:], oh_lo[:], start=True, stop=True)
                                nc.tensor.transpose(ohtp[:, 0:EP], oh_hi[:], identb[0:EP, 0:EP]).then_inc(counted, 1)
                                pe.wait_ge(turned, j + 1)
                                nc.tensor.matmul(found[:], hi_t[:], free[:], start=True, stop=True).then_inc(looked_up, 1)
                        with pe.Else():
                            pe.drain()

                    @block.gpsimd
                    def _(pool):
                        with pool.If(flag(pool) > 0):
                            pool.sem_inc(rows_left, 1)
                            with pool.Fori(0, EC) as j:
                                pool.wait_ge(placed, j + 1)
                                pool.wait_ge(rows_loaded, 16 * (j + 1))
                                pool.sem_inc(tally, 1)
                                nc.gpsimd.indirect_dma_start(out=srcw, out_offset=bass.IndirectOffsetOnAxis(ap=place_i[:, 0:1], axis=0),
                                                             in_=src_col[:], in_offset=None).then_inc(src_stored, 16)
                                nc.gpsimd.indirect_dma_start(out=attw, out_offset=bass.IndirectOffsetOnAxis(ap=place_i[:, 0:1], axis=0),
                                                             in_=rows[:], in_offset=None).then_inc(attr_stored, 16)
                                pool.wait_ge(src_stored, 16 * (j + 1))
                                pool.wait_ge(attr_stored, 16 * (j + 1))
                                pool.sem_inc(rows_left, 1)
                        with pool.Else():
                            pool.drain()

        def load_weights(act, weights_loaded):
            act.dma_start(selfw[0:8, 0:8], A["si_w0"]).then_inc(weights_loaded, 16)
            for m in range(3):
                for i in range(8):
                    act.dma_start(selfw[8 + 3 * i + m:9 + 3 * i + m, 8 + 8 * m:16 + 8 * m], A["si_w1"][i:i + 1, :]).then_inc(weights_loaded, 16)
            for c in range(4):
                act.dma_start(w1[D * c:D * (c + 1), c % 2, MH * (c // 2):MH * (c // 2 + 1)], A["W1"]).then_inc(weights_loaded, 16)
            w2_in = A["W2"].rearrange("h (k c) -> h k c", k=4)
            b2_in = A["b2"].rearrange("(z k c) -> z k c", z=1, k=4)
            for half in range(2):
                rows = slice(MH * half, MH * (half + 1))
                act.dma_start(b1[rows], A["b1"].rearrange("(a b) -> a b", b=1)).then_inc(weights_loaded, 16)
                for k, of in enumerate((0, 3, 1, 2)):
                    act.dma_start(w2[rows, k], w2_in[:, of]).then_inc(weights_loaded, 16)
            for k, of in enumerate((0, 3, 1, 2)):
                act.dma_start(b2[:, k], b2_in[:, of].broadcast_to([3, 64])).then_inc(weights_loaded, 16)
            spread = lambda a, n: a.rearrange("(a b) -> a b", a=1).broadcast_to([P, n])
            for to, of in ((cw[:], A["cheb_W"]), (cb[:], spread(A["cheb_b"], D)), (fw[:, 0:D], A["src_W"]), (fw[:, D:2 * D], A["dst_W"]),
                           (fb[:, 0:D], spread(A["src_b"], D)), (fb[:, D:2 * D], spread(A["dst_b"], D)),
                           (att[:], A["attn"].broadcast_to([P, D])), (small[:, 5, 4:5], spread(A["lambda_max"], 1)),
                           (win_[0:D, :], A["W_l_in_T"]), (win_[D:2 * D, :], A["W_r_in_T"]), (bin_[:], spread(A["b_l_in"], MH)),
                           (wout[:, 0:D], A["W_l_out_T"]), (wout[:, D:2 * D], A["W_r_out_T"]), (bout[:], spread(A["b_l_out"], D))):
                act.dma_start(to, of).then_inc(weights_loaded, 16)

        def prepare_weights(dve):
            nc.vector.tensor_scalar(w2[:, 1], w2[:, 1], 1.0 / 3 ** 0.5, None, ALU.mult)
            nc.vector.tensor_scalar(b2[:, 1], b2[:, 1], 1.0 / 3 ** 0.5, None, ALU.mult)
            dve.drain()
            left = b2[:].rearrange("p k c -> p (k c)")
            for k in range(3):
                nc.vector.tensor_copy(b2b[:, k], left)
                dve.drain()
                nc.vector.tensor_tensor(left, left, b2b[:, k], ALU.subtract)
                nc.vector.tensor_scalar(b2t[:, k], b2b[:, k], ident[0:3, k:k + 1], None, ALU.mult)
                dve.drain()
            nc.vector.tensor_reduce(left, b2t[:].rearrange("p k c -> p c k"), axis=AX.X, op=ALU.add)
            dve.drain()
            nc.vector.tensor_copy(b2s[:], over(left, 1, [3, 2, 4 * 64]))

        def count_and_order():
            CH = 16
            pe_ctx = ExitStack()
            with pe_ctx:
                s = lambda n, sh, dt=F32: pe_ctx.enter_context(sbuf(nc, n, sh, dt))
                ps = lambda n, sh: pe_ctx.enter_context(psum(nc, n, sh, F32))
                dst_i = s("dst_i", [EP, EC], I32)
                next_i = s("next_i", [EP, EC], I32)
                part_i = s("part_i", [EP, EC], I32)
                falls = s("falls", [EP, 1])
                unsorted = s("unsorted", [P, 1], I32)
                hi = s("hi", [EP, EC], BF16)
                lo = s("lo", [EP, EC], BF16)
                iob = s("iob", [P, P], BF16)
                ioi = s("ioi", [P, P], I32)
                iobs = big[0:EP, 0:P * CH // 2].bitcast(BF16).rearrange("p (n c) -> p n c", c=CH)
                ohh = s("ohh", [EP, 2, NT, CH], BF16)
                ohl = s("ohl", [EP, 2, P, CH], BF16)
                zb = s("zb", [EP, P], BF16)
                hist = ps("hist", [NT, P])
                with phase(nc, "dst_loaded", "onehot", "used", "hist_zero", "iota_ready", "weights_loaded") as \
                        (dst_loaded, onehot, used, hist_zero, iota_ready, weights_loaded), nc.Block() as block:
                    @block.scalar
                    def _(act):
                        load_weights(act, weights_loaded)

                    @block.sync
                    def _(sp):
                        sp.dma_start(dst_i[:], A["dst"].rearrange("(p c) -> p c", c=EC)).then_inc(dst_loaded, 16)
                        sp.dma_start(next_i[0:EP - 1, :], A["dst"][1:1 + (EP - 1) * EC].rearrange("(p c) -> p c", c=EC)).then_inc(dst_loaded, 16)
                        sp.dma_start(next_i[EP - 1:EP, 0:EC - 1], A["dst"][E - EC + 1:E].rearrange("(p c) -> p c", p=1)).then_inc(dst_loaded, 16)
                        sp.dma_start(next_i[EP - 1:EP, EC - 1:EC], A["dst"][E - 1:E].rearrange("(p c) -> p c", p=1)).then_inc(dst_loaded, 16)

                    @block.gpsimd
                    def _(pool):
                        nc.gpsimd.iota(ioi[:], [[1, P]], base=0, channel_multiplier=0).then_inc(iota_ready, 1)

                    @block.vector
                    def _(dve):
                        nc.vector.memset(zb[:], 0.0).then_inc(hist_zero, 1)
                        dve.wait_ge(iota_ready, 1)
                        nc.vector.tensor_copy(iob[:], ioi[:])
                        nc.vector.tensor_copy(iobs, over(ioi[0:EP, :], 2, [EP, P, CH]))
                        dve.wait_ge(dst_loaded, 16 * 4)
                        nc.vector.tensor_tensor(part_i[:], next_i[:], dst_i[:], ALU.is_lt)
                        dve.drain()
                        nc.vector.tensor_reduce(falls[:], part_i[:], axis=AX.X, op=ALU.add)
                        dve.drain()
                        nc.vector.tensor_scalar(part_i[:], dst_i[:], 7, None, ALU.logical_shift_right)
                        dve.drain()
                        nc.vector.tensor_copy(hi[:], part_i[:])
                        dve.drain()
                        nc.vector.tensor_scalar(part_i[:], dst_i[:], P - 1, None, ALU.bitwise_and)
                        dve.drain()
                        nc.vector.tensor_copy(lo[:], part_i[:])
                        dve.drain()
                        with dve.Fori(0, EC // (2 * CH)) as it:
                            for h in range(2):
                                dve.wait_ge(used, 2 * it + h + 1)
                                dve.sem_inc(tally, 1)
                                c0 = (2 * it + h) * CH
                                nc.vector.tensor_tensor(ohh[:, h], iobs[:, 0:NT],
                                                        over(hi[:, bass.ds(c0, CH)], 1, [EP, NT, CH]), ALU.is_equal)
                                nc.vector.tensor_tensor(ohl[:, h], iobs,
                                                        over(lo[:, bass.ds(c0, CH)], 1, [EP, P, CH]), ALU.is_equal)
                                dve.drain().then_inc(onehot, 1)
                        dve.wait_ge(weights_loaded, 16 * WEIGHT_LOADS)
                        prepare_weights(dve)

                    @block.tensor
                    def _(pe):
                        pe.wait_ge(hist_zero, 1)
                        nc.tensor.matmul(hist[:], zb[:, 0:NT], zb[:], start=True, stop=False)
                        pe.drain().then_inc(used, 2)
                        with pe.Fori(0, EC // (2 * CH)) as it:
                            for h in range(2):
                                pe.wait_ge(onehot, 2 * it + h + 1)
                                pe.sem_inc(tally, 1)
                                for c in range(CH):
                                    last = nc.tensor.matmul(hist[:], ohh[:, h, :, c], ohl[:, h, :, c], start=False, stop=False)
                                last.then_inc(used, 1)
                        nc.tensor.matmul(hist[:], zb[:, 0:NT], zb[:], start=False, stop=True)

                with ExitStack() as st:
                    s2 = lambda n, sh, dt=F32: st.enter_context(sbuf(nc, n, sh, dt))
                    deg = s2("deg", [NT, P])
                    first = s2("first", [NT, P])
                    z1 = s2("z1", [NT, 1])
                    cls = s2("cls", [NT, P])
                    oh = big[0:NT, 0:SPLIT * P].rearrange("p (b l) -> p b l", b=SPLIT)
                    cum = s2("cum", [NT, SPLIT, P])
                    cnt = s2("cnt", [NT, SPLIT + 1])
                    rowx = s2("rowx", [NT, SPLIT])
                    base = s2("base", [NT, SPLIT])
                    tot = s2("tot", [NT, SPLIT])
                    pos = s2("pos", [NT, P])
                    posi = s2("posi", [NT, P], I32)
                    ent = s2("ent", [NT, P, 4], I32)
                    iocl = s2("iocl", [NT, SPLIT])
                    pfx = st.enter_context(psum(nc, "pfx", [NT, SPLIT + 1], F32))
                    tots = st.enter_context(psum(nc, "tots", [NT, SPLIT], F32))
                    falling = st.enter_context(psum(nc, "falling", [P, 1], F32))
                    with phase(nc, "counted", "summed", "node_iota") as (counted, summed, node_iota), nc.Block() as block:
                        @block.gpsimd
                        def _(pool):
                            nc.gpsimd.memset(ent[:], 0).then_inc(node_iota, 1)
                            pool.wait_ge(node_iota, 1)
                            nc.gpsimd.iota(ent[:, :, 0], [[1, P]], base=0, channel_multiplier=P).then_inc(node_iota, 1)

                        @block.vector
                        def _(dve):
                            nc.vector.tensor_copy(deg[:], hist[:])
                            nc.vector.memset(z1[:], 0.0)
                            nc.vector.tensor_copy(iocl[:], ioi[0:NT, 0:SPLIT])
                            dve.drain()
                            nc.vector.tensor_tensor_scan(first[:], deg[:], z1[:].broadcast_to([NT, P]), 0.0, ALU.add, ALU.add)
                            nc.vector.tensor_reduce(cnt[:, SPLIT:SPLIT + 1], deg[:], axis=AX.X, op=ALU.add)
                            nc.vector.tensor_scalar(cls[:], deg[:], float(SPLIT - 1), -1.0, ALU.min, ALU.mult)
                            dve.drain()
                            nc.vector.tensor_scalar(cls[:], cls[:], float(SPLIT - 1), None, ALU.add)
                            dve.drain()
                            nc.vector.tensor_tensor(oh, over(iocl[:], 2, [NT, SPLIT, P]), over(cls[:], 1, [NT, SPLIT, P]), ALU.is_equal)
                            dve.drain()
                            nc.vector.tensor_reduce(cnt[:, 0:SPLIT], oh, axis=AX.X, op=ALU.add)
                            nc.vector.tensor_tensor_scan(cum[:].rearrange("p b l -> p (b l)"), big[0:NT, 0:SPLIT * P],
                                                         z1[:].broadcast_to([NT, SPLIT * P]), 0.0, ALU.add, ALU.add)
                            dve.drain().then_inc(counted, 1)
                            nc.vector.tensor_tensor_scan(rowx[:], cnt[:, 0:SPLIT], z1[:].broadcast_to([NT, SPLIT]), 0.0, ALU.add, ALU.add)
                            dve.drain()
                            nc.vector.tensor_tensor(rowx[:], rowx[:], cnt[:, 0:SPLIT], ALU.subtract)
                            dve.wait_ge(summed, 1)
                            nc.vector.tensor_copy(tot[:], tots[:])
                            nc.vector.tensor_copy(unsorted[:], falling[:])
                            nc.vector.tensor_tensor(first[:], first[:], deg[:], ALU.subtract)
                            dve.drain()
                            nc.vector.tensor_scalar(first[:], first[:], pfx[:, SPLIT:SPLIT + 1], None, ALU.add)
                            nc.vector.tensor_tensor_scan(base[:], tot[:], z1[:].broadcast_to([NT, SPLIT]), 0.0, ALU.add, ALU.add)
                            dve.drain()
                            nc.vector.tensor_tensor(base[:], base[:], tot[:], ALU.subtract)
                            dve.drain()
                            nc.vector.tensor_tensor(base[:], base[:], pfx[:, 0:SPLIT], ALU.add)
                            dve.drain()
                            nc.vector.tensor_tensor(base[:], base[:], rowx[:], ALU.subtract)
                            dve.drain()
                            nc.vector.tensor_tensor(cum[:], cum[:], over(base[:], 2, [NT, SPLIT, P]), ALU.add)
                            dve.drain()
                            nc.vector.tensor_tensor(cum[:], cum[:], oh, ALU.mult)
                            dve.drain()
                            nc.vector.tensor_reduce(pos[:], cum[:].rearrange("p b l -> p l b"), axis=AX.X, op=ALU.add)
                            dve.wait_ge(node_iota, 2)
                            nc.vector.tensor_copy(ent[:, :, 1], first[:])
                            nc.vector.tensor_copy(ent[:, :, 2], deg[:])
                            dve.drain()
                            nc.vector.tensor_scalar(posi[:], pos[:], -1.0, None, ALU.add)

                        @block.tensor
                        def _(pe):
                            pe.wait_ge(counted, 1)
                            nc.tensor.matmul(pfx[:], tri[0:NT, 0:NT], cnt[:], start=True, stop=True)
                            nc.tensor.matmul(falling[:], onesq[0:EP, :], falls[:], start=True, stop=True)
                            nc.tensor.matmul(tots[:], onesq[0:NT, 0:NT], cnt[:, 0:SPLIT], start=True, stop=True).then_inc(summed, 1)

                    edges_by_target(unsorted, first, dst_i, hi, lo, iob)

                    C8 = 8
                    ix = s2("ix", [NT, 2, C8], I32)
                    en = s2("en", [NT, 2, C8 * 4], I32)
                    xn = big[0:NT, 0:P * D].rearrange("p (n f) -> p n f", f=D)
                    rown = big[0:NT, P * D:P * (D + W)].rearrange("p (n w) -> p n w", w=W)
                    whole = N // P
                    norm = s2("norm", [NT, 2, P])
                    rank = s2("rank", [NT, 2, P], I32)
                    rankf = s2("rankf", [NT, 3, P])
                    with phase(nc, "staged0", "staged1", "free0", "free1", "stored0", "stored1", "cleared", "x_loaded",
                               "squares", "roots", "rows_ready", "table_stored") as sem, nc.Block() as block:
                        staged, free, stored = sem[0:2], sem[2:4], sem[4:6]
                        cleared, x_loaded, squares, roots, rows_ready, table_stored = sem[6:]

                        @block.sync
                        def _(sp):
                            sp.wait_ge(cleared, 1)
                            sp.dma_start(xn[0:whole], A["x"][0:whole * P, :].rearrange("(t n) f -> t n f", n=P)).then_inc(x_loaded, 16)
                            sp.dma_start(xn[whole:NT, 0:N - whole * P], A["x"][whole * P:N, :].rearrange("(t n) f -> t n f", t=1)).then_inc(x_loaded, 16)
                            sp.wait_ge(rows_ready, 1)
                            sp.dma_start(table.rearrange("(t n) w -> t n w", n=P), rown).then_inc(table_stored, 16)
                            sp.wait_ge(table_stored, 16)

                        @block.vector
                        def _(dve):
                            nc.vector.memset(xn[:, N - whole * P:P], 0.0)
                            nc.vector.memset(rown[:, :, ONE:W], 1.0)
                            dve.drain().then_inc(cleared, 1)
                            nc.vector.tensor_scalar(rank[:, 0], posi[:], P - 1, None, ALU.bitwise_and)
                            nc.vector.tensor_scalar(rank[:, 1], posi[:], 7, None, ALU.logical_shift_right)
                            dve.drain()
                            nc.vector.tensor_copy(rankf[:, 0:2], rank[:])
                            dve.drain()
                            nc.vector.scalar_tensor_tensor(rankf[:, 2], rankf[:, 0], float(NT), rankf[:, 1], ALU.mult, ALU.add)
                            dve.drain()
                            nc.vector.tensor_copy(rown[:, :, PLACE].bitcast(I32), rankf[:, 2])
                            dve.wait_ge(x_loaded, 16 * 2)
                            nc.vector.tensor_copy(rown[:, :, 0:D], xn)
                            dve.drain()
                            nc.vector.tensor_tensor(xn, xn, xn, ALU.mult)
                            dve.drain()
                            nc.vector.tensor_reduce(norm[:, 0], xn, axis=AX.X, op=ALU.add)
                            dve.drain()
                            nc.vector.tensor_scalar(norm[:, 0], norm[:, 0], EPS_NORM ** 2 / 100, None, ALU.max)
                            dve.drain().then_inc(squares, 1)
                            dve.wait_ge(roots, 1)
                            nc.vector.tensor_scalar(norm[:, 0], norm[:, 1], EPS_NORM, None, ALU.max)
                            dve.drain()
                            nc.vector.reciprocal(norm[:, 1], norm[:, 0])
                            dve.drain()
                            nc.vector.tensor_copy(rown[:, :, RN], norm[:, 1]).then_inc(rows_ready, 1)

                        @block.scalar
                        def _(act):
                            with act.Fori(0, P // (2 * C8)) as it:
                                for h in range(2):
                                    act.wait_ge(free[h], it + 1)
                                    act.sem_inc(tally, 1)
                                    c0 = (2 * it + h) * C8
                                    nc.scalar.copy(ix[:, h], posi[:, bass.ds(c0, C8)]).then_inc(staged[h], 1)
                                    nc.scalar.copy(en[:, h], ent[:, bass.ds(c0, C8), :].rearrange("p a b -> p (a b)")).then_inc(staged[h], 1)
                            act.wait_ge(squares, 1)
                            nc.scalar.activation(norm[:, 1], norm[:, 0], ACT.Sqrt).then_inc(roots, 1)

                        @block.gpsimd
                        def _(pool):
                            for h in range(2):
                                pool.sem_inc(free[h], 1)
                            with pool.Fori(0, P // (2 * C8)) as it:
                                for h in range(2):
                                    pool.wait_ge(staged[h], 2 * it + 2)
                                    pool.sem_inc(tally, 1)
                                    for c in range(C8):
                                        nc.gpsimd.indirect_dma_start(
                                            out=order, out_offset=bass.IndirectOffsetOnAxis(ap=ix[:, h, c:c + 1], axis=0),
                                            in_=en[:, h, 4 * c:4 * c + 4], in_offset=None).then_inc(stored[h], 16)
                                for h in range(2):
                                    pool.wait_ge(stored[h], 16 * C8 * (it + 1))
                                    pool.sem_inc(tally, 1)
                                    pool.sem_inc(free[h], 1)

        def load_order():
            with ExitStack() as st:
                s2 = lambda n, sh, dt=F32: st.enter_context(sbuf(nc, n, sh, dt))
                ordt = s2("ordt", [P, NT, 4], I32)
                kcol = s2("kcol", [NT, 1])
                diag = s2("diag", [NT, NT])
                ki = s2("ki", [P, NT], I32)
                nu = s2("nu", [P, NT])
                uf = s2("uf", [P, NT + 1])
                z1 = s2("z1b", [P, 1])
                tps = st.enter_context(psum(nc, "tps", [NT, P], F32))
                kps = st.enter_context(psum(nc, "kps", [P, NT], F32))
                with phase(nc, "order_loaded", "deg_ready", "transposed", "diag_ready", "spread") as \
                        (order_loaded, deg_ready, transposed, diag_ready, spread), nc.Block() as block:
                    @block.sync
                    def _(sp):
                        sp.dma_start(ordt[:], order.rearrange("(t p) c -> p t c", p=P)).then_inc(order_loaded, 16)

                    @block.vector
                    def _(dve):
                        dve.wait_ge(order_loaded, 16)
                        nc.vector.tensor_copy(nid[:], ordt[:, :, 0])
                        nc.vector.tensor_copy(row[:, :, ID].bitcast(I32), ordt[:, :, 0])
                        nc.vector.tensor_copy(row[:, :, PLACE].bitcast(I32), place[:])
                        nc.vector.tensor_copy(startf[:], ordt[:, :, 1])
                        nc.vector.tensor_copy(degf[:], ordt[:, :, 2])
                        nc.vector.memset(z1[:], 0.0)
                        dve.drain().then_inc(deg_ready, 1)
                        dve.wait_ge(transposed, 1)
                        nc.vector.tensor_reduce(kcol[:], tps[:], axis=AX.X, op=ALU.max)
                        dve.drain()
                        nc.vector.tensor_scalar(diag[:], ident[0:NT, 0:NT], kcol[:, 0:1], None, ALU.mult).then_inc(diag_ready, 1)
                        dve.wait_ge(spread, 1)
                        nc.vector.tensor_copy(kmax[:], kps[:])
                        dve.drain()
                        nc.vector.tensor_scalar(ki[:], kmax[:], float(U - 1), None, ALU.add)
                        dve.drain()
                        nc.vector.tensor_scalar(ki[:], ki[:], 4, None, ALU.logical_shift_right)
                        dve.drain()
                        nc.vector.tensor_scalar(nu[:], ki[:], 1.0, None, ALU.max)
                        nc.vector.memset(uf[:, 0:1], 0.0)
                        dve.drain()
                        nc.vector.tensor_tensor_scan(uf[:, 1:NT + 1], nu[:], z1[:].broadcast_to([P, NT]), 0.0, ALU.add, ALU.add)
                        dve.drain()
                        nc.vector.tensor_copy(ulimf[:], uf[:])
                        nc.vector.tensor_scalar(ki[:, 0:1], uf[:, NT:NT + 1], float(B - 1), None, ALU.add)
                        nc.vector.tensor_scalar(ki[:, 1:2], uf[:, NT:NT + 1], float(BR - 1), float(NG * BR), ALU.add, ALU.max)
                        dve.drain()
                        nc.vector.memset(uf[:, NT:NT + 1], float(1 << 20))
                        nc.vector.tensor_scalar(ucnt[:, 0:1], ki[:, 0:1], B.bit_length() - 1, None, ALU.logical_shift_right)
                        nc.vector.tensor_scalar(ucnt[:, 1:2], ki[:, 1:2], BR.bit_length() - 1, None, ALU.logical_shift_right)
                        dve.drain()
                        nc.vector.tensor_copy(ulim[:], uf[:])

                    @block.tensor
                    def _(pe):
                        pe.wait_ge(deg_ready, 1)
                        nc.tensor.transpose(tps[:], degf[:], ident[:]).then_inc(transposed, 1)
                        pe.wait_ge(diag_ready, 1)
                        nc.tensor.matmul(kps[:], onesq[0:NT, :], diag[:], start=True, stop=True).then_inc(spread, 1)

        def groups(eng):
            return eng.value_load(ucnt[0:1, 0:1], min_val=1, max_val=MAXU // B)

        def record_groups(eng):
            return eng.value_load(ucnt[0:1, 1:2], min_val=NG, max_val=MAXU // BR)

        def write_records():
            with sbuf(nc, "ixs", [P, G7], I32) as ixs, sbuf(nc, "xs", [P, G7, D], F32) as xs, \
                    sbuf(nc, "k0", [P, BR], F32) as k0, sbuf(nc, "bi", [P, BR], I32) as bi, \
                    sbuf(nc, "win", [P, BR, U], I32) as win, sbuf(nc, "rb", [P, BR, RW], I32) as rb, \
                    sbuf(nc, "nv", [P, BR], F32) as nv, sbuf(nc, "nk", [P, BR], F32) as nk, \
                    sbuf(nc, "vd", [P, BR, U], F32) as vd, sbuf(nc, "uu", [P, BR], F32) as uu, \
                    phase(nc, "base_ready", "rec_ready", "rec_left", "rec_stored", "nodes_named", "nodes_got", *[f"win{b}" for b in range(BR)]) as sem, \
                    nc.Block() as block:
                base_ready, rec_ready, rec_left, rec_stored, nodes_named, nodes_got = sem[0:6]
                window = sem[6:]

                @block.vector
                def _(dve):
                    nc.vector.tensor_copy(uu[:], iota16[:, 0:BR])
                    tile = dve.alloc_register(unique(nc, "tile"))
                    dve.reg_mov(tile, 0)
                    dve.drain()
                    with dve.Fori(0, record_groups(dve)) as it:
                        ts = []
                        for b in range(BR):
                            last = dve.value_load(ulim[0:1, bass.ds(dve.snap(tile, min_val=0, max_val=NT - 1) + 1, 1)], min_val=0, max_val=1 << 20)
                            with dve.If(last == it * BR + b):
                                dve.reg_add(tile, tile, 1)
                            t = dve.snap(tile, min_val=0, max_val=NT - 1)
                            ts.append(t)
                            nc.vector.tensor_scalar(k0[:, b:b + 1], ulimf[:, bass.ds(t, 1)], uu[:, b:b + 1], -float(U), ALU.subtract, ALU.mult)
                        dve.drain()
                        nc.vector.tensor_scalar(uu[:], uu[:], float(BR), None, ALU.add)
                        for b, t in enumerate(ts):
                            nc.vector.tensor_scalar(bi[:, b:b + 1], startf[:, bass.ds(t, 1)], k0[:, b:b + 1], float(E), ALU.add, ALU.min)
                            dve.drain().then_inc(base_ready, 1)
                            nc.vector.tensor_tensor(nv[:, b:b + 1], degf[:, bass.ds(t, 1)], k0[:, b:b + 1], ALU.subtract)
                            nc.vector.tensor_scalar(nk[:, b:b + 1], kmax[:, bass.ds(t, 1)], k0[:, b:b + 1], float(U), ALU.subtract, ALU.min)
                        dve.wait_ge(rec_left, it + 1)
                        dve.sem_inc(tally, 1)
                        dve.drain()
                        for b, t in enumerate(ts):
                            nc.vector.tensor_copy(rb[:, b, R_TILE:R_TILE + 1], tcol[:, bass.ds(t, 1)])
                            nc.vector.tensor_scalar(vd[:, b], iota16[:], nv[:, b:b + 1], None, ALU.is_lt)
                        nc.vector.tensor_copy(rb[:, :, R_BASE], bi[:])
                        nc.vector.tensor_copy(rb[:, :, R_NV].bitcast(F32), nv[:])
                        nc.vector.tensor_scalar(rb[:, :, R_NK], nk[:], 1.0, None, ALU.max)
                        dve.drain()
                        for b in range(BR):
                            dve.wait_ge(window[b], 16 * (it + 1))
                            nc.vector.tensor_tensor(rb[:, b, 0:U], win[:, b], vd[:, b], ALU.mult)
                        dve.drain().then_inc(rec_ready, 1)
                    dve.free_register(tile)

                @block.gpsimd
                def _(pool):
                    with pool.Fori(0, record_groups(pool)) as it:
                        for b in range(BR):
                            pool.wait_ge(base_ready, BR * it + b + 1)
                            pool.sem_inc(tally, 1)
                            nc.gpsimd.indirect_dma_start(out=win[:, b], out_offset=None, in_=srcw,
                                                         in_offset=bass.IndirectOffsetOnAxis(ap=bi[:, b:b + 1], axis=0)).then_inc(window[b], 16)
                        with pool.If(it < NG):
                            pool.wait_ge(nodes_named, it + 1)
                            pool.sem_inc(tally, 1)
                            for c in range(G7):
                                nc.gpsimd.indirect_dma_start(out=xs[:, c], out_offset=None, in_=A["x"],
                                                             in_offset=bass.IndirectOffsetOnAxis(ap=ixs[:, c:c + 1], axis=0),
                                                             bounds_check=N - 1, oob_is_err=False).then_inc(nodes_got, 16)

                @block.scalar
                def _(act):
                    nc.scalar.copy(ixs[:], nid[:, 0:G7])
                    nc.scalar.activation(xs[:], row[:, 0:G7, 0:D], ACT.Copy, scale=0.0)
                    act.drain().then_inc(nodes_named, 1)
                    with act.Fori(0, NG - 1) as i:
                        act.wait_ge(nodes_got, 16 * G7 * (i + 1))
                        act.sem_inc(tally, 1)
                        nc.scalar.copy(x[:, bass.ds(i * G7, G7), :], xs[:])
                        nc.scalar.copy(ixs[:], nid[:, bass.ds((i + 1) * G7, G7)])
                        act.drain().then_inc(nodes_named, 1)
                    act.wait_ge(nodes_got, 16 * G7 * NG)
                    nc.scalar.copy(x[:, NT - G7:NT, :], xs[:])

                @block.sync
                def _(sp):
                    sp.sem_inc(rec_left, 1)
                    with sp.Fori(0, record_groups(sp)) as it:
                        sp.wait_ge(rec_ready, it + 1)
                        sp.dma_start(recs[bass.ds(it * BR, BR), :, :].rearrange("u p w -> p u w"), rb[:]).then_inc(rec_stored, 16)
                        sp.wait_ge(rec_stored, 16 * (it + 1))
                        sp.sem_inc(rec_left, 1)

        by_place = table.rearrange("(p t) w -> p t w", p=P)

        def scatter_rows(dest, width, bound=None):
            more = {} if bound is None else {"bounds_check": bound, "oob_is_err": False}
            with phase(nc, "staged0", "staged1", "stored0", "stored1") as sem, nc.Block() as block:
                staged, stored = sem[0:2], sem[2:4]

                @block.sync
                def _(sp):
                    for h in range(2):
                        sp.dma_start(rs[:, h], row[:, h * G7:(h + 1) * G7, :]).then_inc(staged[h], 16)
                    with sp.Fori(1, NG // 2) as it:
                        for h in range(2):
                            sp.wait_ge(stored[h], 16 * G7 * it)
                            sp.sem_inc(tally, 1)
                            sp.dma_start(rs[:, h], row[:, bass.ds((2 * it + h) * G7, G7), :]).then_inc(staged[h], 16)

                @block.gpsimd
                def _(pool):
                    with pool.Fori(0, NG // 2) as it:
                        for h in range(2):
                            pool.wait_ge(staged[h], 16 * (it + 1))
                            pool.sem_inc(tally, 1)
                            for c in range(G7):
                                nc.gpsimd.indirect_dma_start(
                                    out=dest, out_offset=bass.IndirectOffsetOnAxis(ap=rs[:, h, c, ID:ID + 1].bitcast(I32), axis=0),
                                    in_=rs[:, h, c, 0:width], in_offset=None, **more).then_inc(stored[h], 16)
                    for h in range(2):
                        pool.wait_ge(stored[h], 16 * G7 * (NG // 2))

        def store_table(beside=None):
            with phase(nc, "stored") as (stored,), nc.Block() as block:
                @block.sync
                def _(sp):
                    sp.dma_start(by_place, row[:]).then_inc(stored, 16)
                    sp.wait_ge(stored, 16)

                if beside is not None:
                    @block.vector
                    def _(dve):
                        beside(dve)

        NAMES = [f"{n}{b}" for n in ("full", "used", "got") for b in range(B)]

        def load_record(sp, it, h, full, used):
            sp.wait_ge(used, it + 1)
            sp.dma_start(rec[:, h], recs[bass.ds(B * it + h, 1), :, :].rearrange("a p w -> p (a w)")).then_inc(full, 16)

        def gather_unit(pool, it, h, full, got):
            pool.wait_ge(full, 16 * (it + 1))
            pool.sem_inc(tally, 1)
            nk = pool.value_load(rec[0:1, h, R_NK:R_NK + 1], min_val=0, max_val=U)
            for c in range(U):
                with pool.If(nk > c):
                    nc.gpsimd.indirect_dma_start(out=g[:, h, c], out_offset=None, in_=table,
                                                 in_offset=bass.IndirectOffsetOnAxis(ap=rec[:, h, c:c + 1], axis=0)).then_inc(got, 16)

        def wait_rows(eng, h, it, full, got, total):
            eng.wait_ge(full, 16 * (it + 1))
            eng.sem_inc(tally, 1)
            t = eng.value_load(rec[0:1, h, R_TILE:R_TILE + 1], min_val=0, max_val=NT - 1)
            nk = eng.value_load(rec[0:1, h, R_NK:R_NK + 1], min_val=0, max_val=U)
            eng.reg_add(total[h], total[h], nk)
            eng.wait_ge(got, eng.snap(total[h]) * 16)
            eng.sem_inc(tally, 1)
            return t

        def sum_rows(dve, values, keep, t, h, valid, wp, red, cols):
            nc.vector.tensor_tensor(wp[:, h, :, 0:cols], values[:, :, 0:cols], over(keep, 2, [P, U, cols]), ALU.mult)
            dve.drain()
            nc.vector.tensor_reduce(red[:, h, 0:cols], wp[:, h, :, 0:cols].rearrange("p c f -> p f c"), axis=AX.X, op=ALU.add)
            dve.drain()

        def root(act, squares, roots):
            act.wait_ge(squares, 1)
            nc.scalar.activation(small[:, 1], small[:, 0], ACT.Sqrt).then_inc(roots, 1)

        def gather_sum(then, after_root=None):
            with sbuf(nc, "valid", [P, B, U], F32) as valid, sbuf(nc, "wp", [P, B, U, D + 1], F32) as wp, \
                    sbuf(nc, "red", [P, B, D + 1], F32) as red, \
                    phase(nc, *NAMES, "squares", "roots") as sem, nc.Block() as block:
                full, used, got, squares, roots = sem[0:B], sem[B:2 * B], sem[2 * B:3 * B], sem[-2], sem[-1]

                @block.scalar
                def _(act):
                    if after_root is not None:
                        root(act, squares, roots)

                @block.sync
                def _(sp):
                    with sp.Fori(0, groups(sp)) as it:
                        for h in range(B):
                            load_record(sp, it, h, full[h], used[h])

                @block.gpsimd
                def _(pool):
                    with pool.Fori(0, groups(pool)) as it:
                        for h in range(B):
                            gather_unit(pool, it, h, full[h], got[h])

                @block.vector
                def _(dve):
                    nc.vector.memset(agg[:], 0.0)
                    dve.drain()
                    total = [dve.alloc_register(unique(nc, f"rows{h}")) for h in range(B)]
                    for h in range(B):
                        dve.reg_mov(total[h], 0)
                        dve.sem_inc(used[h], 1)
                    with dve.Fori(0, groups(dve)) as it:
                        for h in range(B):
                            t = wait_rows(dve, h, it, full[h], got[h], total)
                            nc.vector.tensor_scalar(valid[:, h], iota16[:], rec[:, h, R_NV:R_NV + 1].bitcast(F32), None, ALU.is_lt)
                            dve.drain()
                            sum_rows(dve, g[:, h], valid[:, h], t, h, valid, wp, red, D)
                            own = agg[:, bass.ds(t, 1), 0:D].rearrange("p a f -> p (a f)")
                            nc.vector.tensor_tensor(own, own, red[:, h, 0:D], ALU.add)
                            dve.drain().then_inc(used[h], 1)
                    for h in range(B):
                        dve.free_register(total[h])
                    then(dve)
                    if after_root is not None:
                        dve.drain().then_inc(squares, 1)
                        dve.wait_ge(roots, 1)
                        after_root(dve)

        def gather_attend(logits, then, after_root, place_sources=False):
            with sbuf(nc, "valid", [P, B, U], F32) as valid, sbuf(nc, "wp", [P, B, U, D + 1], F32) as wp, \
                    sbuf(nc, "red", [P, B, D + 1], F32) as red, sbuf(nc, "lg", [P, B, U], F32) as lg, \
                    sbuf(nc, "pr", [P, B, U], F32) as pr, sbuf(nc, "st", [P, B, 4], F32) as st, \
                    phase(nc, *NAMES, "logits", "exps", "squares", "roots",
                          *[f"rewritten{b}" for b in range(B)]) as sem, nc.Block() as block:
                full, used, got = sem[0:B], sem[B:2 * B], sem[2 * B:3 * B]
                logits_ready, exps_ready, squares, roots = sem[3 * B:3 * B + 4]
                rewritten = sem[3 * B + 4:]

                @block.sync
                def _(sp):
                    if place_sources:
                        count = groups(sp)
                        for h in range(B):
                            sp.wait_ge(used[h], 1)
                            sp.dma_start(rec[:, h], recs[h:h + 1, :, :].rearrange("a p w -> p (a w)")).then_inc(full[h], 16)
                        with sp.Fori(1, count) as it:
                            for h in range(B):
                                sp.wait_ge(used[h], it + 1)
                                sp.dma_start(recs[bass.ds(B * it - B + h, 1), :, :].rearrange("a p w -> p (a w)"), rec[:, h]).then_inc(rewritten[h], 16)
                                sp.wait_ge(rewritten[h], 16 * it)
                                sp.dma_start(rec[:, h], recs[bass.ds(B * it + h, 1), :, :].rearrange("a p w -> p (a w)")).then_inc(full[h], 16)
                        for h in range(B):
                            sp.wait_ge(used[h], count + 1)
                            sp.dma_start(recs[bass.ds(B * count - B + h, 1), :, :].rearrange("a p w -> p (a w)"), rec[:, h]).then_inc(rewritten[h], 16)
                        for h in range(B):
                            sp.wait_ge(rewritten[h], 16 * count)
                            sp.sem_inc(tally, 1)
                    else:
                        with sp.Fori(0, groups(sp)) as it:
                            for h in range(B):
                                load_record(sp, it, h, full[h], used[h])

                @block.gpsimd
                def _(pool):
                    with pool.Fori(0, groups(pool)) as it:
                        for h in range(B):
                            gather_unit(pool, it, h, full[h], got[h])

                @block.scalar
                def _(act):
                    with act.Fori(0, groups(act)) as it:
                        for h in range(B):
                            act.wait_ge(logits_ready, B * it + h + 1)
                            act.sem_inc(tally, 1)
                            nc.scalar.activation(pr[:, h], lg[:, h], ACT.Exp, bias=st[:, h, 1:2], scale=-1.0)
                            nc.scalar.activation(st[:, h, 2:3], st[:, h, 0:1], ACT.Exp, bias=st[:, h, 1:2], scale=-1.0)
                            act.drain().then_inc(exps_ready, 1)
                    root(act, squares, roots)

                @block.vector
                def _(dve):
                    total = [dve.alloc_register(unique(nc, f"rows{h}")) for h in range(B)]
                    for h in range(B):
                        dve.reg_mov(total[h], 0)
                        dve.sem_inc(used[h], 1)
                    with dve.Fori(0, groups(dve)) as it:
                        for h in range(B):
                            t = wait_rows(dve, h, it, full[h], got[h], total)
                            nc.vector.tensor_scalar(valid[:, h], iota16[:], rec[:, h, R_NV:R_NV + 1].bitcast(F32), None, ALU.is_lt)
                            if place_sources:
                                nc.vector.tensor_copy(rec[:, h, 0:U], g[:, h, :, PLACE].bitcast(I32))
                            mine = aux[:, bass.ds(t, 1), :].rearrange("p a f -> p (a f)")
                            logits(dve, h, over(mine, 1, [P, U, D]), wp[:, h], lg[:, h], valid[:, h])
                            dve.drain()
                            m_t = mx[:, bass.ds(t, 1)]
                            nc.vector.tensor_reduce(st[:, h, 3:4], lg[:, h], axis=AX.X, op=ALU.min)
                            nc.vector.tensor_copy(st[:, h, 0:1], m_t)
                            dve.drain()
                            nc.vector.tensor_tensor(st[:, h, 1:2], st[:, h, 3:4], st[:, h, 0:1], ALU.min)
                            dve.drain().then_inc(logits_ready, 1)
                            dve.wait_ge(exps_ready, B * it + h + 1)
                            dve.sem_inc(tally, 1)
                            nc.vector.tensor_copy(m_t, st[:, h, 1:2])
                            sum_rows(dve, g[:, h], pr[:, h], t, h, valid, wp, red, D + 1)
                            own = agg[:, bass.ds(t, 1), :].rearrange("p a f -> p (a f)")
                            nc.vector.scalar_tensor_tensor(own, own, st[:, h, 2:3], red[:, h, :], ALU.mult, ALU.add)
                            dve.drain().then_inc(used[h], 1)
                    for h in range(B):
                        dve.free_register(total[h])
                    then(dve)
                    dve.drain().then_inc(squares, 1)
                    dve.wait_ge(roots, 1)
                    after_root(dve)

        def masked(dve, lg, valid, scale):
            nc.vector.tensor_scalar(valid, valid, -BIG, BIG, ALU.mult, ALU.add)
            dve.drain()
            nc.vector.scalar_tensor_tensor(lg, lg, scale, valid, ALU.mult, ALU.add)

        def node_product(source, kin, weight, m, finish, store=None):
            with sbuf(nc, "stage", [P, 2, G7, kin], F32) as stage, sbuf(nc, "xt", [kin, 2, G7 * P], F32) as xt, \
                    psum(nc, "tp", [kin, 2, 8 * P], F32) as tp, psum(nc, "po", [P, 2, 512], F32) as po, \
                    phase(nc, "staged", "transposed", "copied", "product", "finished",
                          "stored") as sem, nc.Block() as block:
                staged, transposed, copied, product, finished, stored = sem

                @block.sync
                def _(sp):
                    if store == "ready":
                        sp.dma_start(by_place, row[:]).then_inc(stored, 16)
                        sp.wait_ge(stored, 16)
                    if store == "made":
                        with sp.Fori(0, NG) as i:
                            sp.wait_ge(finished, i + 3)
                            sp.dma_start(by_place[:, bass.ds(i * G7, G7), :], row[:, bass.ds(i * G7, G7), :]).then_inc(stored, 16)
                        sp.wait_ge(stored, 16 * NG)

                @block.scalar
                def _(act):
                    def put(i, h):
                        tiles = slice(i * G7, (i + 1) * G7) if isinstance(i, int) else bass.ds(i * G7, G7)
                        nc.scalar.copy(stage[:, h], source[:, tiles, :]).then_inc(staged, 1)

                    def take(i, h):
                        act.wait_ge(transposed, i + 1)
                        act.sem_inc(tally, 1)
                        act.wait_ge(product, i + 1)
                        act.sem_inc(tally, 1)
                        nc.scalar.copy(xt[:, h, 0:4 * P], tp[:, h, 0:4 * P])
                        nc.scalar.copy(xt[:, h, 4 * P:G7 * P], tp[:, h, 4 * P:G7 * P])
                        act.drain().then_inc(copied, 1)

                    put(0, 0)
                    with act.Fori(0, NG // 2 - 1) as j:
                        put(2 * j + 1, 1)
                        take(2 * j, 0)
                        put(2 * j + 2, 0)
                        take(2 * j + 1, 1)
                    put(NG - 1, 1)
                    take(NG - 2, 0)
                    take(NG - 1, 1)

                @block.tensor
                def _(pe):
                    def turn(i, h):
                        pe.wait_ge(staged, i + 1)
                        pe.sem_inc(tally, 1)
                        for c in range(G7):
                            last = nc.tensor.transpose(tp[:, h, c * P:(c + 1) * P], stage[:, h, c], ident[:])
                        last.then_inc(transposed, 1)

                    def multiply(i, h):
                        pe.wait_ge(copied, i + 1)
                        pe.sem_inc(tally, 1)
                        pe.wait_ge(finished, i + 1)
                        pe.sem_inc(tally, 1)
                        for c in range(G7):
                            last = nc.tensor.matmul(po[:, h, c * m:(c + 1) * m], xt[:, h, c * P:(c + 1) * P], weight, start=True, stop=True)
                        last.then_inc(product, 1)

                    pe.sem_inc(product, 2)
                    turn(0, 0)
                    with pe.Fori(0, NG // 2 - 1) as j:
                        turn(2 * j + 1, 1)
                        multiply(2 * j, 0)
                        turn(2 * j + 2, 0)
                        multiply(2 * j + 1, 1)
                    turn(NG - 1, 1)
                    multiply(NG - 2, 0)
                    multiply(NG - 1, 1)

                @block.vector
                def _(dve):
                    dve.sem_inc(finished, 2)
                    with dve.Fori(0, NG // 2) as j:
                        for h in range(2):
                            dve.wait_ge(product, 2 * j + h + 3)
                            dve.sem_inc(tally, 1)
                            finish(dve, bass.ds((2 * j + h) * G7, G7), po[:, h, 0:G7 * m].rearrange("p (c m) -> p c m", c=G7))
                            dve.drain().then_inc(finished, 1)

        def with_sqrt(then, after_root):
            with phase(nc, "squares", "roots") as (squares, roots), nc.Block() as block:
                @block.vector
                def _(dve):
                    then(dve)
                    dve.drain().then_inc(squares, 1)
                    dve.wait_ge(roots, 1)
                    after_root(dve)

                @block.scalar
                def _(act):
                    root(act, squares, roots)

        scratch = big[:, 0:NT * D].rearrange("p (t f) -> p t f", f=D)
        scratch2 = big[:, NT * D:NT * 2 * D].rearrange("p (t f) -> p t f", f=D)
        own = row[:, :, 0:D]

        def on_vector(work):
            with nc.Block() as block:
                @block.vector
                def _(dve):
                    work(dve)

        def moments(dve):
            nc.vector.tensor_reduce(small[:, 2], scratch, axis=AX.X, op=ALU.add)
            dve.drain()
            nc.vector.tensor_scalar(small[:, 2], small[:, 2], 1.0 / D, None, ALU.mult)
            dve.drain()
            nc.vector.tensor_tensor(x[:], scratch, over(small[:, 2], 2, [P, NT, D]), ALU.subtract)
            dve.drain()
            nc.vector.tensor_tensor(scratch, x[:], x[:], ALU.mult)
            dve.drain()
            nc.vector.tensor_reduce(small[:, 3], scratch, axis=AX.X, op=ALU.add)
            dve.drain()
            nc.vector.tensor_scalar(small[:, 0], small[:, 3], 1.0 / D, EPS_LN, ALU.mult, ALU.add)

        def divide(dve):
            nc.vector.reciprocal(small[:, 2], small[:, 1])
            dve.drain()
            nc.vector.tensor_tensor(x[:], x[:], over(small[:, 2], 2, [P, NT, D]), ALU.mult)
            dve.drain()

        def divide_to_row(dve):
            divide(dve)
            nc.vector.tensor_copy(own, x[:])

        make_constants()
        count_and_order()
        load_order()
        write_records()

        dinv, lam = small[:, 4], small[:, 5, 4:8]

        def degrees(dve):
            nc.vector.tensor_scalar(small[:, 0], degf[:], 1.0, None, ALU.max)
            nc.vector.reciprocal(lam[:, 1:2], lam[:, 0:1])
            dve.drain()
            nc.vector.tensor_scalar(lam[:, 1:2], lam[:, 1:2], 2.0, None, ALU.mult)
            dve.drain()
            nc.vector.tensor_scalar(lam[:, 2:3], lam[:, 1:2], -1.0, None, ALU.add)
            nc.vector.tensor_scalar(lam[:, 3:4], lam[:, 1:2], -1.0, None, ALU.mult)
        with_sqrt(degrees, lambda dve: nc.vector.reciprocal(dinv, small[:, 1]))

        beta = small[:, 5, 0:1]

        def square(dve):
            nc.vector.tensor_tensor(scratch, own, own, ALU.mult)
            dve.drain()
            nc.vector.tensor_reduce(small[:, 0], scratch, axis=AX.X, op=ALU.add)
            dve.drain()
            nc.vector.tensor_scalar(small[:, 0], small[:, 0], EPS_NORM ** 2 / 100, None, ALU.max)

        def first_square(dve):
            nc.vector.tensor_copy(own, x[:])
            dve.drain()
            square(dve)

        def divide_and_square(dve):
            nc.vector.reciprocal(small[:, 2], agg[:, :, D])
            dve.drain()
            nc.vector.tensor_tensor(own, agg[:, :, 0:D], over(small[:, 2], 2, [P, NT, D]), ALU.mult)
            dve.drain()
            square(dve)

        def norms(dve):
            nc.vector.tensor_scalar(small[:, 2], small[:, 1], EPS_NORM, None, ALU.max)
            dve.drain()
            nc.vector.reciprocal(small[:, 3], small[:, 2])
            dve.drain()
            nc.vector.tensor_copy(row[:, :, RN], small[:, 3])

        with_sqrt(first_square, norms)

        def start_with_self(r):
            def start(dve):
                nc.vector.tensor_copy(beta, negbeta[:, bass.ds(r, 1)])
                nc.vector.tensor_tensor(aux[:], own, over(small[:, 3], 2, [P, NT, D]), ALU.mult)
                dve.drain()
                nc.vector.tensor_tensor(scratch, aux[:], aux[:], ALU.mult)
                nc.vector.tensor_copy(agg[:], row[:, :, 0:D + 1])
                dve.drain()
                nc.vector.tensor_reduce(mx[:], scratch, axis=AX.X, op=ALU.add)
                dve.drain()
                nc.vector.tensor_scalar(mx[:], mx[:], beta, None, ALU.mult)
            return start

        def cosine(dve, h, mine, wp, lg, valid):
            nc.vector.tensor_tensor(wp[:, :, 0:D], g[:, h, :, 0:D], mine, ALU.mult)
            dve.drain()
            nc.vector.tensor_reduce(lg, wp[:, :, 0:D], axis=AX.X, op=ALU.add)
            dve.drain()
            nc.vector.tensor_tensor(lg, lg, g[:, h, :, RN], ALU.mult)
            masked(dve, lg, valid, beta)

        on_vector(start_with_self(0))
        gather_attend(cosine, divide_and_square, norms, place_sources=True)
        with nc.Fori(1, 3) as r:
            store_table(beside=start_with_self(r))
            gather_attend(cosine, divide_and_square, norms)

        def attended_sum(dve):
            nc.vector.tensor_tensor(scratch, x[:], own, ALU.add)
            dve.drain()
            moments(dve)
        with_sqrt(attended_sum, divide_to_row)

        lin = big[:, 2 * NT * D:3 * NT * D].rearrange("p (t f) -> p t f", f=D)
        node_product(x, D, selfw[:], D, lambda dve, tiles, prod: nc.vector.tensor_copy(lin[:, tiles, :], prod), store="ready")

        def messages_in(dve):
            nc.vector.tensor_scalar(scratch2, lin, 1.0 / 8 ** 0.5, None, ALU.mult)
            dve.drain()
            nc.vector.scalar_tensor_tensor(scratch2, agg[:, :, 0:D], 0.25, scratch2, ALU.mult, ALU.add)
            dve.drain()
            nc.vector.tensor_tensor(scratch[:, :, 0:8], x[:, :, 0:8], scratch2[:, :, 0:8], ALU.add)
            for m in range(3):
                nc.vector.tensor_tensor(scratch[:, :, 8 + m:D:3], x[:, :, 8 + m:D:3], scratch2[:, :, 8 + 8 * m:16 + 8 * m], ALU.add)
            dve.drain()
            moments(dve)

        def divide_and_scale(dve):
            divide(dve)
            nc.vector.tensor_tensor(own, x[:], over(dinv, 2, [P, NT, D]), ALU.mult)
        edge_messages(nc, locals(), messages_in, divide_and_scale)

        cat = big[:].rearrange("p (t f) -> p t f", f=3 * D)
        with ExitStack() as st:
            hc = st.enter_context(sbuf(nc, "hc", [P, NT, D], F32))
            store_table(beside=lambda dve: nc.vector.tensor_copy(cat[:, :, 0:D], x[:]))

            def first_term(dve):
                c1 = cat[:, :, D:2 * D]
                nc.vector.tensor_tensor(c1, agg[:, :, 0:D], over(dinv, 2, [P, NT, D]), ALU.mult)
                nc.vector.tensor_scalar(hc[:], x[:], lam[:, 2:3], None, ALU.mult)
                dve.drain()
                nc.vector.scalar_tensor_tensor(c1, c1, lam[:, 3:4], hc[:], ALU.mult, ALU.add)
                dve.drain()
                nc.vector.tensor_tensor(own, c1, over(dinv, 2, [P, NT, D]), ALU.mult)
            gather_sum(first_term)
            store_table()

            def second_term(dve):
                c2 = cat[:, :, 2 * D:3 * D]
                nc.vector.tensor_tensor(c2, agg[:, :, 0:D], over(dinv, 2, [P, NT, D]), ALU.mult)
                nc.vector.tensor_scalar(hc[:], cat[:, :, D:2 * D], lam[:, 2:3], None, ALU.mult)
                dve.drain()
                nc.vector.scalar_tensor_tensor(c2, c2, lam[:, 3:4], hc[:], ALU.mult, ALU.add)
                dve.drain()
                nc.vector.scalar_tensor_tensor(c2, c2, 2.0, x[:], ALU.mult, ALU.subtract)
                nc.vector.memset(agg[:], 0.0)
                nc.vector.memset(mx[:], BIG / 10)
            gather_sum(second_term)

            def relu_bias(dve, tiles, prod):
                nc.vector.tensor_tensor(hc[:, tiles, :], prod, over(cb[:], 1, [P, G7, D]), ALU.add)
                dve.drain()
                nc.vector.tensor_scalar(hc[:, tiles, :], hc[:, tiles, :], 0.0, None, ALU.max)
            node_product(cat, 3 * D, cw[:], D, relu_bias)

            def both(dve, tiles, prod):
                nc.vector.tensor_tensor(row[:, tiles, 0:D], prod[:, :, 0:D], over(fb[:, 0:D], 1, [P, G7, D]), ALU.add)
                nc.vector.tensor_tensor(aux[:, tiles, :], prod[:, :, D:2 * D], over(fb[:, D:2 * D], 1, [P, G7, D]), ALU.add)
            node_product(hc, D, fw[:], 2 * D, both, store="made")

            def additive(dve, h, mine, wp, lg, valid):
                e = wp[:, :, 0:D]
                nc.vector.tensor_tensor(e, g[:, h, :, 0:D], mine, ALU.add)
                dve.drain()
                nc.vector.scalar_tensor_tensor(e, e, 0.2, e, ALU.mult, ALU.max)
                dve.drain()
                nc.vector.tensor_tensor(e, e, over(att[:], 1, [P, U, D]), ALU.mult)
                dve.drain()
                nc.vector.tensor_reduce(lg, e, axis=AX.X, op=ALU.add)
                dve.drain()
                masked(dve, lg, valid, -1.0)

            def attended(dve):
                nc.vector.tensor_scalar(small[:, 2], agg[:, :, D], 0.0, None, ALU.is_equal)
                dve.drain()
                nc.vector.tensor_tensor(small[:, 2], small[:, 2], agg[:, :, D], ALU.add)
                dve.drain()
                nc.vector.reciprocal(small[:, 3], small[:, 2])
                dve.drain()
                nc.vector.tensor_tensor(scratch, agg[:, :, 0:D], over(small[:, 3], 2, [P, NT, D]), ALU.mult)
                dve.drain()
                nc.vector.tensor_tensor(scratch, scratch, x[:], ALU.add)
                dve.drain()
                moments(dve)
            gather_attend(additive, attended, divide_to_row)

        ax = big[:, 0:NT * 2 * D].rearrange("p (t f) -> p t f", f=2 * D)
        with ExitStack() as st:
            hid = st.enter_context(sbuf(nc, "hid", [P, NT, MH], F32))
            store_table(beside=lambda dve: nc.vector.tensor_copy(ax[:, :, D:2 * D], x[:]))
            gather_sum(lambda dve: nc.vector.tensor_copy(ax[:, :, 0:D], agg[:, :, 0:D]))

            def relu_in(dve, tiles, prod):
                nc.vector.tensor_tensor(hid[:, tiles, :], prod, over(bin_[:], 1, [P, G7, MH]), ALU.add)
                dve.drain()
                nc.vector.tensor_scalar(hid[:, tiles, :], hid[:, tiles, :], 0.0, None, ALU.max)
            node_product(ax, 2 * D, win_[:], MH, relu_in)

            def outs(dve, tiles, prod):
                nc.vector.tensor_copy(row[:, tiles, 0:D], prod[:, :, 0:D])
                nc.vector.tensor_tensor(aux[:, tiles, :], prod[:, :, D:2 * D], over(bout[:], 1, [P, G7, D]), ALU.add)
            node_product(hid, MH, wout[:], 2 * D, outs, store="made")

            def last_sum(dve):
                nc.vector.tensor_tensor(scratch, agg[:, :, 0:D], aux[:], ALU.add)
                dve.drain()
                nc.vector.tensor_tensor(scratch, scratch, x[:], ALU.add)
                dve.drain()
                moments(dve)
            gather_sum(last_sum, divide_to_row)
        scatter_rows(out, D, bound=N - 1)


def edge_messages(nc, v, then, after_root):
    tally, g, rec, agg, iota16, attw, ident = (v[k] for k in ("tally", "g", "rec", "agg", "iota16", "attw", "ident"))
    s_attr, root = v["s_attr"], v["root"]
    w1, w2, b1, b2s, ones3 = (v[k] for k in ("w1", "w2", "b1", "b2s", "ones3"))
    groups, load_record, gather_unit = (v[k] for k in ("groups", "load_record", "gather_unit"))
    S = U // 4
    w2f = w2[:].rearrange("h k c -> h (k c)")
    with ExitStack() as st:
        s2 = lambda n, sh, dt=F32: st.enter_context(sbuf(nc, n, sh, dt))
        ea = s2("ea", [P, B, U, AW])
        valid = s2("valid", [P, U])
        sh = s2("sh", [P, U, 4])
        zz = s2("zz", [P, U, 24])
        v0 = s2("v0", [P, 3, U, 8])
        vm = s2("vm", [P, U, 8, 3])
        ep = s2("ep", [P, 2, U * D])
        et = s2("et", [P, 2, P])
        ht = s2("ht", [P, 4, 2, P])
        p1 = s2("p1", [P, 2, 4, 24, 8])
        p2 = s2("p2", [P, 2, 3, 32, 8])
        t1 = s2("t1", [P, U, 8])
        tm = s2("tm", [P, 3, U, 8])
        part = s2("part", [P, S + 1, D])
        red = s2("red", [P, D])
        etp = st.enter_context(psum(nc, "etp", [P, 2, 512], F32))
        hps = st.enter_context(psum(nc, "hps", [P, 2, 512], F32))
        wps = st.enter_context(psum(nc, "wps", [P, 2, 4, 256], F32))
        names = v["NAMES"] + [f"attr{b}" for b in range(B)] + \
            ["packed", "turned", "turned_copied", "hidden", "hidden_relu", "weights", "weights_used", "squares", "roots"]
        with phase(nc, *names) as sem, nc.Block() as block:
            full, used, got, attr = (sem[B * k:B * (k + 1)] for k in range(4))
            packed, turned, turned_copied, hidden, hidden_relu, weights, weights_used, squares, roots = sem[4 * B:]

            @block.sync
            def _(sp):
                with sp.Fori(0, groups(sp)) as it:
                    for h in range(B):
                        load_record(sp, it, h, full[h], used[h])

            @block.gpsimd
            def _(pool):
                pool.wait_ge(s_attr, 16)
                with pool.Fori(0, groups(pool)) as it:
                    for h in range(B):
                        pool.wait_ge(full[h], 16 * (it + 1))
                        pool.sem_inc(tally, 1)
                        nc.gpsimd.indirect_dma_start(out=ea[:, h].rearrange("p a b -> p (a b)"), out_offset=None, in_=attw,
                                                     in_offset=bass.IndirectOffsetOnAxis(ap=rec[:, h, R_BASE:R_BASE + 1], axis=0)).then_inc(attr[h], 16)
                        gather_unit(pool, it, h, full[h], got[h])

            @block.tensor
            def _(pe):
                def turn(nk, h, s, n):
                    with pe.If(nk > 4 * s):
                        pe.wait_ge(turned_copied, n + 1)
                        pe.sem_inc(tally, 1)
                        nc.tensor.transpose(etp[:, s % 2, 0:P], ep[:, h % 2, 4 * s * D:4 * (s + 1) * D], ident[:]).then_inc(turned, 1)
                    with pe.Else():
                        pe.drain().then_inc(turned, 1)

                def hide(nk, s, n):
                    with pe.If(nk > 4 * s):
                        pe.wait_ge(turned_copied, n + 3)
                        pe.wait_ge(hidden_relu, n + 1)
                        for c in range(2):
                            last = nc.tensor.matmul(hps[:, s % 2, c * P:(c + 1) * P], w1[:, c], et[:, s % 2], start=True, stop=True)
                        last.then_inc(hidden, 1)
                    with pe.Else():
                        pe.drain().then_inc(hidden, 1)

                def weigh(nk, s, n):
                    with pe.If(nk > 4 * s):
                        pe.wait_ge(hidden_relu, n + 3)
                        pe.wait_ge(weights_used, n + 1)
                        for half in range(2):
                            nc.tensor.matmul(wps[:, s % 2, 2 * half:2 * half + 2].rearrange("p c k -> p (c k)"), ones3[:],
                                             b2s[:].rearrange("b c k -> b (c k)"), start=True, stop=False)
                        for c in (0, 2, 1, 3):
                            rows = slice(MH * (c // 2), MH * (c // 2 + 1))
                            last = nc.tensor.matmul(wps[:, s % 2, c], ht[rows, s, c % 2], w2f[rows], start=False, stop=c % 2 == 1)
                        last.then_inc(weights, 1)
                    with pe.Else():
                        pe.drain().then_inc(weights, 1)

                pe.sem_inc(turned, 5)
                pe.sem_inc(hidden, 2)
                pe.sem_inc(weights, 4)
                with pe.Fori(0, groups(pe)) as it:
                    for h in range(B):
                        pe.wait_ge(packed, B * it + h + 1)
                        pe.sem_inc(tally, 1)
                        nk = pe.value_load(rec[0:1, h, R_NK:R_NK + 1], min_val=0, max_val=U)
                        n = S * (B * it + h)
                        turn(nk, h, 0, n)
                        for s in range(1, S):
                            turn(nk, h, s, n + s)
                            hide(nk, s - 1, n + s - 1)
                        hide(nk, S - 1, n + S - 1)
                        for s in range(S):
                            weigh(nk, s, n + s)

            @block.scalar
            def _(act):
                def copy(nk, s, n):
                    act.wait_ge(turned, n + 6)
                    act.wait_ge(hidden, n + 1)
                    act.sem_inc(tally, 1)
                    with act.If(nk > 4 * s):
                        nc.scalar.copy(et[:, s % 2], etp[:, s % 2, 0:P]).then_inc(turned_copied, 1)
                    with act.Else():
                        act.drain().then_inc(turned_copied, 1)

                def relu(nk, s, n):
                    act.wait_ge(hidden, n + 3)
                    act.wait_ge(weights, n + 1)
                    act.sem_inc(tally, 1)
                    with act.If(nk > 4 * s):
                        nc.scalar.activation(ht[:, s].rearrange("p c n -> p (c n)"), hps[:, s % 2, 0:2 * P], ACT.Relu, bias=b1[:, 0:1]).then_inc(hidden_relu, 1)
                    with act.Else():
                        act.drain().then_inc(hidden_relu, 1)

                act.sem_inc(turned_copied, 2)
                act.sem_inc(hidden_relu, 2)
                with act.Fori(0, groups(act)) as it:
                    for h in range(B):
                        act.wait_ge(full[h], 16 * (it + 1))
                        act.sem_inc(tally, 1)
                        nk = act.value_load(rec[0:1, h, R_NK:R_NK + 1], min_val=0, max_val=U)
                        n = S * (B * it + h)
                        act.wait_ge(attr[h], 16 * (it + 1))
                        act.wait_ge(turned, n + 1)
                        nc.scalar.activation(ep[:, h % 2].rearrange("p (c f) -> p c f", f=D), ea[:, h, :, 0:D], ACT.Copy).then_inc(packed, 1)
                        copy(nk, 0, n)
                        for s in range(1, S):
                            copy(nk, s, n + s)
                            relu(nk, s - 1, n + s - 1)
                        relu(nk, S - 1, n + S - 1)
                root(act, squares, roots)

            @block.vector
            def _(dve):
                nc.vector.memset(agg[:], 0.0)
                nc.vector.memset(t1[:], 0.0)
                nc.vector.memset(part[:], 0.0)
                dve.drain()
                total = [dve.alloc_register(unique(nc, f"rows{h}")) for h in range(B)]
                for h in range(B):
                    dve.reg_mov(total[h], 0)
                    dve.sem_inc(used[h], 1)
                dve.sem_inc(weights_used, 2)
                def numbers(h, it):
                    dve.wait_ge(full[h], 16 * (it + 1))
                    dve.sem_inc(tally, 1)
                    return (dve.value_load(rec[0:1, h, R_TILE:R_TILE + 1], min_val=0, max_val=NT - 1),
                            dve.value_load(rec[0:1, h, R_NK:R_NK + 1], min_val=0, max_val=U))

                with dve.Fori(0, groups(dve)) as it:
                    following = numbers(0, it)
                    for h in range(B):
                        t, nk = following
                        dve.reg_add(total[h], total[h], nk)
                        dve.wait_ge(attr[h], 16 * (it + 1))
                        dve.wait_ge(got[h], dve.snap(total[h]) * 16)
                        nc.vector.tensor_scalar(valid[:], iota16[:], rec[:, h, R_NV:R_NV + 1].bitcast(F32), None, ALU.is_lt)
                        nc.vector.tensor_copy(zz[:, :, 16:24], g[:, h, :, 0:8])
                        dve.drain()
                        nc.vector.tensor_tensor(sh[:], ea[:, h, :, D:D + 4], over(valid[:], 2, [P, U, 4]), ALU.mult)
                        dve.drain()
                        vec = g[:, h, :, 8:D].rearrange("p c (i m) -> p c i m", m=3)
                        nc.vector.tensor_tensor(vm[:], vec, over(sh[:, :, 1:4], 2, [P, U, 8, 3]), ALU.mult)
                        nc.vector.tensor_tensor(v0[:].rearrange("p m c i -> p c i m"), vec,
                                                sh[:, :, 0:1].unsqueeze(3).broadcast_to([P, U, 8, 3]), ALU.mult)
                        nc.vector.tensor_tensor(zz[:, :, 0:8], g[:, h, :, 0:8], over(sh[:, :, 0], 2, [P, U, 8]), ALU.mult)
                        dve.drain()
                        nc.vector.tensor_reduce(zz[:, :, 8:16], vm[:], axis=AX.X, op=ALU.add)
                        dve.drain()
                        for s in range(S):
                            n = S * (B * it + h) + s
                            dve.wait_ge(weights, n + 5)
                            dve.sem_inc(tally, 1)
                            with dve.If(nk > 4 * s):
                                c4 = slice(4 * s, 4 * s + 4)
                                pa, pb = p1[:, s % 2], p2[:, s % 2]
                                nc.vector.tensor_tensor(pa, wps[:, s % 2, :, 0:192].rearrange("p c (r o) -> p c r o", o=8),
                                                        over(zz[:, c4], 3, [P, 4, 24, 8]), ALU.mult)
                                nc.vector.tensor_tensor(pb.rearrange("p m (c i) o -> p m c i o", c=4),
                                                        over(wps[:, s % 2, :, 192:256].rearrange("p c (i o) -> p c i o", o=8), 1, [P, 3, 4, 8, 8]),
                                                        over(v0[:, :, c4], 4, [P, 3, 4, 8, 8]), ALU.mult)
                                dve.drain().then_inc(weights_used, 1)
                                nc.vector.tensor_reduce(part[:, s, 0:8], pa[:, :, 0:16].rearrange("p c r o -> p o c r"), axis=AX.XY, op=ALU.add)
                                nc.vector.tensor_reduce(t1[:, c4], pa[:, :, 16:24].rearrange("p c i o -> p c o i"), axis=AX.X, op=ALU.add)
                                nc.vector.tensor_reduce(part[:, s, 8:D].rearrange("p (m o) -> p m o", m=3),
                                                        pb.rearrange("p m r o -> p m o r"), axis=AX.X, op=ALU.add)
                            with dve.Else():
                                dve.drain().then_inc(weights_used, 1)
                                nc.vector.memset(part[:, s], 0.0)
                        if h + 1 < B:
                            following = numbers(h + 1, it)
                        dve.drain()
                        for m in range(3):
                            nc.vector.tensor_tensor(tm[:, m], t1[:], over(sh[:, :, 1 + m], 2, [P, U, 8]), ALU.mult)
                        dve.drain()
                        nc.vector.tensor_reduce(part[:, S, 8:D].rearrange("p (m o) -> p m o", m=3),
                                                tm[:].rearrange("p m c o -> p m o c"), axis=AX.X, op=ALU.add)
                        dve.drain()
                        nc.vector.tensor_reduce(red[:], part[:].rearrange("p s f -> p f s"), axis=AX.X, op=ALU.add)
                        dve.drain().then_inc(used[h], 1)
                        own = agg[:, bass.ds(t, 1), 0:D].rearrange("p a f -> p (a f)")
                        nc.vector.tensor_tensor(own, own, red[:], ALU.add)
                for h in range(B):
                    dve.free_register(total[h])
                dve.drain()
                then(dve)
                dve.drain().then_inc(squares, 1)
                dve.wait_ge(roots, 1)
                after_root(dve)


_PLAIN = {
    "x": "x", "src": "src", "dst": "dst", "W1": "L1_gnn_W1", "b1": "L1_gnn_b1", "W2": "L1_gnn_W2", "b2": "L1_gnn_b2",
    "si_w0": "L1_gnn_si_w0", "si_w1": "L1_gnn_si_w1", "lambda_max": "L2_gnn_lambda_max", "cheb_W": "L2_gnn_cheb_W",
    "cheb_b": "L2_gnn_cheb_b", "src_W": "L2_gnn_src_W", "src_b": "L2_gnn_src_b", "dst_W": "L2_gnn_dst_W",
    "dst_b": "L2_gnn_dst_b", "attn": "L2_gnn_attn", "b_l_in": "L3_gnn_b_l_in", "b_l_out": "L3_gnn_b_l_out",
}
_TURNED = {"W_l_in_T": "L3_gnn_W_l_in", "W_r_in_T": "L3_gnn_W_r_in", "W_l_out_T": "L3_gnn_W_l_out", "W_r_out_T": "L3_gnn_W_r_out"}


def kernel(**inputs):
    import numpy as np
    import concourse.bacc as bacc
    from concourse.bass_utils import run_bass_kernel_spmd

    arrays = {name: np.ascontiguousarray(inputs[of]) for name, of in _PLAIN.items()}
    arrays |= {name: np.ascontiguousarray(np.asarray(inputs[of]).T) for name, of in _TURNED.items()}
    arrays["betas"] = np.concatenate([np.asarray(inputs[f"L0_gnn_beta{i}"]) for i in (1, 2, 3)])
    arrays["attr"] = np.concatenate([np.asarray(inputs["edge_attr_32"]), np.asarray(inputs["edge_attr_4"])], axis=1)

    nc = bacc.Bacc("TRN2", target_bir_lowering=False, num_devices=1)
    aps = {n: nc.dram_tensor(f"in_{n}", a.shape, mybir.dt.from_np(a.dtype), kind="ExternalInput").ap() for n, a in arrays.items()}
    out = nc.dram_tensor("out_x", (N, D), F32, kind="ExternalOutput").ap()
    build(nc, aps, out)
    r = run_bass_kernel_spmd(nc, [{f"in_{n}": a for n, a in arrays.items()}], core_ids=[0])
    return r.results[0]["out_x"]
```
